# Optimizing a Trainium2 kernel written in Bass

```python
import numpy as np
import jax
import jax.numpy as jnp

def _softmax(x, axis=-1):
    return jax.nn.softmax(x, axis=axis)
def _gelu(x):
    return jax.nn.gelu(x, approximate=True)
def _silu(x):
    return jax.nn.silu(x)
def _sigmoid(x):
    return jax.nn.sigmoid(x)
def _layernorm(x, axis=-1, eps=1e-5):
    m = jnp.mean(x, axis=axis, keepdims=True)
    v = jnp.var(x, axis=axis, keepdims=True)
    return (x - m) / jnp.sqrt(v + eps)
def _scatter_add(tgt, idx, src, axis=0):
    return tgt.at[idx].add(src)
def _segment_sum(src, seg, n):
    return jax.ops.segment_sum(src, seg, n)

kernel_name = 'mk_metaformer_d2_conv_nchw256_30769f'

def setup_inputs(seed: int = 0):
    np.random.seed(seed)
    _w = jnp.asarray
    def _rec_inputs():
        import jax
        import jax.numpy as jnp
        _gk = jax.random.key(seed)
        x = -0.000929 + 1 * jax.random.normal(jax.random.fold_in(_gk, 1), (1, 256, 64, 64), jnp.float32)
        return x
    x = _rec_inputs()
    def _L0_conv_setup():
        import jax, jax.numpy as jnp
        import numpy as np
        N_FEAT = 256
        NUM_HEADS = 8
        EPS = 1e-12

        def _l2norm(t):
            n = jnp.linalg.norm(t, axis=-1, keepdims=True)
            return t / jnp.maximum(n, EPS)
        key = jax.random.key(seed)
        k1, k2, k3 = jax.random.split(key, 3)
        b, c, h, w = (1, N_FEAT, 64, 64)
        x = jax.random.normal(k1, (b, c, h, w), dtype=jnp.float32)
        w_qkv = jax.random.normal(k2, (3 * c, c), dtype=jnp.float32) * (1.0 / np.sqrt(c))
        w_proj = jax.random.normal(k3, (c, c), dtype=jnp.float32) * (1.0 / np.sqrt(c))
        temperature = jnp.ones((NUM_HEADS, 1, 1), dtype=jnp.float32)
        return {'x': x, 'w_qkv': w_qkv, 'w_proj': w_proj, 'temperature': temperature}
    _L0_conv_all = _L0_conv_setup()
    _L0_conv_in = {k: v for k, v in _L0_conv_all.items() if k in ('w_qkv', 'w_proj', 'temperature', )}
    del _L0_conv_all

    def _L0_ffn_setup():
        import math
        import jax, jax.numpy as jnp
        import numpy as np
        CAPACITY_FACTOR = 1.25
        TOP_K = 2
        LN_EPS = 1e-05

        def _layer_norm(x, gamma, beta):
            mu = jnp.mean(x, axis=-1, keepdims=True)
            var = jnp.var(x, axis=-1, keepdims=True)
            return (x - mu) * jax.lax.rsqrt(var + LN_EPS) * gamma + beta
        key = jax.random.key(seed)
        ks = jax.random.split(key, 4)
        B, S, D, F, E = (8, 4096, 256, 512, 8)
        x = jax.random.normal(ks[0], (B, S, D), dtype=jnp.float32)
        Wr = jax.random.normal(ks[1], (D, E), dtype=jnp.float32) / np.sqrt(D)
        br = jnp.zeros((E,), jnp.float32)
        W1 = jax.random.normal(ks[2], (E, D, F), dtype=jnp.float32) / np.sqrt(D)
        b1 = jnp.zeros((E, F), jnp.float32)
        W2 = jax.random.normal(ks[3], (E, F, D), dtype=jnp.float32) / np.sqrt(F)
        b2 = jnp.zeros((E, D), jnp.float32)
        gamma = jnp.ones((D,), jnp.float32)
        beta = jnp.zeros((D,), jnp.float32)
        return {'x': x, 'Wr': Wr, 'br': br, 'W1': W1, 'b1': b1, 'W2': W2, 'b2': b2, 'gamma': gamma, 'beta': beta}
    _L0_ffn_all = _L0_ffn_setup()
    _L0_ffn_in = {k: v for k, v in _L0_ffn_all.items() if k in ('Wr', 'br', 'W1', 'b1', 'W2', 'b2', 'gamma', 'beta', )}
    del _L0_ffn_all

    def _L1_conv_setup():
        import jax, jax.numpy as jnp
        import numpy as np
        RADIUS = 2
        DILATION = 1

        def conv1x1(x, W, b):
            return jnp.einsum('nchw,oc->nohw', x, W) + b[None, :, None, None]

        def unfold_neighbors(f, radius, dilation):
            n, c, h, w = f.shape
            k = 2 * radius + 1
            pad = (k - 1) * dilation // 2
            fp = jnp.pad(f, ((0, 0), (0, 0), (pad, pad), (pad, pad)))
            patches = [fp[:, :, i * dilation:i * dilation + h, j * dilation:j * dilation + w] for i in range(k) for j in range(k)]
            return jnp.stack(patches, axis=2)

        def neighbor_correlation_filter(f1, f2, radius, dilation):
            n, c, h, w = f2.shape
            f2u = unfold_neighbors(f2, radius, dilation)
            corr = jnp.sum(f1[:, :, None] * f2u, axis=1) / jnp.sqrt(jnp.float32(c))
            attn = jax.nn.softmax(corr, axis=1)
            sample = jnp.sum(attn[:, None] * f2u, axis=2)
            return (sample, corr)
        key = jax.random.key(seed)
        ks = jax.random.split(key, 7)
        n, cin, ch, h, w = (8, 256, 128, 64, 64)
        x = jax.random.normal(ks[0], (n, cin, h, w), dtype=jnp.float32)
        s1 = 1.0 / np.sqrt(cin)
        s2 = 1.0 / np.sqrt(ch)
        W1 = jax.random.uniform(ks[1], (ch, cin), jnp.float32, -s1, s1)
        b1 = jax.random.uniform(ks[2], (ch,), jnp.float32, -s1, s1)
        W2 = jax.random.uniform(ks[3], (ch, ch), jnp.float32, -s2, s2)
        b2 = jax.random.uniform(ks[4], (ch,), jnp.float32, -s2, s2)
        Wout = jax.random.uniform(ks[5], (cin, ch), jnp.float32, -s2, s2)
        bout = jax.random.uniform(ks[6], (cin,), jnp.float32, -s2, s2)
        return {'x': x, 'W1': W1, 'b1': b1, 'W2': W2, 'b2': b2, 'Wout': Wout, 'bout': bout}
    _L1_conv_all = _L1_conv_setup()
    _L1_conv_in = {k: v for k, v in _L1_conv_all.items() if k in ('W1', 'b1', 'W2', 'b2', 'Wout', 'bout', )}
    del _L1_conv_all

    def _L1_ffn_setup():
        import jax, jax.numpy as jnp
        import numpy as np
        B, N, D = (16, 4096, 256)
        NUM_EXPERTS, TOP_K, HEADS = (4, 2, 4)
        N_EDGES = 1048576
        LN_EPS = 1e-05

        def _layernorm(x, g, b):
            mu = x.mean(-1, keepdims=True)
            var = ((x - mu) ** 2).mean(-1, keepdims=True)
            return (x - mu) * jax.lax.rsqrt(var + LN_EPS) * g + b

        def _forward(x, edge_index, W_gat, att_src, att_dst, b_gat, ln_gamma, ln_beta, W1, b1, W2, b2):
            Bc, Nc, Dc = x.shape
            M = Bc * Nc
            x_flat = x.reshape(M, Dc)
            h = (x_flat @ W_gat).reshape(M, HEADS, NUM_EXPERTS)
            loops = jnp.arange(M, dtype=edge_index.dtype)
            src = jnp.concatenate([edge_index[0], loops])
            dst = jnp.concatenate([edge_index[1], loops])
            a_src = (h * att_src).sum(-1)
            a_dst = (h * att_dst).sum(-1)
            e = jax.nn.leaky_relu(a_src[src] + a_dst[dst], negative_slope=0.2)
            e_max = jax.ops.segment_max(e, dst, num_segments=M)
            ee = jnp.exp(e - e_max[dst])
            denom = jax.ops.segment_sum(ee, dst, num_segments=M)
            alpha = ee / (denom[dst] + 1e-16)
            msg = h[src] * alpha[:, :, None]
            agg = jax.ops.segment_sum(msg, dst, num_segments=M).reshape(M, HEADS * NUM_EXPERTS) + b_gat
            scores = _layernorm(agg, ln_gamma, ln_beta).reshape(M, HEADS, NUM_EXPERTS).mean(1)
            scores = scores.reshape(Bc, Nc, NUM_EXPERTS)
            topk_s, topk_i = jax.lax.top_k(scores, TOP_K)
            w = jax.nn.softmax(topk_s, axis=-1)
            out = jnp.zeros_like(x)
            for ei in range(NUM_EXPERTS):
                g = jnp.where(topk_i == ei, w, 0.0).sum(-1)
                hh = jax.nn.gelu(x @ W1[ei] + b1[ei], approximate=False)
                out = out + g[..., None] * (hh @ W2[ei] + b2[ei])
            return out
        key = jax.random.key(seed)
        ks = jax.random.split(key, 8)
        s = 0.05
        return {'x': jax.random.normal(ks[0], (B, N, D), jnp.float32), 'W_gat': jax.random.normal(ks[1], (D, HEADS * NUM_EXPERTS), jnp.float32) * s, 'att_src': jax.random.normal(ks[2], (HEADS, NUM_EXPERTS), jnp.float32) * s, 'att_dst': jax.random.normal(ks[3], (HEADS, NUM_EXPERTS), jnp.float32) * s, 'b_gat': jnp.zeros((HEADS * NUM_EXPERTS,), jnp.float32), 'ln_gamma': jnp.ones((HEADS * NUM_EXPERTS,), jnp.float32), 'ln_beta': jnp.zeros((HEADS * NUM_EXPERTS,), jnp.float32), 'W1': jax.random.normal(ks[4], (NUM_EXPERTS, D, 2 * D), jnp.float32) * s, 'b1': jnp.zeros((NUM_EXPERTS, 2 * D), jnp.float32), 'W2': jax.random.normal(ks[5], (NUM_EXPERTS, 2 * D, D), jnp.float32) * s, 'b2': jnp.zeros((NUM_EXPERTS, D), jnp.float32), 'edge_index': jax.random.randint(ks[6], (2, N_EDGES), 0, B * N, jnp.int32)}
    _L1_ffn_all = _L1_ffn_setup()
    _L1_ffn_in = {k: v for k, v in _L1_ffn_all.items() if k in ('W_gat', 'att_src', 'att_dst', 'b_gat', 'ln_gamma', 'ln_beta', 'W1', 'b1', 'W2', 'b2', 'edge_index', )}
    del _L1_ffn_all

    return {
        "x": x,
        "L0_conv_w_qkv": _L0_conv_in["w_qkv"],
        "L0_conv_w_proj": _L0_conv_in["w_proj"],
        "L0_conv_temperature": _L0_conv_in["temperature"],
        "L0_ffn_Wr": _L0_ffn_in["Wr"],
        "L0_ffn_br": _L0_ffn_in["br"],
        "L0_ffn_W1": _L0_ffn_in["W1"],
        "L0_ffn_b1": _L0_ffn_in["b1"],
        "L0_ffn_W2": _L0_ffn_in["W2"],
        "L0_ffn_b2": _L0_ffn_in["b2"],
        "L0_ffn_gamma": _L0_ffn_in["gamma"],
        "L0_ffn_beta": _L0_ffn_in["beta"],
        "L1_conv_W1": _L1_conv_in["W1"],
        "L1_conv_b1": _L1_conv_in["b1"],
        "L1_conv_W2": _L1_conv_in["W2"],
        "L1_conv_b2": _L1_conv_in["b2"],
        "L1_conv_Wout": _L1_conv_in["Wout"],
        "L1_conv_bout": _L1_conv_in["bout"],
        "L1_ffn_W_gat": _L1_ffn_in["W_gat"],
        "L1_ffn_att_src": _L1_ffn_in["att_src"],
        "L1_ffn_att_dst": _L1_ffn_in["att_dst"],
        "L1_ffn_b_gat": _L1_ffn_in["b_gat"],
        "L1_ffn_ln_gamma": _L1_ffn_in["ln_gamma"],
        "L1_ffn_ln_beta": _L1_ffn_in["ln_beta"],
        "L1_ffn_W1": _L1_ffn_in["W1"],
        "L1_ffn_b1": _L1_ffn_in["b1"],
        "L1_ffn_W2": _L1_ffn_in["W2"],
        "L1_ffn_b2": _L1_ffn_in["b2"],
        "L1_ffn_edge_index": _L1_ffn_in["edge_index"],
    }

def reference(x, L0_conv_w_qkv, L0_conv_w_proj, L0_conv_temperature, L0_ffn_Wr, L0_ffn_br, L0_ffn_W1, L0_ffn_b1, L0_ffn_W2, L0_ffn_b2, L0_ffn_gamma, L0_ffn_beta, L1_conv_W1, L1_conv_b1, L1_conv_W2, L1_conv_b2, L1_conv_Wout, L1_conv_bout, L1_ffn_W_gat, L1_ffn_att_src, L1_ffn_att_dst, L1_ffn_b_gat, L1_ffn_ln_gamma, L1_ffn_ln_beta, L1_ffn_W1, L1_ffn_b1, L1_ffn_W2, L1_ffn_b2, L1_ffn_edge_index):
    import jax
    import jax.numpy as jnp
    def _L0_conv_ref(x, w_qkv, w_proj, temperature):
        import jax, jax.numpy as jnp
        import numpy as np
        N_FEAT = 256
        NUM_HEADS = 8
        EPS = 1e-12

        def _l2norm(t):
            n = jnp.linalg.norm(t, axis=-1, keepdims=True)
            return t / jnp.maximum(n, EPS)
        b, c, h, w = x.shape
        heads = temperature.shape[0]
        d = c // heads
        hw = h * w
        xf = x.reshape(b, c, hw)
        qkv = jnp.einsum('oc,bcs->bos', w_qkv, xf)
        qkv = qkv.reshape(b, 3, heads, d, hw)
        q, k, v = (qkv[:, 0], qkv[:, 1], qkv[:, 2])
        q = jnp.swapaxes(q, -2, -1)
        k = jnp.swapaxes(k, -2, -1)
        v = jnp.swapaxes(v, -2, -1)
        q = _l2norm(q)
        k = _l2norm(k)
        attn = jnp.einsum('bhsd,bhtd->bhst', q, k) * temperature[None]
        attn = jax.nn.softmax(attn, axis=-1)
        out = jnp.einsum('bhst,bhtd->bhsd', attn, v)
        out = out.transpose(0, 2, 1, 3).reshape(b, c, h, w)
        out = jnp.einsum('oc,bchw->bohw', w_proj, out)
        return out

    def _L0_ffn_ref(x, Wr, br, W1, b1, W2, b2, gamma, beta):
        import math
        import jax, jax.numpy as jnp
        import numpy as np
        CAPACITY_FACTOR = 1.25
        TOP_K = 2
        LN_EPS = 1e-05

        def _layer_norm(x, gamma, beta):
            mu = jnp.mean(x, axis=-1, keepdims=True)
            var = jnp.var(x, axis=-1, keepdims=True)
            return (x - mu) * jax.lax.rsqrt(var + LN_EPS) * gamma + beta
        B, S, D = x.shape
        E = Wr.shape[1]
        N = B * S
        K = TOP_K
        logits = jnp.mean(x, axis=1) @ Wr + br
        routing_weights = jax.nn.softmax(logits, axis=-1)
        capacity = float(math.ceil(N * CAPACITY_FACTOR / E))
        expected_loads = routing_weights.sum(axis=0) * (N / B)
        scale = jnp.where(expected_loads > capacity, capacity / expected_loads, 1.0)
        routing_weights = jax.nn.softmax(routing_weights * scale, axis=-1)
        rw_tok = jnp.broadcast_to(routing_weights[:, None, :], (B, S, E)).reshape(N, E)
        top_w, top_i = jax.lax.top_k(rw_tok, K)
        top_w = jax.nn.softmax(top_w, axis=-1)
        xf = x.reshape(N, D)
        h = jax.nn.gelu(jnp.einsum('nd,edf->enf', xf, W1) + b1[:, None, :], approximate=False)
        y = jnp.einsum('enf,efd->end', h, W2) + b2[:, None, :]
        w_dense = jnp.zeros((N, E), x.dtype).at[jnp.arange(N)[:, None], top_i].add(top_w)
        out = jnp.einsum('ne,end->nd', w_dense, y).reshape(B, S, D)
        out = _layer_norm(out + x, gamma, beta)
        return out

    def _L1_conv_ref(x, W1, b1, W2, b2, Wout, bout):
        import jax, jax.numpy as jnp
        import numpy as np
        RADIUS = 2
        DILATION = 1

        def conv1x1(x, W, b):
            return jnp.einsum('nchw,oc->nohw', x, W) + b[None, :, None, None]

        def unfold_neighbors(f, radius, dilation):
            n, c, h, w = f.shape
            k = 2 * radius + 1
            pad = (k - 1) * dilation // 2
            fp = jnp.pad(f, ((0, 0), (0, 0), (pad, pad), (pad, pad)))
            patches = [fp[:, :, i * dilation:i * dilation + h, j * dilation:j * dilation + w] for i in range(k) for j in range(k)]
            return jnp.stack(patches, axis=2)

        def neighbor_correlation_filter(f1, f2, radius, dilation):
            n, c, h, w = f2.shape
            f2u = unfold_neighbors(f2, radius, dilation)
            corr = jnp.sum(f1[:, :, None] * f2u, axis=1) / jnp.sqrt(jnp.float32(c))
            attn = jax.nn.softmax(corr, axis=1)
            sample = jnp.sum(attn[:, None] * f2u, axis=2)
            return (sample, corr)
        h = conv1x1(x, W1, b1)
        attribution, _ = neighbor_correlation_filter(h, h, RADIUS, DILATION)
        gate = jax.nn.sigmoid(jax.nn.relu(conv1x1(h, W2, b2)))
        attribution = gate * attribution
        return conv1x1(attribution, Wout, bout)

    def _L1_ffn_ref(x, W_gat, att_src, att_dst, b_gat, ln_gamma, ln_beta, W1, b1, W2, b2, edge_index):
        import jax, jax.numpy as jnp
        import numpy as np
        B, N, D = (16, 4096, 256)
        NUM_EXPERTS, TOP_K, HEADS = (4, 2, 4)
        N_EDGES = 1048576
        LN_EPS = 1e-05

        def _layernorm(x, g, b):
            mu = x.mean(-1, keepdims=True)
            var = ((x - mu) ** 2).mean(-1, keepdims=True)
            return (x - mu) * jax.lax.rsqrt(var + LN_EPS) * g + b

        def _forward(x, edge_index, W_gat, att_src, att_dst, b_gat, ln_gamma, ln_beta, W1, b1, W2, b2):
            Bc, Nc, Dc = x.shape
            M = Bc * Nc
            x_flat = x.reshape(M, Dc)
            h = (x_flat @ W_gat).reshape(M, HEADS, NUM_EXPERTS)
            loops = jnp.arange(M, dtype=edge_index.dtype)
            src = jnp.concatenate([edge_index[0], loops])
            dst = jnp.concatenate([edge_index[1], loops])
            a_src = (h * att_src).sum(-1)
            a_dst = (h * att_dst).sum(-1)
            e = jax.nn.leaky_relu(a_src[src] + a_dst[dst], negative_slope=0.2)
            e_max = jax.ops.segment_max(e, dst, num_segments=M)
            ee = jnp.exp(e - e_max[dst])
            denom = jax.ops.segment_sum(ee, dst, num_segments=M)
            alpha = ee / (denom[dst] + 1e-16)
            msg = h[src] * alpha[:, :, None]
            agg = jax.ops.segment_sum(msg, dst, num_segments=M).reshape(M, HEADS * NUM_EXPERTS) + b_gat
            scores = _layernorm(agg, ln_gamma, ln_beta).reshape(M, HEADS, NUM_EXPERTS).mean(1)
            scores = scores.reshape(Bc, Nc, NUM_EXPERTS)
            topk_s, topk_i = jax.lax.top_k(scores, TOP_K)
            w = jax.nn.softmax(topk_s, axis=-1)
            out = jnp.zeros_like(x)
            for ei in range(NUM_EXPERTS):
                g = jnp.where(topk_i == ei, w, 0.0).sum(-1)
                hh = jax.nn.gelu(x @ W1[ei] + b1[ei], approximate=False)
                out = out + g[..., None] * (hh @ W2[ei] + b2[ei])
            return out
        return _forward(x, edge_index, W_gat, att_src, att_dst, b_gat, ln_gamma, ln_beta, W1, b1, W2, b2)

    def _gn(v, G=32, eps=1e-5):
        B_, C_, H_, W_ = v.shape
        g = v.reshape(B_, G, C_ // G, H_, W_)
        m = jnp.mean(g, axis=(2, 3, 4), keepdims=True)
        s = jnp.var(g, axis=(2, 3, 4), keepdims=True)
        return ((g - m) / jnp.sqrt(s + eps)).reshape(v.shape)

    def _ln_c(v, eps=1e-6):
        m = jnp.mean(v, axis=1, keepdims=True)
        s = jnp.var(v, axis=1, keepdims=True)
        return (v - m) / jnp.sqrt(s + eps)

    def _ln_t(v, eps=1e-5):
        m = jnp.mean(v, axis=-1, keepdims=True)
        s = jnp.var(v, axis=-1, keepdims=True)
        return (v - m) / jnp.sqrt(s + eps)

    def _to_tokens(v):
        B_, C_, H_, W_ = v.shape
        return v.reshape(B_, C_, H_ * W_).transpose(0, 2, 1)
    def _from_tokens(t, like):
        B_, C_, H_, W_ = like.shape
        return t.transpose(0, 2, 1).reshape(B_, C_, H_, W_)

    x = x + _L0_conv_ref(_ln_c(x), L0_conv_w_qkv, L0_conv_w_proj, L0_conv_temperature)
    t = _to_tokens(x)
    t = t + _L0_ffn_ref(_ln_t(t), L0_ffn_Wr, L0_ffn_br, L0_ffn_W1, L0_ffn_b1, L0_ffn_W2, L0_ffn_b2, L0_ffn_gamma, L0_ffn_beta)
    x = _from_tokens(t, x)
    x = x + _L1_conv_ref(_ln_c(x), L1_conv_W1, L1_conv_b1, L1_conv_W2, L1_conv_b2, L1_conv_Wout, L1_conv_bout)
    t = _to_tokens(x)
    t = t + _L1_ffn_ref(_ln_t(t), L1_ffn_W_gat, L1_ffn_att_src, L1_ffn_att_dst, L1_ffn_b_gat, L1_ffn_ln_gamma, L1_ffn_ln_beta, L1_ffn_W1, L1_ffn_b1, L1_ffn_W2, L1_ffn_b2, L1_ffn_edge_index)
    x = _from_tokens(t, x)
    return x


_drawn_inputs = setup_inputs


def setup_inputs(seed=0):
    import zlib

    import numpy as np

    out = dict(_drawn_inputs(seed))
    spreads = {'L0_conv_temperature': (1.0, 0.6),
     'L0_ffn_br': (0.0, 0.1),
     'L0_ffn_b1': (0.0, 0.1),
     'L0_ffn_b2': (0.0, 0.1),
     'L0_ffn_gamma': (1.0, 0.2),
     'L0_ffn_beta': (0.0, 0.1),
     'L1_ffn_b_gat': (0.0, 0.1),
     'L1_ffn_ln_gamma': (1.0, 0.6),
     'L1_ffn_ln_beta': (0.0, 0.301),
     'L1_ffn_b1': (0.0, 0.305),
     'L1_ffn_b2': (0.0, 0.1)}
    factors = {'L0_conv_w_proj': 3.11,
     'L0_ffn_Wr': 8.0,
     'L1_conv_b1': 8.0,
     'L1_conv_W2': 6.204,
     'L1_conv_b2': 33.358,
     'L1_ffn_att_src': 6.382,
     'L1_ffn_att_dst': 22.221}
    for name, (base, spread) in spreads.items():
        noise = np.random.default_rng([zlib.crc32(name.encode()), seed]).standard_normal(out[name].shape)
        drawn = base * np.exp(spread * noise) if base else spread * noise
        out[name] = jnp.asarray(drawn.astype(out[name].dtype))
    for name, factor in factors.items():
        out[name] = (out[name] * factor).astype(out[name].dtype)
    return out
```

```python
import concourse.bass as bass
from concourse import mybir
from contextlib import ExitStack

F32 = mybir.dt.float32
F16 = mybir.dt.float16
I32 = mybir.dt.int32
ALU = mybir.AluOpType
ACT = mybir.ActivationFunctionType
AX = mybir.AxisListType

P = 128
C = 256
KC = C // P
N = 4096
CH = 512
NCH = N // CH
NT = N // P
HEADS = 8
DH = C // HEADS
QS, KS = 16.0, 1024.0


class Memory:

    spent = []

    def __init__(self, nc, stack, stage):
        self.nc, self.stack, self.stage = nc, stack, stage

    def sb(self, name, shape, dt=F32):
        return self.stack.enter_context(self.nc.sbuf_tensor(f"{self.stage}_{name}", shape, dt))

    def ps(self, name, shape, dt=F32):
        return self.stack.enter_context(self.nc.psum_tensor(f"{self.stage}_{name}", shape, dt))

    def sem(self, name, start=1):
        sem = self.nc.alloc_semaphore(name=f"{self.stage}_{name}")
        if start:
            self.nc.sync.sem_inc(sem, start)
        self.spent.append(sem)
        return sem

    @classmethod
    def clear_semaphores(cls, nc):
        nc.all_engine_barrier()
        nc.clear_and_free_semaphores(cls.spent)
        nc.all_engine_barrier()
        cls.spent = []


def fill_constants(nc, ones_mean, block_ones, ident, stack_ident, den_pick):
    with ExitStack() as s:
        filled = Memory(nc, s, "fill_constants").sem("const_filled")
        block = s.enter_context(nc.Block())

        @block.gpsimd
        def _(pool):
            pool.memset(ones_mean[:], 1.0 / C).then_inc(filled, 1)
            pool.memset(block_ones[:], 1.0).then_inc(filled, 1)
            pool.memset(ident[:], 0.0).then_inc(filled, 1)
            pool.memset(stack_ident[:], 0.0).then_inc(filled, 1)
            pool.memset(den_pick[:], 0.0).then_inc(filled, 1)
            pool.wait_ge(filled, 6)
            v = block_ones[:].rearrange("p (g j) -> p g j", g=4)
            pool.affine_select(out=v, in_=v, compare_op=ALU.is_ge, fill=0.0, base=0,
                               pattern=[[-32, 4], [0, 32]], channel_multiplier=1).then_inc(filled, 1)
            pool.wait_ge(filled, 7)
            pool.affine_select(out=v, in_=v, compare_op=ALU.is_ge, fill=0.0, base=31,
                               pattern=[[32, 4], [0, 32]], channel_multiplier=-1).then_inc(filled, 1)
            pool.affine_select(out=ident[:], in_=ident[:], compare_op=ALU.not_equal, fill=1.0, base=0,
                               pattern=[[-1, P]], channel_multiplier=1).then_inc(filled, 1)
            for j in range(4):
                pool.affine_select(out=stack_ident[:], in_=stack_ident[:], compare_op=ALU.not_equal, fill=1.0,
                                   base=-32 * j, pattern=[[-1, DH]], channel_multiplier=1).then_inc(filled, 1)
                pool.wait_ge(filled, 9 + 2 * j + 1)
                pool.affine_select(out=den_pick[:], in_=den_pick[:], compare_op=ALU.not_equal, fill=1.0,
                                   base=-32 * j, pattern=[[0, 1]], channel_multiplier=1).then_inc(filled, 1)
                pool.wait_ge(filled, 10 + 2 * j + 1)


def qkv_stage(nc, x, wqkvT, temp, qk_dram, v_dram, ones_mean, block_ones):
    x_v = x.rearrange("(k p) n -> p k n", p=P)
    w_v = wqkvT.rearrange("(k p) o -> p k o", p=P)
    with ExitStack() as s:
        m = Memory(nc, s, "qkv")
        w = m.sb("wqkv_sb", [P, KC, 3 * C])
        xin = m.sb("x_in", [P, 2, KC, CH])
        xc = m.sb("x_centred", [P, 2, KC, CH])
        sq = m.sb("x_squared", [P, KC, CH])
        rstd = m.sb("x_rstd", [P, CH])
        sd = m.sb("x_deviation", [P, CH])
        eps = m.sb("ln_eps", [P, 1])
        norm = m.sb("qk_norm", [P, CH])
        nm = m.sb("qk_norm_floored", [P, CH])
        qsq = m.sb("qk_squared", [P, 2, CH])
        rn = m.sb("qk_rnorm", [P, CH])
        qn = m.sb("qk_unit", [P, 2, CH])
        tcol = m.sb("temp_col", [P, 2])
        scale = m.sb("qk_scale", [P, 4])
        parts = m.sb("qk_parts", [P, 4, 2, N], F16)
        v_sb = m.sb("v_sb", [P, HEADS, NT, DH])
        mean_ps = m.ps("mean_ps", [P, CH])
        var_ps = m.ps("var_ps", [P, CH])
        qk_ps = m.ps("qk_ps", [P, 2, CH])
        n2_ps = m.ps("n2_ps", [P, CH])
        v_ps = m.ps("v_ps", [P, 2, 2, C])
        w_loaded, t_loaded = m.sem("w_loaded"), m.sem("t_loaded")
        x_loaded = [m.sem("x_loaded0"), m.sem("x_loaded1")]
        scale_ready = m.sem("scale_ready")
        eps_ready, sd_ready, norm_ready, floored = m.sem("eps_ready"), m.sem("sd_ready"), m.sem("norm_ready"), m.sem("floored")
        mean_ready, centred, squared = m.sem("mean_ready"), m.sem("centred"), m.sem("squared")
        var_ready, rstd_ready, normed = m.sem("var_ready"), m.sem("rstd_ready"), m.sem("normed")
        qk_ready, qk_squared, n2_ready = m.sem("qk_ready"), m.sem("qk_squared"), m.sem("n2_ready")
        rn_ready, unit_ready = m.sem("rn_ready"), m.sem("unit_ready")
        high_ready, low_ready = m.sem("high_ready"), m.sem("low_ready")
        v_ready, v_copied, stored = m.sem("v_ready"), m.sem("v_copied"), m.sem("stored")
        block = s.enter_context(nc.Block())

        @block.sync
        def _(sp):
            sp.dma_start(w[:], w_v).then_inc(w_loaded, 16)
            for g in range(2):
                for h in range(4):
                    sp.dma_start(tcol[32 * h:32 * h + 32, g:g + 1],
                                 temp[4 * g + h:4 * g + h + 1].rearrange("(a b) -> a b", a=1).to_broadcast([32, 1]))\
                      .then_inc(t_loaded, 16)
            with sp.Fori(0, NCH // 2) as i:
                for b in range(2):
                    sp.wait_ge(centred, 2 * i + b + 1)
                    sp.dma_start(xin[:, b], x_v[:, :, bass.ds((2 * i + b) * CH, CH)]).then_inc(x_loaded[b], 16)
            sp.wait_ge(high_ready, 4 * NCH + 1)
            sp.wait_ge(low_ready, 4 * NCH + 1)
            for g in range(4):
                for part in range(2):
                    sp.dma_start(qk_dram[g, part], parts[:, g, part]).then_inc(stored, 16)
            sp.wait_ge(v_copied, 2 * NCH + 1)
            for h in range(HEADS):
                sp.dma_start(v_dram[h], v_sb[:, h].rearrange("p t d -> p (t d)")).then_inc(stored, 16)
            sp.wait_ge(stored, 16 * (8 + HEADS) + 1)

        @block.tensor
        def _(pe):
            pe.wait_ge(w_loaded, 17)
            with pe.Fori(0, NCH // 2) as i:
                for b in range(2):
                    n = 2 * i + b
                    pe.wait_ge(x_loaded[b], 16 * i + 16 + 1)
                    pe.wait_ge(centred, n + 1)
                    for k in range(KC):
                        mm = nc.tensor.matmul(mean_ps[:], ones_mean[:], xin[:, b, k], start=k == 0, stop=k == KC - 1)
                    mm.then_inc(mean_ready, 1)
                    pe.wait_ge(squared, n + 2)
                    pe.wait_ge(sd_ready, n + 1)
                    for k in range(KC):
                        mm = nc.tensor.matmul(var_ps[:], ones_mean[:], sq[:, k], start=k == 0, stop=k == KC - 1)
                    mm.then_inc(var_ready, 1)
                    pe.wait_ge(normed, n + 2)

                    def norm2(g):
                        pe.wait_ge(qk_squared, 4 * n + g + 2)
                        pe.wait_ge(norm_ready, 4 * n + g + 1)
                        nc.tensor.matmul(n2_ps[:], block_ones[:], qsq[:, g % 2], start=True, stop=True)\
                            .then_inc(n2_ready, 1)

                    def values(half):
                        pe.wait_ge(v_copied, 2 * n + 1)
                        for j in range(2):
                            t = 2 * half + j
                            for k in range(KC):
                                mm = nc.tensor.matmul(v_ps[:, half, j], xc[:, b, k, t * P:(t + 1) * P],
                                                      w[:, k, 2 * C:3 * C], start=k == 0, stop=k == KC - 1)
                        mm.then_inc(v_ready, 1)

                    for g in range(4):
                        pe.wait_ge(unit_ready, 4 * n + max(g - 1, 0) + 1)
                        for k in range(KC):
                            mm = nc.tensor.matmul(qk_ps[:, g % 2], w[:, k, g * P:(g + 1) * P], xc[:, b, k],
                                                  start=k == 0, stop=k == KC - 1)
                        mm.then_inc(qk_ready, 1)
                        if g == 0:
                            values(0)
                        if g == 1:
                            values(1)
                        if g >= 1:
                            norm2(g - 1)
                    norm2(3)

        def part_of(g, part, n):
            if g >= 2:
                return parts[:, g, part, bass.ds(n * CH, CH)]
            return parts[:, g, part].rearrange("p (r c) -> p c r", r=16)[:, bass.ds(n * 32, 32), :]

        def unit_of(g):
            return qn[:, g % 2] if g >= 2 else qn[:, g % 2].rearrange("p (c r) -> p c r", r=16)

        def high(act, n, g):
            act.wait_ge(n2_ready, 4 * n + g + 2)
            act.wait_ge(floored, 4 * n + g + 1)
            nc.scalar.activation(norm[:], n2_ps[:], ACT.Sqrt).then_inc(norm_ready, 1)
            act.wait_ge(unit_ready, 4 * n + g + 2)
            act.wait_ge(eps_ready, 2)
            nc.scalar.activation(part_of(g, 0, n), unit_of(g), ACT.Copy).then_inc(high_ready, 1)

        @block.scalar
        def _(act):
            act.wait_ge(eps_ready, 2)
            with act.Fori(0, NCH // 2) as i:
                for b in range(2):
                    n = 2 * i + b
                    act.wait_ge(centred, n + 2)
                    act.wait_ge(var_ready, n + 1)
                    for k in range(KC):
                        a = nc.scalar.activation(sq[:, k], xc[:, b, k], ACT.Square)
                    a.then_inc(squared, 1)
                    act.wait_ge(var_ready, n + 2)
                    act.wait_ge(rstd_ready, n + 1)
                    nc.scalar.activation(sd[:], var_ps[:], ACT.Sqrt, bias=eps[:]).then_inc(sd_ready, 1)
                    for g in range(4):
                        act.wait_ge(qk_ready, 4 * n + g + 2)
                        act.wait_ge(n2_ready, 4 * n + max(g - 1, 0) + 1)
                        nc.scalar.activation(qsq[:, g % 2], qk_ps[:, g % 2], ACT.Square).then_inc(qk_squared, 1)
                        if g in (1, 2):
                            half = g - 1
                            act.wait_ge(v_ready, 2 * n + half + 2)
                            act.wait_ge(eps_ready, 2)
                            for j in range(2):
                                a = nc.scalar.activation(
                                    v_sb[:, :, bass.ds(4 * n + 2 * half + j, 1), :].rearrange("p h o d -> p (h o) d"),
                                    v_ps[:, half, j].rearrange("p (h d) -> p h d", h=HEADS), ACT.Copy)
                            a.then_inc(v_copied, 1)
                        if g >= 1:
                            high(act, n, g - 1)
                    high(act, n, 3)

        @block.vector
        def _(dve):
            dve.memset(eps[:], 1e-6).then_inc(eps_ready, 1)
            dve.wait_ge(t_loaded, 16 * 8 + 1)
            dve.tensor_scalar(scale[:, 0:2], tcol[:], QS, None, ALU.mult).then_inc(scale_ready, 1)
            dve.memset(scale[:, 2:4], KS).then_inc(scale_ready, 1)
            dve.wait_ge(scale_ready, 3)
            with dve.Fori(0, NCH // 2) as i:
                for b in range(2):
                    n = 2 * i + b
                    dve.wait_ge(mean_ready, n + 2)
                    for k in range(KC):
                        d = dve.tensor_tensor(xc[:, b, k], xin[:, b, k], mean_ps[:], ALU.subtract)
                    d.then_inc(centred, 1)
                    dve.wait_ge(sd_ready, n + 2)
                    dve.reciprocal(rstd[:], sd[:]).then_inc(rstd_ready, 1)
                    dve.wait_ge(rstd_ready, n + 2)
                    dve.wait_ge(squared, n + 2)
                    for k in range(KC):
                        d = dve.tensor_tensor(xc[:, b, k], xc[:, b, k], rstd[:], ALU.mult)
                    d.then_inc(normed, 1)
                    for g in range(4):
                        dve.wait_ge(norm_ready, 4 * n + g + 2)
                        dve.tensor_scalar(nm[:], norm[:], 1e-12, None, ALU.max).then_inc(floored, 1)
                        dve.wait_ge(floored, 4 * n + g + 2)
                        dve.reciprocal(rn[:], nm[:]).then_inc(rn_ready, 1)
                        dve.wait_ge(rn_ready, 4 * n + g + 2)
                        dve.wait_ge(low_ready, 4 * n + max(g - 1, 0) + 1)
                        dve.scalar_tensor_tensor(qn[:, g % 2], rn[:], scale[:, g:g + 1], qk_ps[:, g % 2],
                                                 ALU.mult, ALU.mult).then_inc(unit_ready, 1)
                        dve.wait_ge(high_ready, 4 * n + g + 2)
                        dve.wait_ge(unit_ready, 4 * n + g + 2)
                        dve.tensor_tensor(part_of(g, 1, n), unit_of(g), part_of(g, 0, n), ALU.subtract)\
                            .then_inc(low_ready, 1)


def attention_stage(nc, passed, temp, qk_dram, v_dram, attn, stack_ident, den_pick, ident):
    PAIRS = NT // 2
    QUADS = NT // 4
    NQ = 3
    with ExitStack() as s:
        m = Memory(nc, s, "attention")
        qst = m.sb("q_stack", [P, 2, N], F16)
        kst = m.sb("k_stack", [P, 2, N], F16)
        vb = m.sb("v_head", [P, 2, NT, DH])
        tb = m.sb("temp_all", [P, HEADS])
        nbias = m.sb("neg_bound", [P, HEADS])
        tneg = m.sb("temp_neg", [P, HEADS])
        tneg_ready = m.sem("tneg_ready")
        probs = m.sb("probs", [P, 2, 4, CH])
        half = m.sb("half_sums", [P, 2, 2, CH])
        quad = m.sb("quad_sums", [P, 2, CH])
        oc = m.sb("o_copy", [P, CH])
        dc = m.sb("den_copy", [P, CH])
        rden = m.sb("rden", [P, 4, 1])
        ones32 = m.sb("ones32", [P, DH])
        s_ps = m.ps("s_ps", [P, 2, 2, CH])
        o_ps = m.ps("o_ps", [P, CH])
        den_ps = m.ps("den_ps", [P, CH])
        t_ps = m.ps("t_ps", [P, 4, DH + 1])
        stacks_loaded = [m.sem("stacks_loaded0"), m.sem("stacks_loaded1")]
        temp_loaded, bias_ready = m.sem("temp_loaded"), m.sem("bias_ready")
        s_ready, exp_done, pv_done = m.sem("s_ready"), m.sem("exp_done"), m.sem("pv_done")
        half_done, quad_done, den_done = m.sem("half_done"), m.sem("quad_done"), m.sem("den_done")
        o_copied, t_ready, attn_done, rden_done = m.sem("o_copied"), m.sem("t_ready"), m.sem("attn_done"), m.sem("rden_done")
        block = s.enter_context(nc.Block())

        @block.sync
        def _(sp):
            sp.dma_start(tb[:], temp.rearrange("(a h) -> a h", a=1).to_broadcast([P, HEADS])).then_inc(temp_loaded, 16)
            for h in range(HEADS):
                b, g, r = h % 2, h // 4, 32 * (h % 4)
                if h >= 2:
                    sp.wait_ge(den_done, (h - 1) * NCH * QUADS + 1)
                for j in range(4):
                    rows = slice(32 * j, 32 * j + 32)
                    sp.dma_start(qst[rows, b], qk_dram[g, j // 2, r:r + 32]).then_inc(stacks_loaded[b], 16)
                    sp.dma_start(kst[rows, b], qk_dram[2 + g, j % 2, r:r + 32]).then_inc(stacks_loaded[b], 16)
                sp.dma_start(vb[:, b].rearrange("p t d -> p (t d)"), v_dram[h]).then_inc(stacks_loaded[b], 16)

        @block.tensor
        def _(pe):
            pe.wait_ge(bias_ready, 3)
            with pe.Fori(0, HEADS // 2) as hp:
                for b in range(2):
                    pe.wait_ge(stacks_loaded[b], 16 * 9 * (hp + 1) + 1)
                    pe.sem_inc(passed, 1)
                    with pe.Fori(0, NCH) as qc:
                        G = (2 * hp + b) * NCH + qc

                        def scores(u):
                            pe.wait_ge(exp_done, G * PAIRS + u + 1)
                            for j in range(2):
                                t = 2 * u + j
                                mm = nc.tensor.matmul(s_ps[:, u % 2, j], kst[:, b, t * P:(t + 1) * P],
                                                      qst[:, b, bass.ds(qc * CH, CH)], start=True, stop=True)
                            mm.then_inc(s_ready, 1)

                        def values(w):
                            pe.wait_ge(exp_done, G * PAIRS + 2 * w + 3 + 1)
                            if w == 0:
                                pe.wait_ge(o_copied, 2 * G + 1)
                            for j in range(4):
                                mm = nc.tensor.matmul(o_ps[32 * j:32 * j + 32], vb[:, b, 4 * w + j], probs[:, w % 2, j],
                                                      start=w == 0, stop=w == QUADS - 1, skip_group_check=True)
                            mm.then_inc(pv_done, 1)

                        def dens(w):
                            j = w % 4
                            pe.wait_ge(quad_done, G * QUADS + w + 2)
                            nc.tensor.matmul(den_ps[32 * j:32 * j + 32], ones32[:], quad[:, w % 2],
                                             start=w < 4, stop=w >= QUADS - 4, skip_group_check=True).then_inc(den_done, 1)

                        for u in range(PAIRS):
                            scores(u)
                            if u >= 3 and u % 2:
                                values((u - 3) // 2)
                            if u >= 6 and u % 2 == 0:
                                dens((u - 6) // 2)
                        values(QUADS - 1)
                        for w in range(QUADS - 3, QUADS):
                            dens(w)
                        pe.wait_ge(o_copied, 2 * G + 2 + 1)
                        pe.wait_ge(attn_done, G + 1)
                        for blk in range(4):
                            cols = slice(blk * P, (blk + 1) * P)
                            nc.tensor.matmul(t_ps[:, blk, 0:DH], oc[:, cols], stack_ident[:], start=True, stop=True,
                                             skip_group_check=True)
                            mm = nc.tensor.matmul(t_ps[:, blk, DH:DH + 1], dc[:, cols], den_pick[:], start=True,
                                                  stop=True, skip_group_check=True)
                        mm.then_inc(t_ready, 1)

        @block.scalar
        def _(act):
            act.wait_ge(bias_ready, 3)
            act.sem_inc(exp_done, 1)
            with act.Fori(0, HEADS) as h:
                with act.Fori(0, NCH) as qc:
                    G = h * NCH + qc
                    for u in range(PAIRS):
                        w = u // 2
                        act.wait_ge(s_ready, G * PAIRS + u + 2)
                        if u % 2 == 0:
                            act.wait_ge(pv_done, G * QUADS + max(w - 1, 0) + 1)
                            act.wait_ge(half_done, G * QUADS + max(w - 1, 0) + 1)
                        act.sem_inc(passed, 1)
                        nc.scalar.activation(probs[:, w % 2, 2 * (u % 2):2 * (u % 2) + 2], s_ps[:, u % 2], ACT.Exp,
                                             bias=nbias[:, bass.ds(h, 1)], scale=1.0 / (QS * KS)).then_inc(exp_done, 1)

        @block.gpsimd
        def _(pool):
            with pool.Fori(0, HEADS * NCH) as G:
                for w in range(QUADS):
                    pool.wait_ge(half_done, G * QUADS + w + 2)
                    pool.wait_ge(den_done, G * QUADS + max(w - 1, 0) + 1)
                    pool.tensor_tensor(quad[:, w % 2], half[:, w % 2, 0], half[:, w % 2, 1], ALU.add).then_inc(quad_done, 1)

        @block.vector
        def _(dve):
            dve.memset(ones32[:], 1.0).then_inc(bias_ready, 1)
            dve.wait_ge(temp_loaded, 17)
            dve.tensor_scalar(tneg[:], tb[:], -1.0, None, ALU.mult).then_inc(tneg_ready, 1)
            dve.wait_ge(tneg_ready, 2)
            dve.tensor_tensor(nbias[:], tb[:], tneg[:], ALU.min).then_inc(bias_ready, 1)
            with dve.Fori(0, HEADS) as h:
                with dve.Fori(0, NCH) as qc:
                    G = h * NCH + qc
                    for w in range(QUADS):
                        dve.wait_ge(exp_done, G * PAIRS + 2 * w + 3 + 1)
                        dve.wait_ge(quad_done, G * QUADS + max(w - 1, 0) + 1)
                        dve.tensor_tensor(half[:, w % 2], probs[:, w % 2, 0:2], probs[:, w % 2, 2:4], ALU.add)\
                            .then_inc(half_done, 1)
                    dve.wait_ge(t_ready, G + 1)
                    dve.wait_ge(pv_done, (G + 1) * QUADS + 1)
                    dve.tensor_copy(oc[:], o_ps[:]).then_inc(o_copied, 1)
                    dve.wait_ge(den_done, (G + 1) * QUADS + 1)
                    dve.tensor_copy(dc[:], den_ps[:]).then_inc(o_copied, 1)
                    dve.wait_ge(t_ready, G + 2)
                    dve.reciprocal(rden[:], t_ps[:, :, DH:DH + 1]).then_inc(rden_done, 1)
                    dve.wait_ge(rden_done, G + 2)
                    dst = attn[:].rearrange("p k r (h d) -> p r k h d", h=HEADS)[:, bass.ds(2 * qc, 2), :, bass.ds(h, 1), :]\
                        .rearrange("p r k o d -> p r k (o d)")
                    dve.tensor_tensor(dst, t_ps[:, :, 0:DH].rearrange("p (r k) d -> p r k d", r=2),
                                      rden[:].rearrange("p (r k) o -> p r k o", r=2).to_broadcast([P, 2, KC, DH]),
                                      ALU.mult).then_inc(attn_done, 1)


def projection_stage(nc, x, wprojT, attn, res):
    with ExitStack() as s:
        m = Memory(nc, s, "projection")
        w = m.sb("wproj_sb", [P, KC, C])
        o_ps = m.ps("proj_ps", [P, 2, KC, CH])
        w_loaded, x_loaded = m.sem("w_loaded"), m.sem("x_loaded")
        projected, added = m.sem("projected"), m.sem("added")
        block = s.enter_context(nc.Block())

        @block.sync
        def _(sp):
            sp.dma_start(w[:], wprojT.rearrange("(k p) o -> p k o", p=P)).then_inc(w_loaded, 16)
            sp.dma_start(res[:], x.rearrange("(k p) n -> p k n", p=P)).then_inc(x_loaded, 16)

        @block.tensor
        def _(pe):
            pe.wait_ge(w_loaded, 17)
            with pe.Fori(0, NCH // 2) as i:
                for b in range(2):
                    n = 2 * i + b
                    pe.wait_ge(added, 2 * i + 1)
                    for o in range(KC):
                        for k in range(KC):
                            mm = nc.tensor.matmul(o_ps[:, b, o], w[:, k, o * P:(o + 1) * P],
                                                  attn[:, k, bass.ds(2 * n, 2), :].rearrange("p r c -> p (r c)"),
                                                  start=k == 0, stop=k == KC - 1)
                    mm.then_inc(projected, 1)

        @block.vector
        def _(dve):
            dve.wait_ge(x_loaded, 17)
            with dve.Fori(0, NCH // 2) as i:
                for b in range(2):
                    n = 2 * i + b
                    dve.wait_ge(projected, n + 2)
                    chunk = res[:, :, bass.ds(n * CH, CH)]
                    dve.tensor_tensor(chunk, chunk, o_ps[:, b], ALU.add).then_inc(added, 1)


def layer_norm_stage(nc, name, src, dst, eps_value, ones_mean, col_sum=None):
    with ExitStack() as s:
        m = Memory(nc, s, name)
        eps = m.sb("ln_eps", [P, 1])
        xc = m.sb("x_centred", [P, 2, KC, CH])
        sq = m.sb("x_squared", [P, 2, KC, CH])
        sd = m.sb("x_deviation", [P, 2, CH])
        rstd = m.sb("x_rstd", [P, 2, CH])
        mean_ps = m.ps("mean_ps", [P, 2, CH])
        var_ps = m.ps("var_ps", [P, 2, CH])
        eps_ready, mean_ready, centred = m.sem("eps_ready"), m.sem("mean_ready"), m.sem("centred")
        squared, var_ready, sd_ready = m.sem("squared"), m.sem("var_ready"), m.sem("sd_ready")
        rstd_ready, normed = m.sem("rstd_ready"), m.sem("normed")
        block = s.enter_context(nc.Block())

        @block.tensor
        def _(pe):
            with pe.Fori(0, NCH // 2) as i:
                for b in range(2):
                    pe.wait_ge(centred, 2 * i + 1)
                    for k in range(KC):
                        mm = nc.tensor.matmul(mean_ps[:, b], ones_mean[:], src[:, k, bass.ds((2 * i + b) * CH, CH)],
                                              start=k == 0, stop=k == KC - 1)
                    mm.then_inc(mean_ready, 1)
                for b in range(2):
                    pe.wait_ge(squared, 2 * i + b + 2)
                    pe.wait_ge(sd_ready, 2 * i + 1)
                    for k in range(KC):
                        mm = nc.tensor.matmul(var_ps[:, b], ones_mean[:], sq[:, b, k], start=k == 0, stop=k == KC - 1)
                    mm.then_inc(var_ready, 1)

        @block.scalar
        def _(act):
            act.wait_ge(eps_ready, 2)
            with act.Fori(0, NCH // 2) as i:
                for b in range(2):
                    act.wait_ge(centred, 2 * i + b + 2)
                    act.wait_ge(var_ready, 2 * i + 1)
                    nc.scalar.activation(sq[:, b], xc[:, b], ACT.Square).then_inc(squared, 1)
                for b in range(2):
                    act.wait_ge(var_ready, 2 * i + b + 2)
                    act.wait_ge(rstd_ready, 2 * i + 1)
                    nc.scalar.activation(sd[:, b], var_ps[:, b], ACT.Sqrt, bias=eps[:]).then_inc(sd_ready, 1)

        @block.vector
        def _(dve):
            dve.memset(eps[:], eps_value).then_inc(eps_ready, 1)
            with dve.Fori(0, NCH // 2) as i:
                for b in range(2):
                    n = 2 * i + b
                    dve.wait_ge(mean_ready, n + 2)
                    dve.wait_ge(normed, 2 * i + 1)
                    dve.tensor_tensor(xc[:, b], src[:, :, bass.ds(n * CH, CH)],
                                      mean_ps[:, b:b + 1].to_broadcast([P, KC, CH]), ALU.subtract).then_inc(centred, 1)
                for b in range(2):
                    n = 2 * i + b
                    dve.wait_ge(sd_ready, n + 2)
                    dve.reciprocal(rstd[:, b], sd[:, b]).then_inc(rstd_ready, 1)
                    dve.wait_ge(centred, n + 2)
                    dve.wait_ge(rstd_ready, n + 2)
                    dve.tensor_tensor(dst[:, :, bass.ds(n * CH, CH)], xc[:, b],
                                      rstd[:, b:b + 1].to_broadcast([P, KC, CH]), ALU.mult).then_inc(normed, 1)
            if col_sum is not None:
                dve.wait_ge(normed, NCH + 1)
                dve.reduce_sum(col_sum[:], dst[:], axis=AX.X).then_inc(normed, 1)


def routing_stage(nc, a, col_sum, top_w, top_i):
    E = 8
    CAPACITY = float(-(-N * 5 // (4 * E)))
    with ExitStack() as s:
        m = Memory(nc, s, "routing")
        wr = m.sb("wr_sb", [P, KC, E])
        br = m.sb("br_sb", [1, E])
        mcol = m.sb("token_mean", [P, KC])
        row = m.sb("route_rows", [1, 12, E])
        one = m.sb("route_scalars", [1, 12])
        ones_row = m.sb("ones_row", [1, P])
        lg_ps = m.ps("logits_ps", [1, E])
        w_ps = m.ps("top_w_ps", [P, 2])
        loaded, mean_ready, logits_ready = m.sem("loaded"), m.sem("mean_ready"), m.sem("logits_ready")
        step, exp_in, exp_out, w_ready, ws_ready = (m.sem(x) for x in ("step", "exp_in", "exp_out", "w_ready", "ws_ready"))
        block = s.enter_context(nc.Block())

        @block.sync
        def _(sp):
            sp.dma_start(wr[:], a["wr"].rearrange("(k p) e -> p k e", p=P)).then_inc(loaded, 16)
            sp.dma_start(br[:], a["br"].rearrange("(a e) -> a e", a=1)).then_inc(loaded, 16)

        @block.tensor
        def _(pe):
            pe.wait_ge(loaded, 33)
            pe.wait_ge(mean_ready, 2)
            for k in range(KC):
                mm = nc.tensor.matmul(lg_ps[:], mcol[:, k:k + 1], wr[:, k], start=k == 0, stop=k == KC - 1)
            mm.then_inc(logits_ready, 1)
            pe.wait_ge(ws_ready, 2)
            nc.tensor.matmul(w_ps[:], ones_row[:], row[:, 9, 0:2], start=True, stop=True).then_inc(w_ready, 1)

        @block.scalar
        def _(act):
            for n, (src, dst, bias, total) in enumerate(((0, 1, 1, 2), (4, 5, 5, 6), (7, 8, 9, 10))):
                act.wait_ge(exp_in, n + 2)
                w = E if n < 2 else 2
                nc.scalar.activation(row[:, dst, 0:w], row[:, src, 0:w], ACT.Exp, bias=one[:, bias:bias + 1],
                                     accum_out=one[:, total:total + 1]).then_inc(exp_out, 1)

        @block.vector
        def _(dve):
            count = [0]

            def chain(ins):
                count[0] += 1
                ins.then_inc(step, 1)
                dve.wait_ge(step, count[0] + 1)

            dve.memset(ones_row[:], 1.0).then_inc(step, 1)
            count[0] += 1
            dve.tensor_scalar(mcol[:], col_sum[:], 1.0 / N, None, ALU.mult).then_inc(mean_ready, 1)
            dve.wait_ge(logits_ready, 2)
            chain(dve.tensor_tensor(row[:, 0], lg_ps[:], br[:], ALU.add))

            def softmax(n, src, dst, neg, total, w):
                chain(dve.reduce_max(one[:, neg - 1:neg], row[:, src, 0:w], axis=AX.X))
                dve.tensor_scalar(one[:, neg:neg + 1], one[:, neg - 1:neg], -1.0, None, ALU.mult).then_inc(exp_in, 1)
                dve.wait_ge(exp_out, n + 2)
                chain(dve.reciprocal(one[:, total + 1:total + 2], one[:, total:total + 1]))
                return dve.tensor_scalar(row[:, dst, 0:w], row[:, dst, 0:w], one[:, total + 1:total + 2], None, ALU.mult)

            chain(softmax(0, 0, 1, 1, 2, E))
            chain(dve.tensor_scalar(row[:, 2], row[:, 1], float(N), None, ALU.mult))
            chain(dve.reciprocal(row[:, 3], row[:, 2]))
            chain(dve.tensor_scalar(row[:, 3], row[:, 3], CAPACITY, 1.0, ALU.mult, ALU.min))
            chain(dve.tensor_tensor(row[:, 4], row[:, 1], row[:, 3], ALU.mult))
            chain(softmax(1, 4, 5, 5, 6, E))
            chain(dve.max(row[:, 7], row[:, 5]))
            chain(dve.max_index(top_i[:], row[:, 7], row[:, 5]))
            chain(softmax(2, 7, 8, 9, 10, 2))
            dve.tensor_copy(row[:, 9, 0:2], row[:, 8, 0:2]).then_inc(ws_ready, 1)
            dve.wait_ge(w_ready, 2)
            dve.tensor_copy(top_w[:], w_ps[:]).then_inc(step, 1)


def expert_stage(nc, a, xn, top_w, top_i, z):
    F = 512
    KF = F // P
    with ExitStack() as s:
        m = Memory(nc, s, "expert")
        w1 = m.sb("w1_sb", [P, 2, KC, F])
        w2 = m.sb("w2_sb", [P, 2, KF, C])
        b1 = m.sb("b1_sb", [P, 2, KF])
        b2 = m.sb("b2_sb", [P, 2, KC])
        b2w = m.sb("b2_weighted", [P, 2, KC])
        b2s = m.sb("b2_sum", [P, KC])
        hid = m.sb("hidden", [P, 4, CH])
        h_ps = m.ps("hidden_ps", [P, 2, CH])
        y_ps = m.ps("y_ps", [P, 2, KC, CH])
        loaded, weighted = m.sem("loaded"), m.sem("weighted")
        h_ready, h_done, y_ready, z_done = m.sem("h_ready"), m.sem("h_done"), m.sem("y_ready"), m.sem("z_done")
        block = s.enter_context(nc.Block())

        @block.sync
        def _(sp):
            for j in range(2):
                e = sp.value_load(top_i[0:1, j:j + 1], min_val=0, max_val=7)
                sp.dma_start(w1[:, j], a["w1"].rearrange("e (k p) f -> p e k f", p=P)[:, bass.ds(e, 1)]
                             .rearrange("p o k f -> p (o k) f")).then_inc(loaded, 16)
                sp.dma_start(w2[:, j], a["w2"].rearrange("e (k p) d -> p e k d", p=P)[:, bass.ds(e, 1)]
                             .rearrange("p o k d -> p (o k) d")).then_inc(loaded, 16)
                sp.dma_start(b1[:, j], a["b1"].rearrange("p (e k) -> p e k", k=KF)[:, bass.ds(e, 1)]
                             .rearrange("p o k -> p (o k)")).then_inc(loaded, 16)
                sp.dma_start(b2[:, j], a["b2"].rearrange("p (e k) -> p e k", k=KC)[:, bass.ds(e, 1)]
                             .rearrange("p o k -> p (o k)")).then_inc(loaded, 16)

        @block.tensor
        def _(pe):
            pe.wait_ge(weighted, 6)
            with pe.Fori(0, NCH // 2) as i:
                for b in range(2):
                    n = 2 * i + b

                    def out(q):
                        pe.wait_ge(h_done, 8 * n + q + 2)
                        for o in range(KC):
                            mm = nc.tensor.matmul(y_ps[:, b, o], w2[:, q // KF, q % KF, o * P:(o + 1) * P], hid[:, q % 4],
                                                  start=q == 0, stop=q == 2 * KF - 1)
                        mm.then_inc(y_ready, 1)

                    for q in range(2 * KF):
                        pe.wait_ge(h_done, 8 * n + max(q - 1, 0) + 1)
                        for k in range(KC):
                            mm = nc.tensor.matmul(h_ps[:, q % 2], w1[:, q // KF, k, (q % KF) * P:(q % KF + 1) * P],
                                                  xn[:, k, bass.ds(n * CH, CH)], start=k == 0, stop=k == KC - 1)
                        mm.then_inc(h_ready, 1)
                        if q == 2:
                            pe.wait_ge(z_done, 2 * i + 1)
                        if q >= 2:
                            out(q - 2)
                    out(2 * KF - 2)
                    out(2 * KF - 1)

        @block.scalar
        def _(act):
            act.wait_ge(loaded, 16 * 8 + 1)
            with act.Fori(0, NCH) as n:
                for q in range(2 * KF):
                    act.wait_ge(h_ready, 8 * n + q + 2)
                    act.wait_ge(y_ready, 8 * n + max(q - 3, 0) + 1)
                    nc.scalar.activation(hid[:, q % 4], h_ps[:, q % 2], ACT.Gelu,
                                         bias=b1[:, q // KF, q % KF:q % KF + 1]).then_inc(h_done, 1)

        @block.vector
        def _(dve):
            dve.wait_ge(loaded, 16 * 8 + 1)
            for j in range(2):
                dve.tensor_scalar(w2[:, j], w2[:, j], top_w[:, j:j + 1], None, ALU.mult).then_inc(weighted, 1)
                dve.tensor_scalar(b2w[:, j], b2[:, j], top_w[:, j:j + 1], None, ALU.mult).then_inc(weighted, 1)
            dve.wait_ge(weighted, 5)
            dve.tensor_tensor(b2s[:], b2w[:, 0], b2w[:, 1], ALU.add).then_inc(weighted, 1)
            dve.wait_ge(weighted, 6)
            with dve.Fori(0, NCH // 2) as i:
                for b in range(2):
                    n = 2 * i + b
                    dve.wait_ge(y_ready, 8 * n + 8 + 1)
                    for o in range(KC):
                        ins = dve.scalar_tensor_tensor(z[:, o, bass.ds(n * CH, CH)], y_ps[:, b, o], b2s[:, o:o + 1],
                                                       xn[:, o, bass.ds(n * CH, CH)], ALU.add, ALU.add)
                    ins.then_inc(z_done, 1)


def affine_residual_stage(nc, a, zn, res):
    with ExitStack() as s:
        m = Memory(nc, s, "affine_residual")
        gb = m.sb("gamma_beta", [P, 2, KC])
        loaded, scaled, added = m.sem("loaded"), m.sem("scaled"), m.sem("added")
        block = s.enter_context(nc.Block())

        @block.sync
        def _(sp):
            sp.dma_start(gb[:, 0], a["gamma"].rearrange("p k -> p k")).then_inc(loaded, 16)
            sp.dma_start(gb[:, 1], a["beta"].rearrange("p k -> p k")).then_inc(loaded, 16)

        @block.vector
        def _(dve):
            dve.wait_ge(loaded, 33)
            with dve.Fori(0, NCH) as n:
                for o in range(KC):
                    c = bass.ds(n * CH, CH)
                    dve.tensor_scalar(zn[:, o, c], zn[:, o, c], gb[:, 0, o:o + 1], gb[:, 1, o:o + 1], ALU.mult, ALU.add)\
                        .then_inc(scaled, 1)
                    dve.wait_ge(scaled, 2 * n + o + 2)
                    dve.tensor_tensor(res[:, o, c], res[:, o, c], zn[:, o, c], ALU.add).then_inc(added, 1)


W = 64
PW = W + 4
NB6 = 6 * PW


def conv_in_stage(nc, a, cn, hpad, hT, gate, ident):
    with ExitStack() as s:
        m = Memory(nc, s, "conv_in")
        w1 = m.sb("cw1_sb", [P, KC, P])
        w2 = m.sb("cw2_sb", [P, P])
        b1 = m.sb("cb1_sb", [P, 1])
        b2 = m.sb("cb2_sb", [P, 1])
        hc = m.sb("h_chunk", [P, 2, CH])
        g0 = m.sb("gate_in", [P, 2, CH])
        h_ps = m.ps("h_ps", [P, 2, CH])
        g_ps = m.ps("g_ps", [P, 2, CH])
        t_ps = m.ps("t_ps", [P, 2, 4, P])
        loaded, cleared, h_ready, h_done = m.sem("loaded"), m.sem("cleared"), m.sem("h_ready"), m.sem("h_done")
        padded, g_ready, relu_done, gate_done = m.sem("padded"), m.sem("g_ready"), m.sem("relu_done"), m.sem("gate_done")
        t_ready, t_done = m.sem("t_ready"), m.sem("t_done")
        block = s.enter_context(nc.Block())

        @block.sync
        def _(sp):
            sp.dma_start(w1[:], a["cw1T"].rearrange("(k p) o -> p k o", p=P)).then_inc(loaded, 16)
            sp.dma_start(w2[:], a["cw2T"]).then_inc(loaded, 16)
            sp.dma_start(b1[:], a["cb1"]).then_inc(loaded, 16)
            sp.dma_start(b2[:], a["cb2"]).then_inc(loaded, 16)

        @block.tensor
        def _(pe):
            pe.wait_ge(loaded, 65)
            with pe.Fori(0, NCH // 2) as i:
                for b in range(2):
                    n = 2 * i + b
                    pe.wait_ge(h_done, 2 * i + 1)
                    for k in range(KC):
                        mm = nc.tensor.matmul(h_ps[:, b], w1[:, k], cn[:, k, bass.ds(n * CH, CH)],
                                              start=k == 0, stop=k == KC - 1)
                    mm.then_inc(h_ready, 1)
                    pe.wait_ge(h_done, n + 2)
                    pe.wait_ge(relu_done, 2 * i + 1)
                    nc.tensor.matmul(g_ps[:, b], w2[:], hc[:, b], start=True, stop=True).then_inc(g_ready, 1)
                    pe.wait_ge(t_done, 2 * i + 1)
                    for j in range(4):
                        mm = nc.tensor.transpose(t_ps[:, b, j], hc[:, b, j * P:(j + 1) * P], ident[:])
                    mm.then_inc(t_ready, 1)

        @block.gpsimd
        def _(pool):
            pool.memset(hpad[:], 0.0).then_inc(cleared, 1)
            pool.memset(hT[:, 0], 0.0).then_inc(cleared, 1)
            pool.memset(hT[:, NT + 1], 0.0).then_inc(cleared, 1)
            pool.wait_ge(cleared, 4)
            with pool.Fori(0, NCH // 2) as i:
                for b in range(2):
                    n = 2 * i + b
                    pool.wait_ge(h_done, n + 2)
                    pool.tensor_copy(hpad[:].rearrange("p (y x) -> p y x", x=PW)[:, bass.ds(8 * n + 2, 8), 2:2 + W],
                                     hc[:, b].rearrange("p (y x) -> p y x", x=W)).then_inc(padded, 1)

        @block.scalar
        def _(act):
            act.wait_ge(loaded, 65)
            with act.Fori(0, NCH // 2) as i:
                for b in range(2):
                    n = 2 * i + b
                    act.wait_ge(h_ready, n + 2)
                    act.wait_ge(padded, 2 * i + 1)
                    act.wait_ge(t_ready, 2 * i + 1)
                    nc.scalar.activation(hc[:, b], h_ps[:, b], ACT.Identity, bias=b1[:]).then_inc(h_done, 1)
                    act.wait_ge(loaded, 65)
                    act.wait_ge(relu_done, n + 2)
                    nc.scalar.activation(gate[:, bass.ds(n * CH, CH)], g0[:, b], ACT.Sigmoid).then_inc(gate_done, 1)

        @block.vector
        def _(dve):
            dve.wait_ge(loaded, 65)
            dve.wait_ge(cleared, 4)
            with dve.Fori(0, NCH // 2) as i:
                for b in range(2):
                    n = 2 * i + b
                    dve.wait_ge(g_ready, n + 2)
                    dve.wait_ge(gate_done, 2 * i + 1)
                    dve.tensor_scalar(g0[:, b], g_ps[:, b], b2[:], 0.0, ALU.add, ALU.max).then_inc(relu_done, 1)
                    dve.wait_ge(t_ready, n + 2)
                    dve.tensor_copy(hT[:, bass.ds(4 * n + 1, 4)], t_ps[:, b]).then_inc(t_done, 1)


def conv_out_stage(nc, a, hpad, hT, gate, res, ident):
    with ExitStack() as s:
        m = Memory(nc, s, "conv_out")
        wo = m.sb("wout_sb", [P, C])
        bo = m.sb("bout_sb", [P, KC])
        mask = m.sb("mask", [P, 6, PW])
        hc = m.sb("h_chunk", [P, 2, 4, P])
        hw = m.sb("hT_window", [P, 2, 6, P])
        sc = m.sb("scores", [P, 2, NB6])
        mx = m.sb("score_max", [P, 2])
        nmx = m.sb("neg_max", [P, 2])
        ex = m.sb("exps", [P, 2, 6, PW])
        den = m.sb("dens", [P, 2])
        rden = m.sb("rdens", [P, 2])
        an = m.sb("weights", [P, 2, 6 * W])
        aT = m.sb("weightsT", [P, 2, 3, P])
        att = m.sb("gated", [P, CH])
        g_ps = m.ps("gram_ps", [P, 2, CH])
        t_ps = m.ps("wT_ps", [P, 2, CH])
        s_ps = m.ps("sample_ps", [P, 4, P])
        o_ps = m.ps("out_ps", [P, KC, CH])
        loaded, masked, staged = m.sem("loaded"), m.sem("masked"), m.sem("staged")
        gram_ready, sc_ready, max_ready, nmax_ready = (m.sem(x) for x in ("gram_ready", "sc_ready", "max_ready", "nmax_ready"))
        ex_ready, rden_ready, an_ready, t_ready = (m.sem(x) for x in ("ex_ready", "rden_ready", "an_ready", "t_ready"))
        aT_ready, s_ready, att_ready, o_ready, added = (m.sem(x) for x in ("aT_ready", "s_ready", "att_ready", "o_ready", "added"))
        block = s.enter_context(nc.Block())

        @block.sync
        def _(sp):
            sp.dma_start(wo[:], a["cwoT"]).then_inc(loaded, 16)
            sp.dma_start(bo[:], a["cbo"]).then_inc(loaded, 16)

        @block.gpsimd
        def _(pool):
            pool.memset(mask[:], 0.0).then_inc(masked, 1)
            for dy in range(2):
                rows = mask[W * dy:W * dy + W]
                for q, (pattern, base, mult) in enumerate((
                        ([[0, 6], [1, PW]], 0, -1), ([[0, 6], [-1, PW]], 4, 1),
                        ([[1, 6], [0, PW]], -dy, 0), ([[-1, 6], [0, PW]], 4 + dy, 0))):
                    pool.wait_ge(masked, 4 * dy + q + 2)
                    pool.affine_select(out=rows, in_=rows, compare_op=ALU.is_ge, fill=-1e30, base=base,
                                       pattern=pattern, channel_multiplier=mult).then_inc(masked, 1)
            pool.wait_ge(masked, 10)
            with pool.Fori(0, NCH // 2) as i:
                for b in range(2):
                    n = 2 * i + b
                    pool.wait_ge(s_ready, 2 * i + 1)
                    pool.tensor_copy(hc[:, b].rearrange("p t (y x) -> p (t y) x", x=W),
                                     hpad[:].rearrange("p (y x) -> p y x", x=PW)[:, bass.ds(8 * n + 2, 8), 2:2 + W])\
                        .then_inc(staged, 1)
                    pool.tensor_copy(hw[:, b], hT[:, bass.ds(4 * n, 6)]).then_inc(staged, 1)

        @block.tensor
        def _(pe):
            pe.wait_ge(loaded, 33)
            with pe.Fori(0, NCH // 2) as i:
                for b in range(2):
                    n = 2 * i + b
                    for half in range(2):
                        H = 2 * n + half
                        pe.wait_ge(staged, 2 * n + 2 + 1)
                        pe.wait_ge(sc_ready, H + 1)
                        for j in range(2):
                            t = 2 * half + j
                            mm = nc.tensor.matmul(g_ps[:, j, 0:NB6], hc[:, b, t],
                                                  hpad[:, bass.ds((8 * n + 2 * t) * PW, NB6)], start=True, stop=True)
                        mm.then_inc(gram_ready, 1)
                        pe.wait_ge(an_ready, H + 2)
                        pe.wait_ge(aT_ready, H + 1)
                        for j in range(2):
                            for q in range(3):
                                mm = nc.tensor.transpose(t_ps[:, j, q * P:(q + 1) * P], an[:, j, q * P:(q + 1) * P], ident[:])
                        mm.then_inc(t_ready, 1)
                        pe.wait_ge(aT_ready, H + 2)
                        if half == 0:
                            pe.wait_ge(att_ready, n + 1)
                        for j in range(2):
                            t = 2 * half + j
                            for q in range(3):
                                mm = nc.tensor.matmul(s_ps[:, t], hw[:, b, t + q], aT[:, j, q], start=q == 0, stop=q == 2,
                                                      skip_group_check=True)
                        if half == 1:
                            mm.then_inc(s_ready, 1)
                    pe.wait_ge(att_ready, n + 2)
                    pe.wait_ge(added, n + 1)
                    for o in range(KC):
                        mm = nc.tensor.matmul(o_ps[:, o], wo[:, o * P:(o + 1) * P], att[:], start=True, stop=True)
                    mm.then_inc(o_ready, 1)

        @block.scalar
        def _(act):
            with act.Fori(0, 2 * NCH) as H:
                act.wait_ge(nmax_ready, H + 2)
                act.wait_ge(an_ready, H + 1)
                for j in range(2):
                    e = nc.scalar.activation(ex[:, j].rearrange("p y x -> p (y x)"), sc[:, j], ACT.Exp,
                                             bias=nmx[:, j:j + 1], accum_out=den[:, j:j + 1])
                e.then_inc(ex_ready, 1)
                act.wait_ge(t_ready, H + 2)
                nc.scalar.activation(aT[:].rearrange("p j q c -> p j (q c)"), t_ps[:, :, 0:3 * P], ACT.Copy)\
                    .then_inc(aT_ready, 1)

        @block.vector
        def _(dve):
            dve.wait_ge(masked, 10)
            dve.wait_ge(loaded, 33)
            with dve.Fori(0, NCH) as n:
                for half in range(2):
                    H = 2 * n + half
                    dve.wait_ge(gram_ready, H + 2)
                    dve.wait_ge(ex_ready, H + 1)
                    dve.scalar_tensor_tensor(sc[:], g_ps[:, :, 0:NB6], float(P) ** -0.5,
                                             mask[:].rearrange("p y x -> p (y x)").rearrange("p (o z) -> p o z", o=1)
                                             .to_broadcast([P, 2, NB6]), ALU.mult, ALU.add).then_inc(sc_ready, 1)
                    dve.wait_ge(sc_ready, H + 2)
                    dve.reduce_max(mx[:], sc[:], axis=AX.X).then_inc(max_ready, 1)
                    dve.wait_ge(max_ready, H + 2)
                    dve.tensor_scalar(nmx[:], mx[:], -1.0, None, ALU.mult).then_inc(nmax_ready, 1)
                    dve.wait_ge(ex_ready, H + 2)
                    dve.reciprocal(rden[:], den[:]).then_inc(rden_ready, 1)
                    dve.wait_ge(rden_ready, H + 2)
                    dve.wait_ge(t_ready, H + 1)
                    for j in range(2):
                        ins = dve.tensor_scalar(an[:, j].rearrange("p (y x) -> p y x", x=W), ex[:, j, :, 2:2 + W],
                                                rden[:, j:j + 1], None, ALU.mult)
                    ins.then_inc(an_ready, 1)
                dve.wait_ge(s_ready, n + 2)
                dve.wait_ge(o_ready, n + 1)
                dve.tensor_tensor(att[:], s_ps[:].rearrange("p t x -> p (t x)"), gate[:, bass.ds(n * CH, CH)], ALU.mult)\
                    .then_inc(att_ready, 1)
                dve.wait_ge(o_ready, n + 2)
                for o in range(KC):
                    c = res[:, o, bass.ds(n * CH, CH)]
                    ins = dve.scalar_tensor_tensor(c, o_ps[:, o], bo[:, o:o + 1], c, ALU.add, ALU.add)
                ins.then_inc(added, 1)


EDGES = 1048576
EC = EDGES // P
BITS = 12
CC = 2048
SEG = 64
KEEP = 16
KEPT = EC * KEEP // SEG
LISTED = 64
HB = 256
U32 = mybir.dt.uint32
BF16 = mybir.dt.bfloat16
RMAX = bass.bass_isa.ReduceOp.max


def edge_keys_stage(nc, passed, edges, keys_dram, plan):
    e_v = edges.rearrange("t (p c) -> t p c", p=P)
    SEGS = CC // SEG
    with ExitStack() as s:
        m = Memory(nc, s, "keys")
        raw = m.sb("raw", [P, 2, 2, CC], I32)
        sp1 = m.sb("src_plus_1", [P, CC])
        kk = m.sb("key_any", [P, CC])
        kb = m.sb("key_chunk", [P, 2, CC])
        work = m.sb("key_left", [P, CC])
        cand = m.sb("packed", [P, 2, SEGS, KEEP])
        ki = m.sb("packed_int", [P, SEGS * KEEP], I32)
        ksrc = m.sb("packed_src", [P, SEGS * KEEP], I32)
        cl = m.sb("listed_from", [P, SEGS * KEEP])
        l1 = m.sb("list_part", [P, 2, KEEP])
        lc = m.sb("list_parts", [P, EC // CC, 2 * KEEP])
        lf = m.sb("list", [P, LISTED])
        left = m.sb("left_over", [P, EC // CC, 4])
        lmax = m.sb("left_max", [P, 2])
        lall = m.sb("left_all", [P, 2])
        pf = m.sb("plan_f", [P, 4])
        loaded = [m.sem("loaded0"), m.sem("loaded1")]
        step, keyed, packed, stored, done = m.sem("step"), m.sem("keyed"), m.sem("packed"), m.sem("stored"), m.sem("done")
        listed, left_ready, all_ready = m.sem("listed"), m.sem("left_ready"), m.sem("all_ready")
        block = s.enter_context(nc.Block())

        @block.sync
        def _(sp):
            with sp.Fori(0, EC // CC // 2) as i:
                for b in range(2):
                    n = 2 * i + b
                    sp.wait_ge(keyed, 2 * i + 1)
                    for t in range(2):
                        sp.dma_start(raw[:, b, t], e_v[t, :, bass.ds(n * CC, CC)]).then_inc(loaded[b], 16)
            with sp.Fori(0, EC // CC // 2) as i:
                for b in range(2):
                    n = 2 * i + b
                    sp.wait_ge(keyed, n + 2)
                    sp.dma_start(keys_dram[:, bass.ds(n * CC, CC)], kb[:, b]).then_inc(stored, 16)
                    sp.wait_ge(packed, n + 2)
                    sp.dma_start(keys_dram[:, bass.ds(n * (SEGS * KEEP) + EC, SEGS * KEEP)],
                                 cand[:, b].rearrange("p s k -> p (s k)")).then_inc(stored, 16)
            sp.wait_ge(listed, 2)
            sp.dma_start(keys_dram[:, EC + KEPT:EC + KEPT + LISTED], lf[:]).then_inc(stored, 16)
            sp.wait_ge(stored, 16 * (2 * EC // CC + 1) + 1)

        @block.gpsimd
        def _(pool):
            pool.wait_ge(left_ready, 2)
            pool.partition_all_reduce(lall[:], lmax[:], P, RMAX).then_inc(all_ready, 1)

        @block.vector
        def _(dve):
            STEPS = 3 + 4 * SEGS + 4 + 4 * 2 + 1
            with dve.Fori(0, EC // CC // 2) as i:
                for b in range(2):
                    n = 2 * i + b
                    base = n * STEPS
                    at = [0]

                    def chain(ins):
                        at[0] += 1
                        ins.then_inc(step, 1)
                        dve.wait_ge(step, base + at[0] + 1)
                        dve.sem_inc(passed, 1)

                    dve.wait_ge(loaded[b], 32 * i + 32 + 1)
                    chain(dve.tensor_scalar(sp1[:], raw[:, b, 0], 4095, 1, ALU.min, ALU.add))
                    chain(dve.scalar_tensor_tensor(kk[:], raw[:, b, 1], 4096.0, sp1[:], ALU.mult, ALU.add))
                    dve.wait_ge(stored, 64 * i + 1)
                    dve.scalar_tensor_tensor(kb[:, b], raw[:, b, 1], 4096.0, kk[:], ALU.is_lt, ALU.mult).then_inc(keyed, 1)
                    dve.wait_ge(keyed, n + 2)
                    chain(dve.tensor_copy(work[:], kb[:, b]))
                    for half in range(2):
                        for g in range(SEGS):
                            ins = dve.max(cand[:, b, g, 8 * half:8 * half + 8], work[:, g * SEG:(g + 1) * SEG])
                            at[0] += 1
                            ins.then_inc(step, 1)
                        dve.wait_ge(step, base + at[0] + 1)
                        dve.sem_inc(passed, 1)
                        for g in range(SEGS):
                            part = work[:, g * SEG:(g + 1) * SEG]
                            ins = dve.match_replace(part, cand[:, b, g, 8 * half:8 * half + 8], part, 0.0)
                            at[0] += 1
                            ins.then_inc(step, 1)
                        dve.wait_ge(step, base + at[0] + 1)
                        dve.sem_inc(passed, 1)
                    flat = cand[:, b].rearrange("p s k -> p (s k)")
                    dve.reduce_max(left[:, bass.ds(n, 1), 0:1].rearrange("p a c -> p (a c)"), work[:], axis=AX.X).then_inc(packed, 1)
                    chain(dve.tensor_scalar(ki[:], flat, 1.0, None, ALU.subtract))
                    chain(dve.tensor_scalar(ksrc[:], ki[:], 4095, None, ALU.bitwise_and))
                    chain(dve.scalar_tensor_tensor(cl[:], ksrc[:], 4095.0, flat, ALU.is_lt, ALU.mult))
                    for h in range(2):
                        part = cl[:, h * 256:(h + 1) * 256]
                        for r in range(2):
                            chain(dve.max(l1[:, h, 8 * r:8 * r + 8], part))
                            chain(dve.match_replace(part, l1[:, h, 8 * r:8 * r + 8], part, 0.0))
                    chain(dve.reduce_max(left[:, bass.ds(n, 1), 1:2].rearrange("p a c -> p (a c)"), cl[:], axis=AX.X))
                    chain(dve.tensor_copy(lc[:, bass.ds(n, 1)].rearrange("p a c -> p (a c)"),
                                          l1[:].rearrange("p h k -> p (h k)")))
                    assert at[0] == STEPS, (at[0], STEPS)
            at = [STEPS * (EC // CC)]

            def chain(ins):
                at[0] += 1
                ins.then_inc(step, 1)
                dve.wait_ge(step, at[0] + 1)

            flat = lc[:].rearrange("p n k -> p (n k)")
            for r in range(LISTED // 8):
                chain(dve.max(lf[:, 8 * r:8 * r + 8], flat))
                ins = dve.match_replace(flat, lf[:, 8 * r:8 * r + 8], flat, 0.0)
                if r == LISTED // 8 - 1:
                    ins.then_inc(listed, 1)
                    dve.wait_ge(listed, 2)
                else:
                    chain(ins)
            chain(dve.reduce_max(lmax[:, 0:1], left[:, :, 0:1].rearrange("p n o -> p (n o)"), axis=AX.X))
            chain(dve.reduce_max(lmax[:, 1:2], left[:, :, 1:2].rearrange("p n o -> p (n o)"), axis=AX.X))
            chain(dve.reduce_max(pf[:, 0:1], flat, axis=AX.X))
            chain(dve.tensor_tensor(pf[:, 1:2], pf[:, 0:1], lmax[:, 1:2], ALU.max))
            dve.tensor_tensor(lmax[:, 1:2], pf[:, 1:2], lmax[:, 0:1], ALU.max).then_inc(left_ready, 1)
            dve.wait_ge(all_ready, 2)
            chain(dve.tensor_scalar(pf[:, 0:2], lall[:], 0.0, None, ALU.is_gt))
            for q, (start, n_fit, n_all) in enumerate(((EC, KEPT // HB // 2, EC // HB // 2),
                                                        (EC + KEPT, LISTED // 8, EC // 8))):
                dve.tensor_scalar(plan[:, 2 * q:2 * q + 1], pf[:, q:q + 1], float(-start), float(start), ALU.mult, ALU.add).then_inc(done, 1)
                dve.tensor_scalar(plan[:, 2 * q + 1:2 * q + 2], pf[:, q:q + 1], float(n_all - n_fit), float(n_fit), ALU.mult, ALU.add).then_inc(done, 1)


def clamped_count_stage(nc, keys_dram, plan, clamped, ident):
    with ExitStack() as s:
        m = Memory(nc, s, "count")
        kb = m.sb("keys", [P, 2, HB])
        ki = m.sb("key_int", [P, HB], I32)
        dst = m.sb("dst", [P, HB], I32)
        far = m.sb("src_inner", [P, HB], I32)
        push = m.sb("push_out", [P, HB])
        hi_i = m.sb("hi_int", [P, HB], I32)
        lo_i = m.sb("lo_int", [P, HB], I32)
        hi = m.sb("hi", [P, HB], BF16)
        lo = m.sb("lo", [P, HB], BF16)
        iota_i = m.sb("iota_int", [P, 64], I32)
        iota = m.sb("iota", [P, 64, HB], BF16)
        oh = m.sb("one_hot", [P, 2, 64, HB], BF16)
        zero = m.sb("zeros", [P, 64], BF16)
        cs = m.sb("counts", [64, 64])
        c_ps = m.ps("counts_ps", [64, 64])
        o_ps = m.ps("clamped_ps", [P, NT])
        loaded = [m.sem("loaded0"), m.sem("loaded1")]
        iota_ready, step, split, hot, counted = m.sem("iota_ready"), m.sem("step"), m.sem("split"), m.sem("hot"), m.sem("counted")
        opened, closed, copied, spread = m.sem("opened"), m.sem("closed"), m.sem("copied"), m.sem("spread")
        block = s.enter_context(nc.Block())

        @block.sync
        def _(sp):
            start = sp.value_load(plan[0:1, 0:1], min_val=0, max_val=EC)
            turns = sp.value_load(plan[0:1, 1:2], min_val=KEPT // HB // 2, max_val=EC // HB // 2)
            with sp.Fori(0, turns) as i:
                for b in range(2):
                    sp.wait_ge(split, 2 * i + 1)
                    sp.dma_start(kb[:, b], keys_dram[:, bass.ds(start + (2 * i + b) * HB, HB)]).then_inc(loaded[b], 16)

        @block.gpsimd
        def _(pool):
            pool.iota(iota_i[:], pattern=[[1, 64]], base=0, channel_multiplier=0).then_inc(iota_ready, 1)

        @block.tensor
        def _(pe):
            turns = pe.value_load(plan[0:1, 1:2], min_val=KEPT // HB // 2, max_val=EC // HB // 2)
            pe.wait_ge(iota_ready, 4)
            nc.tensor.matmul(c_ps[:], zero[:], zero[:], start=True, stop=False, skip_group_check=True).then_inc(opened, 1)
            pe.wait_ge(opened, 2)
            with pe.Fori(0, turns) as i:
                for b in range(2):
                    n = 2 * i + b
                    pe.wait_ge(hot, 2 * n + 2 + 1)
                    for c in range(HB):
                        mm = nc.tensor.matmul(c_ps[:], oh[:, 0, :, c], oh[:, 1, :, c], start=False, stop=False,
                                              skip_group_check=True)
                    mm.then_inc(counted, 1)
            nc.tensor.matmul(c_ps[:], zero[:], zero[:], start=False, stop=True, skip_group_check=True).then_inc(closed, 1)
            pe.wait_ge(copied, 2)
            v = cs[:].rearrange("p (t o) -> p t o", o=2)
            for o in range(2):
                mm = nc.tensor.matmul(o_ps[64 * o:64 * o + 64], ident[0:64, 0:64], v[:, :, o], start=True, stop=True,
                                      skip_group_check=True)
            mm.then_inc(spread, 1)

        @block.vector
        def _(dve):
            turns = dve.value_load(plan[0:1, 1:2], min_val=KEPT // HB // 2, max_val=EC // HB // 2)
            dve.memset(zero[:], 0.0).then_inc(iota_ready, 1)
            dve.wait_ge(iota_ready, 3)
            dve.tensor_copy(iota[:], iota_i[:].rearrange("p (v o) -> p v o", o=1).to_broadcast([P, 64, HB])).then_inc(iota_ready, 1)
            dve.wait_ge(iota_ready, 4)
            with dve.Fori(0, turns) as i:
                for b in range(2):
                    n = 2 * i + b
                    at = [0]
                    STEPS = 7

                    def chain(ins):
                        at[0] += 1
                        ins.then_inc(step, 1)
                        dve.wait_ge(step, n * STEPS + at[0] + 1)

                    dve.wait_ge(loaded[b], 16 * i + 16 + 1)
                    dve.tensor_scalar(ki[:], kb[:, b], 1.0, None, ALU.subtract).then_inc(split, 1)
                    dve.wait_ge(split, n + 2)
                    dve.tensor_scalar(dst[:], ki[:], BITS, None, ALU.arith_shift_right).then_inc(step, 1)
                    dve.tensor_scalar(far[:], ki[:], 4095, None, ALU.bitwise_and).then_inc(step, 1)
                    at[0] += 2
                    dve.wait_ge(step, n * STEPS + at[0] + 1)
                    dve.tensor_scalar(push[:], far[:], 4095.0, 64.0, ALU.is_lt, ALU.mult).then_inc(step, 1)
                    dve.tensor_scalar(hi_i[:], dst[:], 6, None, ALU.arith_shift_right).then_inc(step, 1)
                    dve.tensor_scalar(lo_i[:], dst[:], 63, None, ALU.bitwise_and).then_inc(step, 1)
                    at[0] += 3
                    dve.wait_ge(step, n * STEPS + at[0] + 1)
                    dve.tensor_tensor(hi[:], hi_i[:], push[:], ALU.add).then_inc(step, 1)
                    dve.tensor_copy(lo[:], lo_i[:]).then_inc(step, 1)
                    at[0] += 2
                    dve.wait_ge(step, n * STEPS + at[0] + 1)
                    dve.wait_ge(counted, n + 1)
                    for q, v in enumerate((lo, hi)):
                        dve.tensor_tensor(oh[:, q], iota[:], v[:].rearrange("p (o c) -> p o c", o=1).to_broadcast([P, 64, HB]),
                                          ALU.is_equal).then_inc(hot, 1)
            dve.wait_ge(closed, 2)
            dve.tensor_copy(cs[:], c_ps[:]).then_inc(copied, 1)
            dve.wait_ge(spread, 2)
            dve.tensor_copy(clamped[:], o_ps[:]).then_inc(copied, 1)


H4 = 4
NE = 4
G20 = H4 + H4 * NE
BIG = 1e30


def node_features_stage(nc, a, xn, feat, adst, node_dram, ident):
    with ExitStack() as s:
        m = Memory(nc, s, "nodes")
        wg = m.sb("w_gat", [P, KC, 16])
        att = m.sb("att", [P, 2, 16])
        hc = m.sb("h_chunk", [16, 2, CH])
        prod = m.sb("products", [P, NT, 16])
        h_ps = m.ps("h_ps", [16, 2, CH])
        t_ps = m.ps("hT_ps", [P, NT, 16])
        loaded, h_ready, h_done, t_ready = m.sem("loaded"), m.sem("h_ready"), m.sem("h_done"), m.sem("t_ready")
        step, feat_ready, stored = m.sem("step"), m.sem("feat_ready"), m.sem("stored")
        block = s.enter_context(nc.Block())

        @block.sync
        def _(sp):
            sp.dma_start(wg[:], a["wgat"].rearrange("(k p) o -> p k o", p=P)).then_inc(loaded, 16)
            sp.dma_start(att[:, 0], a["att_src"].rearrange("(a n) -> a n", a=1).to_broadcast([P, 16])).then_inc(loaded, 16)
            sp.dma_start(att[:, 1], a["att_dst"].rearrange("(a n) -> a n", a=1).to_broadcast([P, 16])).then_inc(loaded, 16)
            sp.wait_ge(feat_ready, 2)
            sp.dma_start(node_dram.rearrange("(t p) f -> p t f", p=P), feat[:]).then_inc(stored, 16)
            sp.wait_ge(stored, 17)

        @block.tensor
        def _(pe):
            pe.wait_ge(loaded, 49)
            for n in range(NCH):
                b = n % 2
                if n >= 2:
                    pe.wait_ge(h_done, n - 1 + 1)
                for k in range(KC):
                    mm = nc.tensor.matmul(h_ps[:, b], wg[:, k], xn[:, k, n * CH:(n + 1) * CH], start=k == 0, stop=k == KC - 1)
                mm.then_inc(h_ready, 1)
                pe.wait_ge(h_done, n + 2)
                for j in range(4):
                    mm = nc.tensor.transpose(t_ps[:, 4 * n + j], hc[:, b, j * P:(j + 1) * P], ident[0:16, 0:16])
                mm.then_inc(t_ready, 1)

        @block.scalar
        def _(act):
            for n in range(NCH):
                act.wait_ge(h_ready, n + 2)
                if n >= 2:
                    act.wait_ge(t_ready, n - 1 + 1)
                nc.scalar.activation(hc[:, n % 2], h_ps[:, n % 2], ACT.Copy).then_inc(h_done, 1)

        @block.vector
        def _(dve):
            at = [0]

            def chain(ins):
                at[0] += 1
                ins.then_inc(step, 1)
                dve.wait_ge(step, at[0] + 1)

            dve.wait_ge(loaded, 49)
            dve.wait_ge(t_ready, NCH + 1)
            chain(dve.tensor_copy(feat[:, :, H4:G20], t_ps[:]))
            for q in range(2):
                chain(dve.tensor_tensor(prod[:], feat[:, :, H4:G20], att[:, q:q + 1].to_broadcast([P, NT, 16]), ALU.mult))
                dst = feat[:, :, 0:H4] if q == 0 else adst[:]
                chain(dve.reduce_sum(dst, prod[:].rearrange("p t (h e) -> p t h e", h=H4), axis=AX.X))
            dve.tensor_copy(prod[:, 0:1], prod[:, 1:2]).then_inc(feat_ready, 1)


def edge_max_stage(nc, passed, keys_dram, plan, feat, node_dram, shift, table, iota128, iota32, ident):
    with ExitStack() as s:
        m = Memory(nc, s, "emax")
        kb = m.sb("keys", [P, 2, 4])
        dec = EdgeNumbers(m)
        av = m.sb("gathered", [P, 2, 4, G20])
        x = m.sb("columns", [P, 2, 20])
        xT = m.sb("columnsT", [20, 2, P])
        dbc = m.sb("dst_rows", [P, 4, P])
        lower = m.sb("lower", [P, P])
        val = m.sb("masked", [P, H4, P])
        first = m.sb("earlier", [P, 4])
        junk = m.sb("junk", [P, P])
        lead = m.sb("leader", [P, 4])
        best = m.sb("best", [P, 4, H4])
        ohlo = m.sb("lo_rows", [P, 2, P])
        rhs = m.sb("hi_rows", [P, 2, NT, H4])
        fneg = m.sb("neg_feat", [P, H4])
        fall = m.sb("neg_all", [P, H4])
        x_ps = m.ps("columnsT_ps", [20, P])
        d_ps = m.ps("dst_rows_ps", [P, 4, P])
        a_ps = m.ps("a_rows_ps", [P, 2, H4, P])
        s_ps = m.ps("scatter_ps", [P, 2, CH])
        loaded = [m.sem("loaded0"), m.sem("loaded1")]
        gathered = [m.sem("gathered0", 0), m.sem("gathered1", 0)]
        shift_in, shift_out, ready = m.sem("shift_in"), m.sem("shift_out"), m.sem("ready")
        step, decoded, x_ready, xT_ready, xT_done = (m.sem(q) for q in ("step", "decoded", "x_ready", "xT_ready", "xT_done"))
        d_ready, d_done, a_ready, masked = (m.sem(q) for q in ("d_ready", "d_done", "a_ready", "masked"))
        rows_ready, scattered, merged = m.sem("rows_ready"), m.sem("scattered"), m.sem("merged")
        block = s.enter_context(nc.Block())
        MINT, MAXT = LISTED // 8, EC // 8

        @block.sync
        def _(sp):
            start = sp.value_load(plan[0:1, 2:3], min_val=0, max_val=EC + KEPT)
            turns = sp.value_load(plan[0:1, 3:4], min_val=MINT, max_val=MAXT)
            with sp.Fori(0, turns) as i:
                for b in range(2):
                    sp.wait_ge(decoded, 2 * i + 1)
                    sp.dma_start(kb[:, b], keys_dram[:, bass.ds(start + (2 * i + b) * 4, 4)]).then_inc(loaded[b], 16)

        @block.gpsimd
        def _(pool):
            turns = pool.value_load(plan[0:1, 3:4], min_val=MINT, max_val=MAXT)
            pool.memset(lower[:], 1.0).then_inc(ready, 1)
            pool.wait_ge(ready, 2)
            pool.affine_select(out=lower[:], in_=lower[:], compare_op=ALU.is_gt, fill=0.0, base=0,
                               pattern=[[-1, P]], channel_multiplier=1).then_inc(ready, 1)
            pool.wait_ge(ready, 3)
            pool.wait_ge(shift_in, 2)
            pool.partition_all_reduce(fall[:], fneg[:], P, RMAX).then_inc(shift_out, 1)
            with pool.Fori(0, turns) as i:
                for b in range(2):
                    n = 2 * i + b
                    pool.wait_ge(decoded, n + 2)
                    pool.wait_ge(x_ready, 2 * i + 1)
                    pool.sem_inc(passed, 1)
                    for c in range(4):
                        pool.indirect_dma_start(av[:, b, c], None, node_dram,
                                                bass.IndirectOffsetOnAxis(dec.src[:, b, c:c + 1], 0)).then_inc(gathered[b], 16)

        @block.tensor
        def _(pe):
            turns = pe.value_load(plan[0:1, 3:4], min_val=MINT, max_val=MAXT)
            with pe.Fori(0, turns) as i:
                for b in range(2):
                    n = 2 * i + b
                    pe.wait_ge(x_ready, n + 2)
                    pe.wait_ge(xT_done, n + 1)
                    nc.tensor.transpose(x_ps[:], x[:, b], ident[:]).then_inc(xT_ready, 1)
                    pe.wait_ge(xT_done, n + 2)
                    pe.wait_ge(d_done, n + 1)
                    for c in range(4):
                        mm = nc.tensor.matmul(d_ps[:, c], ident[0:20, c:c + 1].to_broadcast([20, P]), xT[:, b], start=True,
                                              stop=True, skip_group_check=True)
                    mm.then_inc(d_ready, 1)
                    for c in range(4):
                        pe.wait_ge(masked, 4 * n + max(c - 1, 0) + 1)
                        for h in range(H4):
                            q = 4 + 4 * c + h
                            mm = nc.tensor.matmul(a_ps[:, c % 2, h], ident[0:20, q:q + 1].to_broadcast([20, P]), xT[:, b],
                                                  start=True, stop=True, skip_group_check=True)
                        mm.then_inc(a_ready, 1)
                    for c in range(4):
                        pe.wait_ge(rows_ready, 4 * n + c + 2)
                        pe.wait_ge(merged, 4 * n + max(c - 1, 0) + 1)
                        nc.tensor.matmul(s_ps[:, c % 2, 0:NT * H4], ohlo[:, c % 2], rhs[:, c % 2].rearrange("p t h -> p (t h)"),
                                         start=True, stop=True, skip_group_check=True).then_inc(scattered, 1)

        @block.scalar
        def _(act):
            turns = act.value_load(plan[0:1, 3:4], min_val=MINT, max_val=MAXT)
            with act.Fori(0, turns) as i:
                for b in range(2):
                    n = 2 * i + b
                    act.wait_ge(xT_ready, n + 2)
                    act.wait_ge(a_ready, 8 * i + 1)
                    nc.scalar.activation(xT[:, b], x_ps[:], ACT.Copy).then_inc(xT_done, 1)
                    act.wait_ge(d_ready, n + 2)
                    act.wait_ge(masked, 4 * n + 1)
                    nc.scalar.activation(dbc[:], d_ps[:], ACT.Copy).then_inc(d_done, 1)

        def merge(dve, n, c):
            dve.wait_ge(scattered, 4 * n + c + 2)
            dve.wait_ge(merged, 4 * n + c + 1)
            dve.tensor_tensor(table[:].rearrange("p t h -> p (t h)"), table[:].rearrange("p t h -> p (t h)"),
                              s_ps[:, c % 2, 0:NT * H4], ALU.max).then_inc(merged, 1)

        @block.vector
        def _(dve):
            turns = dve.value_load(plan[0:1, 3:4], min_val=MINT, max_val=MAXT)
            at = [0]

            def chain(ins, base=0):
                at[0] += 1
                ins.then_inc(step, 1)
                dve.wait_ge(step, base + at[0] + 1)

            chain(dve.memset(table[:], 0.0))
            chain(dve.tensor_reduce(fneg[:], feat[:, :, 0:H4].rearrange("p t h -> p h t"), AX.X, ALU.min))
            dve.tensor_scalar(fneg[:], fneg[:], -1.0, None, ALU.mult).then_inc(shift_in, 1)
            dve.wait_ge(shift_out, 2)
            chain(dve.tensor_scalar(shift[:], fall[:], 1.0, None, ALU.add))
            dve.wait_ge(ready, 3)
            first_steps = at[0]
            STEPS = EdgeNumbers.STEPS + 2 + 4 * 2 + 4
            with dve.Fori(0, turns) as i:
                for b in range(2):
                    n = 2 * i + b
                    at[0] = 0
                    base = n * STEPS + first_steps
                    dve.wait_ge(loaded[b], 16 * i + 16 + 1)
                    dec.decode(dve, b, kb[:, b], step, base)
                    at[0] = EdgeNumbers.STEPS
                    dve.wait_ge(xT_ready, 2 * i + 1)
                    dve.tensor_copy(x[:, b, 0:4], dec.dst[:, b]).then_inc(decoded, 1)
                    dve.wait_ge(gathered[b], 64 * i + 64)
                    dve.tensor_tensor(x[:, b, 4:20].rearrange("p (c h) -> p c h", c=4), av[:, b, :, 0:H4],
                                      shift[:].rearrange("p (o h) -> p o h", o=1).to_broadcast([P, 4, H4]), ALU.add)\
                        .then_inc(x_ready, 1)
                    dve.wait_ge(d_done, n + 2)
                    for c in range(4):
                        d = dec.dst[:, b, c:c + 1]
                        dve.wait_ge(a_ready, 4 * n + c + 2)
                        dve.scalar_tensor_tensor(junk[:], dbc[:, c], d, lower[:], ALU.is_equal, ALU.mult,
                                                 accum_out=first[:, c:c + 1]).then_inc(step, 1)
                        at[0] += 1
                        dve.scalar_tensor_tensor(val[:], dbc[:, c:c + 1].to_broadcast([P, H4, P]), d, a_ps[:, c % 2],
                                                 ALU.is_equal, ALU.mult).then_inc(masked, 1)
                        dve.wait_ge(masked, 4 * n + c + 2)
                        chain(dve.reduce_max(best[:, c], val[:], axis=AX.X), base)
                    chain(dve.tensor_scalar(lead[:], first[:], 0.0, None, ALU.is_equal), base)
                    for c in range(4):
                        dve.wait_ge(scattered, 4 * n + max(c - 1, 0) + 1)
                        dve.tensor_scalar(ohlo[:, c % 2], iota128[:], dec.lo[:, b, c:c + 1], lead[:, c:c + 1],
                                          ALU.is_equal, ALU.mult).then_inc(step, 1)
                        at[0] += 1
                        dve.wait_ge(step, base + at[0] + 1)
                        dve.scalar_tensor_tensor(rhs[:, c % 2], iota32[:].rearrange("p (t o) -> p t o", o=1).to_broadcast([P, NT, H4]),
                                                 dec.hi[:, b, c:c + 1],
                                                 best[:, c:c + 1].to_broadcast([P, NT, H4]), ALU.is_equal, ALU.mult)\
                            .then_inc(rows_ready, 1)
                        if c:
                            merge(dve, n, c - 1)
                    merge(dve, n, 3)
                    chain(dve.tensor_copy(junk[:, 0:1], junk[:, 1:2]), base)
                    assert at[0] == STEPS, (at[0], STEPS)


class EdgeNumbers:
    STEPS = 10

    def __init__(self, m):
        self.ki = m.sb("key_int", [P, 4], I32)
        self.di = m.sb("dst_int", [P, 4], I32)
        self.out = m.sb("not_listed", [P, 4])
        self.li = m.sb("lo_int", [P, 4], I32)
        self.hi_i = m.sb("hi_int", [P, 4], I32)
        self.dg = m.sb("dst_row", [P, 2, 4], I32)
        self.src = m.sb("src", [P, 2, 4], I32)
        self.dst = m.sb("dst", [P, 2, 4])
        self.lo = m.sb("lo", [P, 2, 4])
        self.hi = m.sb("hi", [P, 2, 4])

    def decode(self, dve, b, keys, step, base):
        k = 0

        def then(ins):
            nonlocal k
            k += 1
            ins.then_inc(step, 1)

        def fence():
            dve.wait_ge(step, base + k + 1)

        fence()
        then(dve.tensor_scalar(self.ki[:], keys, 1.0, None, ALU.subtract))
        fence()
        then(dve.tensor_scalar(self.di[:], self.ki[:], BITS, None, ALU.arith_shift_right))
        then(dve.tensor_scalar(self.src[:, b], self.ki[:], 4095, None, ALU.bitwise_and))
        fence()
        then(dve.tensor_scalar(self.out[:], self.src[:, b], 4095.0, -8192.0, ALU.is_equal, ALU.mult))
        then(dve.tensor_scalar(self.li[:], self.di[:], 127, None, ALU.bitwise_and))
        fence()
        then(dve.tensor_tensor(self.dst[:, b], self.di[:], self.out[:], ALU.add))
        then(dve.tensor_copy(self.lo[:, b], self.li[:]))
        fence()
        then(dve.tensor_tensor(self.hi[:, b], self.dst[:, b], self.lo[:, b], ALU.subtract))
        fence()
        then(dve.tensor_scalar(self.hi[:, b], self.hi[:, b], 1.0 / P, None, ALU.mult))
        fence()
        assert k == self.STEPS - 1
        then(dve.tensor_scalar(self.dg[:, b], self.dst[:, b], 0.0, None, ALU.max))
        fence()


def node_max_stage(nc, feat, adst, shift, table, clamped, last, mx, max_dram, ident):
    with ExitStack() as s:
        m = Memory(nc, s, "nmax")
        l_ps = m.ps("last_ps", [P, G20])
        top = m.sb("top", [P, NT, H4])
        alt = m.sb("alt", [P, NT, H4])
        lsh = m.sb("last_shifted", [P, H4])
        has = m.sb("has_clamped", [P, NT])
        last_ready, step, mx_ready, stored = m.sem("last_ready"), m.sem("step"), m.sem("mx_ready"), m.sem("stored")
        block = s.enter_context(nc.Block())

        @block.tensor
        def _(pe):
            nc.tensor.matmul(l_ps[:], ident[:, P - 1:P].to_broadcast([P, P]), feat[:, NT - 1], start=True, stop=True)\
                .then_inc(last_ready, 1)

        @block.sync
        def _(sp):
            sp.wait_ge(mx_ready, 2)
            sp.dma_start(max_dram.rearrange("(t p) f -> p t f", p=P), mx[:]).then_inc(stored, 16)
            sp.wait_ge(stored, 17)

        @block.vector
        def _(dve):
            at = [0]

            def chain(ins):
                at[0] += 1
                ins.then_inc(step, 1)
                dve.wait_ge(step, at[0] + 1)

            sh = shift[:].rearrange("p (o h) -> p o h", o=1).to_broadcast([P, NT, H4])
            chain(dve.tensor_tensor(top[:], feat[:, :, 0:H4], sh, ALU.add))
            chain(dve.tensor_tensor(top[:], top[:], table[:], ALU.max))
            dve.wait_ge(last_ready, 2)
            chain(dve.tensor_copy(last[:], l_ps[:]))
            chain(dve.tensor_tensor(lsh[:], last[:, 0:H4], shift[:], ALU.add))
            chain(dve.tensor_scalar(has[:], clamped[:], 0.0, None, ALU.is_gt))
            chain(dve.tensor_tensor(alt[:], has[:].rearrange("p (t o) -> p t o", o=1).to_broadcast([P, NT, H4]),
                                    lsh[:].rearrange("p (o h) -> p o h", o=1).to_broadcast([P, NT, H4]), ALU.mult))
            chain(dve.tensor_tensor(top[:], top[:], alt[:], ALU.max))
            chain(dve.tensor_tensor(top[:], top[:], sh, ALU.subtract))
            chain(dve.tensor_tensor(top[:], top[:], adst[:], ALU.add))
            chain(dve.tensor_scalar(alt[:], top[:], 0.2, None, ALU.mult))
            chain(dve.tensor_copy(mx[:, :, 0:H4], adst[:]))
            dve.tensor_tensor(mx[:, :, H4:2 * H4], top[:], alt[:], ALU.max).then_inc(mx_ready, 1)


def edge_sum_stage(nc, passed, keys_dram, plan, node_dram, max_dram, sums, iota128, iota32):
    W5 = 1 + NE
    with ExitStack() as s:
        m = Memory(nc, s, "esum")
        kb = m.sb("keys", [P, 2, 4])
        dec = EdgeNumbers(m)
        av = m.sb("src_rows", [P, 2, 4, G20])
        dv = m.sb("dst_rows", [P, 2, 4, 2 * H4])
        z = m.sb("z", [P, 4, H4])
        z2 = m.sb("z2", [P, 4, H4])
        ee = m.sb("exp", [P, 2, 4, H4])
        msg = m.sb("messages", [P, 2, 4, H4, W5])
        ohlo = m.sb("lo_rows", [P, 2, P])
        rhs = m.sb("hi_rows", [P, 2, NT, H4 * W5])
        zero = m.sb("zeros", [P, NT // 2 * H4 * W5])
        junk = m.sb("junk", [P, 1])
        s_ps = m.ps("sums_ps", [P, 2, CH])
        HALF = NT // 2 * H4 * W5
        loaded = [m.sem("loaded0"), m.sem("loaded1")]
        gathered = [m.sem("gathered0", 0), m.sem("gathered1", 0)]
        step, decoded, x_ready, e_ready, msg_ready = (m.sem(q) for q in ("step", "decoded", "x_ready", "e_ready", "msg_ready"))
        rows_ready, summed, ready, opened, closed = (m.sem(q) for q in ("rows_ready", "summed", "ready", "opened", "closed"))
        block = s.enter_context(nc.Block())
        MINT, MAXT = LISTED // 8, EC // 8

        @block.sync
        def _(sp):
            start = sp.value_load(plan[0:1, 2:3], min_val=0, max_val=EC + KEPT)
            turns = sp.value_load(plan[0:1, 3:4], min_val=MINT, max_val=MAXT)
            with sp.Fori(0, turns) as i:
                for b in range(2):
                    sp.wait_ge(decoded, 2 * i + 1)
                    sp.dma_start(kb[:, b], keys_dram[:, bass.ds(start + (2 * i + b) * 4, 4)]).then_inc(loaded[b], 16)

        @block.gpsimd
        def _(pool):
            turns = pool.value_load(plan[0:1, 3:4], min_val=MINT, max_val=MAXT)
            with pool.Fori(0, turns) as i:
                for b in range(2):
                    n = 2 * i + b
                    pool.wait_ge(decoded, n + 2)
                    pool.wait_ge(msg_ready, 2 * i + 1)
                    pool.sem_inc(passed, 1)
                    for c in range(4):
                        pool.indirect_dma_start(av[:, b, c], None, node_dram,
                                                bass.IndirectOffsetOnAxis(dec.src[:, b, c:c + 1], 0)).then_inc(gathered[b], 16)
                        pool.indirect_dma_start(dv[:, b, c], None, max_dram,
                                                bass.IndirectOffsetOnAxis(dec.dg[:, b, c:c + 1], 0)).then_inc(gathered[b], 16)

        @block.tensor
        def _(pe):
            turns = pe.value_load(plan[0:1, 3:4], min_val=MINT, max_val=MAXT)
            pe.wait_ge(ready, 2)
            for h in range(2):
                mm = nc.tensor.matmul(s_ps[:, h, 0:HALF], zero[:, 0:P], zero[:], start=True, stop=False, skip_group_check=True)
            mm.then_inc(opened, 1)
            pe.wait_ge(opened, 2)
            with pe.Fori(0, turns) as i:
                for b in range(2):
                    n = 2 * i + b
                    for c in range(4):
                        pe.wait_ge(rows_ready, 4 * n + c + 2)
                        for h in range(2):
                            mm = nc.tensor.matmul(s_ps[:, h, 0:HALF], ohlo[:, c % 2],
                                                  rhs[:, c % 2, h * NT // 2:(h + 1) * NT // 2].rearrange("p t f -> p (t f)"),
                                                  start=False, stop=False, skip_group_check=True)
                        mm.then_inc(summed, 1)
            for h in range(2):
                mm = nc.tensor.matmul(s_ps[:, h, 0:HALF], zero[:, 0:P], zero[:], start=False, stop=True, skip_group_check=True)
            mm.then_inc(closed, 1)

        @block.scalar
        def _(act):
            turns = act.value_load(plan[0:1, 3:4], min_val=MINT, max_val=MAXT)
            with act.Fori(0, turns) as i:
                for b in range(2):
                    n = 2 * i + b
                    act.wait_ge(x_ready, n + 2)
                    act.wait_ge(msg_ready, 2 * i + 1)
                    nc.scalar.activation(ee[:, b], z[:], ACT.Exp).then_inc(e_ready, 1)

        @block.vector
        def _(dve):
            turns = dve.value_load(plan[0:1, 3:4], min_val=MINT, max_val=MAXT)
            dve.memset(zero[:], 0.0).then_inc(ready, 1)
            STEPS = EdgeNumbers.STEPS + 4 + 1 + 4
            with dve.Fori(0, turns) as i:
                for b in range(2):
                    n = 2 * i + b
                    at = [EdgeNumbers.STEPS]
                    base = n * STEPS

                    def chain(ins):
                        at[0] += 1
                        ins.then_inc(step, 1)
                        dve.wait_ge(step, base + at[0] + 1)

                    dve.wait_ge(loaded[b], 16 * i + 16 + 1)
                    dve.wait_ge(summed, 4 * n + 1)
                    dec.decode(dve, b, kb[:, b], step, base)
                    dve.memset(junk[:], 0.0).then_inc(decoded, 1)
                    dve.wait_ge(gathered[b], 128 * i + 128)
                    dve.wait_ge(e_ready, n + 1)
                    chain(dve.tensor_tensor(z[:], av[:, b, :, 0:H4], dv[:, b, :, 0:H4], ALU.add))
                    chain(dve.tensor_scalar(z2[:], z[:], 0.2, None, ALU.mult))
                    chain(dve.tensor_tensor(z[:], z[:], z2[:], ALU.max))
                    chain(dve.tensor_tensor(z[:], z[:], dv[:, b, :, H4:2 * H4], ALU.subtract))
                    dve.tensor_scalar(z[:], z[:], 0.0, None, ALU.min).then_inc(x_ready, 1)
                    dve.wait_ge(e_ready, n + 2)
                    chain(dve.tensor_copy(msg[:, b, :, :, 0:1].rearrange("p c h o -> p c (h o)"), ee[:, b]))
                    ins = dve.tensor_tensor(msg[:, b, :, :, 1:W5].rearrange("p c h e -> p (c h) e"),
                                            av[:, b, :, H4:G20].rearrange("p c (h e) -> p c h e", h=H4),
                                            ee[:, b].rearrange("p c (h o) -> p c h o", o=1).to_broadcast([P, 4, H4, NE]), ALU.mult)\
                        if False else dve.tensor_tensor(
                            msg[:, b, :, :, 1:W5], av[:, b, :, H4:G20].rearrange("p c (h e) -> p c h e", h=H4),
                            ee[:, b].rearrange("p c (h o) -> p c h o", o=1).to_broadcast([P, 4, H4, NE]), ALU.mult)
                    ins.then_inc(msg_ready, 1)
                    dve.wait_ge(msg_ready, n + 2)
                    for c in range(4):
                        dve.wait_ge(summed, 4 * n + max(c - 1, 0) + 1)
                        chain(dve.tensor_scalar(ohlo[:, c % 2], iota128[:], dec.lo[:, b, c:c + 1], None, ALU.is_equal))
                        dve.scalar_tensor_tensor(
                            rhs[:, c % 2], iota32[:].rearrange("p (t o) -> p t o", o=1).to_broadcast([P, NT, H4 * W5]),
                            dec.hi[:, b, c:c + 1],
                            msg[:, b, c:c + 1].rearrange("p o h f -> p o (h f)").to_broadcast([P, NT, H4 * W5]),
                            ALU.is_equal, ALU.mult).then_inc(rows_ready, 1)
                    assert at[0] == STEPS, (at[0], STEPS)
            dve.wait_ge(closed, 2)
            for h in range(2):
                ins = dve.tensor_copy(sums[:, h * NT // 2:(h + 1) * NT // 2].rearrange("p t h f -> p (t h f)"), s_ps[:, h, 0:HALF])
            ins.then_inc(step, 1)


def gate_stage(nc, a, feat, mx, clamped, last, sums, gates, gT, ident):
    W5 = 1 + NE
    with ExitStack() as s:
        m = Memory(nc, s, "gates")
        par = m.sb("params", [P, 3, 16])
        z = m.sb("z", [P, 2, NT, H4])
        z2 = m.sb("z2", [P, 2, NT, H4])
        ee = m.sb("exp", [P, 2, NT, H4])
        tmp = m.sb("tmp", [P, NT, H4, NE])
        agg = m.sb("agg", [P, NT, H4, NE])
        one = m.sb("per_node", [P, 6, NT])
        eps = m.sb("eps", [P, 1])
        sc = m.sb("scores", [P, NT, NE])
        rank = m.sb("rank", [P, NE, NT])
        beat = m.sb("beats", [P, NT])
        t_ps = m.ps("gT_ps", [NE, 2, 4, P])
        loaded, step, z_ready, e_ready = m.sem("loaded"), m.sem("step"), m.sem("z_ready"), m.sem("e_ready")
        var_ready, sd_ready, sc_ready, sm_ready = (m.sem(q) for q in ("var_ready", "sd_ready", "sc_ready", "sm_ready"))
        gates_ready, t_ready, t_done = m.sem("gates_ready"), m.sem("t_ready"), m.sem("t_done")
        block = s.enter_context(nc.Block())

        @block.sync
        def _(sp):
            for q, name in enumerate(("b_gat", "ln_gamma", "ln_beta")):
                sp.dma_start(par[:, q], a[name].rearrange("(a n) -> a n", a=1).to_broadcast([P, 16])).then_inc(loaded, 16)

        @block.scalar
        def _(act):
            act.wait_ge(z_ready, 2)
            nc.scalar.activation(ee[:], z[:], ACT.Exp).then_inc(e_ready, 1)
            act.wait_ge(var_ready, 2)
            nc.scalar.activation(one[:, 2], one[:, 1], ACT.Sqrt, bias=eps[:], scale=1.0 / 16).then_inc(sd_ready, 1)
            act.wait_ge(sc_ready, 2)
            nc.scalar.activation(sc[:], sc[:], ACT.Exp).then_inc(sm_ready, 1)

        @block.tensor
        def _(pe):
            pe.wait_ge(gates_ready, 2)
            for n in range(NCH):
                if n >= 2:
                    pe.wait_ge(t_done, n - 1 + 1)
                for j in range(4):
                    mm = nc.tensor.transpose(t_ps[:, n % 2, j], gates[:, 4 * n + j], ident[:])
                mm.then_inc(t_ready, 1)

        @block.vector
        def _(dve):
            at = [0]

            def chain(ins):
                at[0] += 1
                ins.then_inc(step, 1)
                dve.wait_ge(step, at[0] + 1)

            def wide(v, *shape):
                return v.rearrange("p (t o) -> p t o", o=1).to_broadcast([P, NT, *shape])

            chain(dve.memset(eps[:], 1e-5))
            chain(dve.tensor_tensor(z[:, 0], feat[:, :, 0:H4], mx[:, :, 0:H4], ALU.add))
            chain(dve.tensor_tensor(z[:, 1], last[:, 0:H4].rearrange("p (o h) -> p o h", o=1).to_broadcast([P, NT, H4]),
                                    mx[:, :, 0:H4], ALU.add))
            chain(dve.tensor_scalar(z2[:], z[:], 0.2, None, ALU.mult))
            chain(dve.tensor_tensor(z[:], z[:], z2[:], ALU.max))
            for q in range(2):
                chain(dve.tensor_tensor(z[:, q], z[:, q], mx[:, :, H4:2 * H4], ALU.subtract))
            dve.tensor_scalar(z[:], z[:], 0.0, None, ALU.min).then_inc(z_ready, 1)
            dve.wait_ge(e_ready, 2)
            chain(dve.tensor_tensor(ee[:, 1], ee[:, 1], wide(clamped[:], H4), ALU.mult))
            for q, h in enumerate((feat[:, :, H4:G20].rearrange("p t (h e) -> p t h e", h=H4),
                                   last[:, H4:G20].rearrange("p (o h e) -> p o h e", o=1, h=H4).to_broadcast([P, NT, H4, NE]))):
                chain(dve.tensor_tensor(tmp[:], h, ee[:, q].rearrange("p t (h o) -> p t h o", o=1).to_broadcast([P, NT, H4, NE]), ALU.mult))
                chain(dve.tensor_tensor(agg[:], tmp[:], sums[:, :, :, 1:W5] if q == 0 else agg[:], ALU.add))
            den = sums[:, :, :, 0:1].rearrange("p t h o -> p t (h o)")
            chain(dve.tensor_tensor(z[:, 0], ee[:, 0], den, ALU.add))
            chain(dve.tensor_tensor(z[:, 0], z[:, 0], ee[:, 1], ALU.add))
            chain(dve.tensor_scalar(z[:, 0], z[:, 0], 1e-16, None, ALU.add))
            chain(dve.reciprocal(z[:, 1], z[:, 0]))
            chain(dve.tensor_tensor(agg[:], agg[:], z[:, 1].rearrange("p t (h o) -> p t h o", o=1).to_broadcast([P, NT, H4, NE]), ALU.mult))
            a16 = agg[:].rearrange("p t h e -> p t (h e)")
            t16 = tmp[:].rearrange("p t h e -> p t (h e)")
            dve.wait_ge(loaded, 49)
            chain(dve.tensor_tensor(a16, a16, par[:, 0:1].to_broadcast([P, NT, 16]), ALU.add))
            chain(dve.reduce_sum(one[:, 0], a16, axis=AX.X))
            chain(dve.tensor_scalar(one[:, 0], one[:, 0], 1.0 / 16, None, ALU.mult))
            chain(dve.tensor_tensor(a16, a16, wide(one[:, 0], 16), ALU.subtract))
            chain(dve.tensor_tensor(t16, a16, a16, ALU.mult))
            dve.reduce_sum(one[:, 1], t16, axis=AX.X).then_inc(var_ready, 1)
            dve.wait_ge(sd_ready, 2)
            chain(dve.reciprocal(one[:, 3], one[:, 2]))
            chain(dve.tensor_tensor(a16, a16, wide(one[:, 3], 16), ALU.mult))
            chain(dve.tensor_tensor(a16, a16, par[:, 1:2].to_broadcast([P, NT, 16]), ALU.mult))
            chain(dve.tensor_tensor(a16, a16, par[:, 2:3].to_broadcast([P, NT, 16]), ALU.add))
            chain(dve.reduce_sum(sc[:], agg[:].rearrange("p t h e -> p t e h"), axis=AX.X))
            chain(dve.tensor_scalar(sc[:], sc[:], 1.0 / H4, None, ALU.mult))
            chain(dve.memset(rank[:], 0.0))
            for i in range(NE):
                for j in range(i + 1, NE):
                    chain(dve.tensor_tensor(beat[:], sc[:, :, i], sc[:, :, j], ALU.is_ge))
                    chain(dve.tensor_tensor(rank[:, j], rank[:, j], beat[:], ALU.add))
                    chain(dve.tensor_scalar(beat[:], beat[:], -1.0, 1.0, ALU.mult, ALU.add))
                    chain(dve.tensor_tensor(rank[:, i], rank[:, i], beat[:], ALU.add))
            chain(dve.tensor_scalar(rank[:], rank[:], 2.0, None, ALU.is_lt))
            chain(dve.reduce_max(one[:, 4], sc[:], axis=AX.X))
            dve.tensor_tensor(sc[:], sc[:], wide(one[:, 4], NE), ALU.subtract).then_inc(sc_ready, 1)
            dve.wait_ge(sm_ready, 2)
            chain(dve.tensor_tensor(sc[:], sc[:], rank[:].rearrange("p e t -> p t e"), ALU.mult))
            chain(dve.reduce_sum(one[:, 5], sc[:], axis=AX.X))
            chain(dve.reciprocal(one[:, 0], one[:, 5]))
            dve.tensor_tensor(gates[:], sc[:], wide(one[:, 0], NE), ALU.mult).then_inc(gates_ready, 1)
            for n in range(NCH):
                dve.wait_ge(t_ready, n + 2)
                dve.tensor_copy(gT[:, n * CH:(n + 1) * CH], t_ps[:, n % 2].rearrange("p j c -> p (j c)")).then_inc(t_done, 1)


def gated_expert_stage(nc, passed, a, xn, gT, res, out, ident):
    F = 512
    KF = F // P
    with ExitStack() as s:
        m = Memory(nc, s, "moe")
        w1 = m.sb("w1_sb", [P, NE, KC, F])
        w2 = m.sb("w2_sb", [P, NE, KF, C])
        b1 = m.sb("b1_sb", [P, NE, KF])
        b2 = m.sb("b2_sb", [NE, C])
        hid = m.sb("hidden", [P, 2, CH])
        gh = m.sb("gated_hidden", [P, 4, CH])
        gb = m.sb("gate_rows", [P, 2, CH])
        h_ps = m.ps("hidden_ps", [P, 2, CH])
        g_ps = m.ps("gate_ps", [P, CH])
        y_ps = m.ps("y_ps", [P, 2, KC, CH])
        loaded, g_ready, g_done = m.sem("loaded"), m.sem("g_ready"), m.sem("g_done")
        h_ready, h_done, gated, y_ready = m.sem("h_ready"), m.sem("h_done"), m.sem("gated"), m.sem("y_ready")
        added, stored = m.sem("added"), m.sem("stored")
        o_v = out.rearrange("(k p) n -> p k n", p=P)
        block = s.enter_context(nc.Block())
        Q = NE * KF

        @block.sync
        def _(sp):
            sp.dma_start(w1[:], a["ew1"].rearrange("e (k p) f -> p e k f", p=P)).then_inc(loaded, 16)
            sp.dma_start(w2[:], a["ew2"].rearrange("e (k p) d -> p e k d", p=P)).then_inc(loaded, 16)
            sp.dma_start(b1[:].rearrange("p e k -> p (e k)"), a["eb1"]).then_inc(loaded, 16)
            sp.dma_start(b2[:], a["eb2"]).then_inc(loaded, 16)
            with sp.Fori(0, NCH) as n:
                sp.wait_ge(added, n + 2)
                sp.dma_start(o_v[:, :, bass.ds(n * CH, CH)], res[:, :, bass.ds(n * CH, CH)]).then_inc(stored, 16)
            sp.wait_ge(stored, 16 * NCH + 1)

        @block.tensor
        def _(pe):
            pe.wait_ge(loaded, 65)
            with pe.Fori(0, NCH // 2) as i:
                for b in range(2):
                    n = 2 * i + b
                    cols = bass.ds(n * CH, CH)

                    def out_tile(q):
                        pe.wait_ge(gated, Q * n + q + 2)
                        for o in range(KC):
                            mm = nc.tensor.matmul(y_ps[:, b, o], w2[:, q // KF, q % KF, o * P:(o + 1) * P], gh[:, q % 4],
                                                  start=False, stop=q == Q - 1)
                        mm.then_inc(y_ready, 1)

                    for q in range(Q):
                        e = q // KF
                        if q % KF == 0:
                            pe.wait_ge(g_done, NE * n + e + 1)
                            pe.sem_inc(passed, 1)
                            nc.tensor.matmul(g_ps[:], ident[0:NE, e:e + 1].to_broadcast([NE, P]), gT[:, cols],
                                             start=True, stop=True).then_inc(g_ready, 1)
                        pe.wait_ge(h_done, Q * n + max(q - 1, 0) + 1)
                        for k in range(KC):
                            mm = nc.tensor.matmul(h_ps[:, q % 2], w1[:, e, k, (q % KF) * P:(q % KF + 1) * P],
                                                  xn[:, k, cols], start=k == 0, stop=k == KC - 1)
                        mm.then_inc(h_ready, 1)
                        if q == 2:
                            pe.wait_ge(added, 2 * i + 1)
                            pe.sem_inc(passed, 1)
                            for o in range(KC):
                                nc.tensor.matmul(y_ps[:, b, o], b2[:, o * P:(o + 1) * P], gT[:, cols], start=True, stop=False)
                        if q >= 2:
                            out_tile(q - 2)
                    out_tile(Q - 2)
                    out_tile(Q - 1)

        @block.scalar
        def _(act):
            act.wait_ge(loaded, 65)
            with act.Fori(0, NCH) as n:
                for q in range(Q):
                    if q % KF == 0:
                        e = q // KF
                        act.wait_ge(g_ready, NE * n + e + 2)
                        act.wait_ge(gated, Q * n + max(q - KF, 0) + 1)
                        nc.scalar.activation(gb[:, e % 2], g_ps[:], ACT.Copy).then_inc(g_done, 1)
                    act.wait_ge(h_ready, Q * n + q + 2)
                    act.wait_ge(gated, Q * n + max(q - 1, 0) + 1)
                    nc.scalar.activation(hid[:, q % 2], h_ps[:, q % 2], ACT.Gelu,
                                         bias=b1[:, q // KF, q % KF:q % KF + 1]).then_inc(h_done, 1)

        @block.vector
        def _(dve):
            with dve.Fori(0, NCH // 2) as i:
                for b in range(2):
                    n = 2 * i + b
                    for q in range(Q):
                        e = q // KF
                        dve.wait_ge(g_done, NE * n + e + 2)
                        dve.wait_ge(h_done, Q * n + q + 2)
                        dve.wait_ge(y_ready, Q * n + max(q - 3, 0) + 1)
                        dve.tensor_tensor(gh[:, q % 4], hid[:, q % 2], gb[:, e % 2], ALU.mult).then_inc(gated, 1)
                    dve.wait_ge(y_ready, Q * n + Q + 1)
                    c = res[:, :, bass.ds(n * CH, CH)]
                    dve.tensor_tensor(c, c, y_ps[:, b], ALU.add).then_inc(added, 1)


def program(nc, a, out, stop=None):
    with ExitStack() as s:
        m = Memory(nc, s, "program")
        passed = nc.alloc_semaphore(name="passed")
        Memory.spent = []
        ones_mean = m.sb("ones_mean", [P, P])
        block_ones = m.sb("block_ones", [P, P])
        ident = m.sb("ident", [P, P])
        stack_ident = m.sb("stack_ident", [P, DH])
        den_pick = m.sb("den_pick", [P, 1])
        col_sum = m.sb("col_sum", [P, KC])
        top_w = m.sb("top_w", [P, 2])
        top_i = m.sb("top_i", [1, 8], mybir.dt.uint32)
        qk_dram = nc.dram_tensor("qk_scratch", [4, 2, P, N], F16, kind="Internal").ap()
        v_dram = nc.dram_tensor("v_scratch", [HEADS, P, NT * DH], F32, kind="Internal").ap()
        iota128 = m.sb("iota128", [P, P])
        iota32 = m.sb("iota32", [P, NT])
        plan = m.sb("plan", [P, 4], I32)
        clamped = m.sb("clamped", [P, NT])
        keys_dram = nc.dram_tensor("keys_scratch", [P, 2 * EC + KEPT], F32, kind="Internal").ap()
        node_dram = nc.dram_tensor("node_scratch", [N, G20], F32, kind="Internal").ap()
        max_dram = nc.dram_tensor("max_scratch", [N, 2 * H4], F32, kind="Internal").ap()
        fill_constants(nc, ones_mean, block_ones, ident, stack_ident, den_pick)
        iotas(nc, iota128, iota32)
        edge_keys_stage(nc, passed, a["edges"], keys_dram, plan)
        clamped_count_stage(nc, keys_dram, plan, clamped, ident)
        if stop != "skip":
            qkv_stage(nc, a["x"], a["wqkvT"], a["temp"], qk_dram, v_dram, ones_mean, block_ones)
        res = m.sb("residual", [P, KC, N])
        with nc.sbuf_tensor("attn", [P, KC, 16, C], F32) as attn:
            if stop != "skip":
                attention_stage(nc, passed, a["temp"], qk_dram, v_dram, attn, stack_ident, den_pick, ident)
            else:
                load(nc, attn, a["attn"])
            projection_stage(nc, a["x"], a["wprojT"], attn, res)
        with nc.sbuf_tensor("normed", [P, KC, N], F32) as xn:
            layer_norm_stage(nc, "ln_ffn", res, xn, 1e-5, ones_mean, col_sum)
            routing_stage(nc, a, col_sum, top_w, top_i)
            with nc.sbuf_tensor("expert_sum", [P, KC, N], F32) as z:
                expert_stage(nc, a, xn, top_w, top_i, z)
                layer_norm_stage(nc, "ln_out", z, z, 1e-5, ones_mean)
                affine_residual_stage(nc, a, z, res)
        with nc.sbuf_tensor("h_padded", [P, PW * PW], F32) as hpad, \
                nc.sbuf_tensor("h_transposed", [P, NT + 2, P], F32) as hT, \
                nc.sbuf_tensor("gate", [P, N], F32) as gate:
            with nc.sbuf_tensor("conv_normed", [P, KC, N], F32) as cn:
                layer_norm_stage(nc, "ln_conv", res, cn, 1e-6, ones_mean)
                conv_in_stage(nc, a, cn, hpad, hT, gate, ident)
            conv_out_stage(nc, a, hpad, hT, gate, res, ident)
        Memory.clear_semaphores(nc)
        with nc.sbuf_tensor("graph_normed", [P, KC, N], F32) as xn, ExitStack() as gs:
            g = Memory(nc, gs, "graph")
            layer_norm_stage(nc, "ln_graph", res, xn, 1e-5, ones_mean)
            feat = g.sb("feat", [P, NT, G20])
            adst = g.sb("adst", [P, NT, H4])
            shift = g.sb("shift", [P, H4])
            table = g.sb("table", [P, NT, H4])
            last = g.sb("last", [P, G20])
            mx = g.sb("mx", [P, NT, 2 * H4])
            sums = g.sb("sums", [P, NT, H4, 1 + NE])
            gates = g.sb("gates", [P, NT, NE])
            gT = g.sb("gT", [NE, N])
            node_features_stage(nc, a, xn, feat, adst, node_dram, ident)
            edge_max_stage(nc, passed, keys_dram, plan, feat, node_dram, shift, table, iota128, iota32, ident)
            node_max_stage(nc, feat, adst, shift, table, clamped, last, mx, max_dram, ident)
            edge_sum_stage(nc, passed, keys_dram, plan, node_dram, max_dram, sums, iota128, iota32)
            gate_stage(nc, a, feat, mx, clamped, last, sums, gates, gT, ident)
            gated_expert_stage(nc, passed, a, xn, gT, res, out, ident)


def iotas(nc, iota128, iota32):
    with ExitStack() as s:
        m = Memory(nc, s, "iotas")
        i128 = m.sb("i128", [P, P], I32)
        made, copied = m.sem("made"), m.sem("copied")
        block = s.enter_context(nc.Block())

        @block.gpsimd
        def _(pool):
            pool.iota(i128[:], pattern=[[1, P]], base=0, channel_multiplier=0).then_inc(made, 1)

        @block.vector
        def _(dve):
            dve.wait_ge(made, 2)
            dve.tensor_copy(iota128[:], i128[:]).then_inc(copied, 1)
            dve.tensor_copy(iota32[:], i128[:, 0:NT]).then_inc(copied, 1)


def load(nc, dst, src):
    with ExitStack() as s:
        sem = Memory(nc, s, "load").sem("load_sem")
        block = s.enter_context(nc.Block())

        @block.sync
        def _(sp):
            sp.dma_start(dst[:], src).then_inc(sem, 16)
            sp.wait_ge(sem, 17)


def store(nc, out, src):
    with ExitStack() as s:
        stored = Memory(nc, s, "store").sem("stored")
        block = s.enter_context(nc.Block())

        @block.sync
        def _(sp):
            sp.dma_start(out.rearrange("(k p) n -> p k n", p=P), src).then_inc(stored, 16)
            sp.wait_ge(stored, 17)


def layout(z):
    import numpy as np

    def cols(v, per):
        return np.ascontiguousarray(v.reshape(-1, per, P).transpose(2, 0, 1).reshape(P, -1))

    T = lambda v: np.ascontiguousarray(v.T)
    return {
        "x": np.ascontiguousarray(z["x"].reshape(C, N)),
        "wqkvT": T(z["L0_conv_w_qkv"]), "wprojT": T(z["L0_conv_w_proj"]),
        "temp": np.ascontiguousarray(z["L0_conv_temperature"].reshape(HEADS)),
        "wr": z["L0_ffn_Wr"], "br": z["L0_ffn_br"], "w1": z["L0_ffn_W1"], "w2": z["L0_ffn_W2"],
        "b1": cols(z["L0_ffn_b1"], 4), "b2": cols(z["L0_ffn_b2"], 2),
        "gamma": cols(z["L0_ffn_gamma"], 2), "beta": cols(z["L0_ffn_beta"], 2),
        "cw1T": T(z["L1_conv_W1"]), "cb1": cols(z["L1_conv_b1"], 1),
        "cw2T": T(z["L1_conv_W2"]), "cb2": cols(z["L1_conv_b2"], 1),
        "wgat": z["L1_ffn_W_gat"], "att_src": z["L1_ffn_att_src"].reshape(16), "att_dst": z["L1_ffn_att_dst"].reshape(16),
        "b_gat": z["L1_ffn_b_gat"], "ln_gamma": z["L1_ffn_ln_gamma"], "ln_beta": z["L1_ffn_ln_beta"],
        "ew1": z["L1_ffn_W1"], "ew2": z["L1_ffn_W2"], "eb1": cols(z["L1_ffn_b1"], 4), "eb2": z["L1_ffn_b2"],
        "edges": z["L1_ffn_edge_index"],
        "cwoT": T(z["L1_conv_Wout"]), "cbo": cols(z["L1_conv_bout"], 2),
    }


def kernel(**inputs):
    import numpy as np
    import concourse.bacc as bacc
    from concourse.bass_utils import run_bass_kernel_spmd

    nc = bacc.Bacc("TRN2", target_bir_lowering=False, num_devices=1)
    arrays = {f"in_{k}": np.ascontiguousarray(v) for k, v in layout({k: np.asarray(v) for k, v in inputs.items()}).items()}
    aps = {k[3:]: nc.dram_tensor(k, v.shape, mybir.dt.from_np(v.dtype), kind="ExternalInput").ap()
           for k, v in arrays.items()}
    out = nc.dram_tensor("out_dram", [C, N], F32, kind="ExternalOutput").ap()
    program(nc, aps, out)
    r = run_bass_kernel_spmd(nc, [arrays], core_ids=[0])
    return r.results[0]["out_dram"].reshape(1, C, 64, 64)
```

```python
import concourse.bass as bass
from concourse import mybir
from contextlib import ExitStack

F32 = mybir.dt.float32
F16 = mybir.dt.float16
I32 = mybir.dt.int32
ALU = mybir.AluOpType
ACT = mybir.ActivationFunctionType
AX = mybir.AxisListType

P = 128
C = 256
KC = C // P
N = 4096
CH = 512
NCH = N // CH
NT = N // P
HEADS = 8
DH = C // HEADS
QS, KS = 16.0, 1024.0


class Memory:

    spent = []

    def __init__(self, nc, stack, stage):
        self.nc, self.stack, self.stage = nc, stack, stage

    def sb(self, name, shape, dt=F32):
        return self.stack.enter_context(self.nc.sbuf_tensor(f"{self.stage}_{name}", shape, dt))

    def ps(self, name, shape, dt=F32):
        return self.stack.enter_context(self.nc.psum_tensor(f"{self.stage}_{name}", shape, dt))

    def sem(self, name, start=1):
        sem = self.nc.alloc_semaphore(name=f"{self.stage}_{name}")
        if start:
            self.nc.sync.sem_inc(sem, start)
        self.spent.append(sem)
        return sem

    @classmethod
    def clear_semaphores(cls, nc):
        nc.all_engine_barrier()
        nc.clear_and_free_semaphores(cls.spent)
        nc.all_engine_barrier()
        cls.spent = []


def fill_constants(nc, ones_mean, block_ones, ident, stack_ident, den_pick):
    with ExitStack() as s:
        filled = Memory(nc, s, "fill_constants").sem("const_filled")
        block = s.enter_context(nc.Block())

        @block.gpsimd
        def _(pool):
            pool.memset(ones_mean[:], 1.0 / C).then_inc(filled, 1)
            pool.memset(block_ones[:], 1.0).then_inc(filled, 1)
            pool.memset(ident[:], 0.0).then_inc(filled, 1)
            pool.memset(stack_ident[:], 0.0).then_inc(filled, 1)
            pool.memset(den_pick[:], 0.0).then_inc(filled, 1)
            pool.wait_ge(filled, 6)
            v = block_ones[:].rearrange("p (g j) -> p g j", g=4)
            pool.affine_select(out=v, in_=v, compare_op=ALU.is_ge, fill=0.0, base=0,
                               pattern=[[-32, 4], [0, 32]], channel_multiplier=1).then_inc(filled, 1)
            pool.wait_ge(filled, 7)
            pool.affine_select(out=v, in_=v, compare_op=ALU.is_ge, fill=0.0, base=31,
                               pattern=[[32, 4], [0, 32]], channel_multiplier=-1).then_inc(filled, 1)
            pool.affine_select(out=ident[:], in_=ident[:], compare_op=ALU.not_equal, fill=1.0, base=0,
                               pattern=[[-1, P]], channel_multiplier=1).then_inc(filled, 1)
            for j in range(4):
                pool.affine_select(out=stack_ident[:], in_=stack_ident[:], compare_op=ALU.not_equal, fill=1.0,
                                   base=-32 * j, pattern=[[-1, DH]], channel_multiplier=1).then_inc(filled, 1)
                pool.wait_ge(filled, 9 + 2 * j + 1)
                pool.affine_select(out=den_pick[:], in_=den_pick[:], compare_op=ALU.not_equal, fill=1.0,
                                   base=-32 * j, pattern=[[0, 1]], channel_multiplier=1).then_inc(filled, 1)
                pool.wait_ge(filled, 10 + 2 * j + 1)


def qkv_stage(nc, x, wqkvT, temp, qk_dram, v_dram, ones_mean, block_ones):
    x_v = x.rearrange("(k p) n -> p k n", p=P)
    w_v = wqkvT.rearrange("(k p) o -> p k o", p=P)
    with ExitStack() as s:
        m = Memory(nc, s, "qkv")
        w = m.sb("wqkv_sb", [P, KC, 3 * C])
        xin = m.sb("x_in", [P, 2, KC, CH])
        xc = m.sb("x_centred", [P, 2, KC, CH])
        sq = m.sb("x_squared", [P, KC, CH])
        rstd = m.sb("x_rstd", [P, CH])
        sd = m.sb("x_deviation", [P, CH])
        eps = m.sb("ln_eps", [P, 1])
        norm = m.sb("qk_norm", [P, CH])
        nm = m.sb("qk_norm_floored", [P, CH])
        qsq = m.sb("qk_squared", [P, 2, CH])
        rn = m.sb("qk_rnorm", [P, CH])
        qn = m.sb("qk_unit", [P, 2, CH])
        tcol = m.sb("temp_col", [P, 2])
        scale = m.sb("qk_scale", [P, 4])
        parts = m.sb("qk_parts", [P, 4, 2, N], F16)
        v_sb = m.sb("v_sb", [P, HEADS, NT, DH])
        mean_ps = m.ps("mean_ps", [P, CH])
        var_ps = m.ps("var_ps", [P, CH])
        qk_ps = m.ps("qk_ps", [P, 2, CH])
        n2_ps = m.ps("n2_ps", [P, CH])
        v_ps = m.ps("v_ps", [P, 2, 2, C])
        w_loaded, t_loaded = m.sem("w_loaded"), m.sem("t_loaded")
        x_loaded = [m.sem("x_loaded0"), m.sem("x_loaded1")]
        scale_ready = m.sem("scale_ready")
        eps_ready, sd_ready, norm_ready, floored = m.sem("eps_ready"), m.sem("sd_ready"), m.sem("norm_ready"), m.sem("floored")
        mean_ready, centred, squared = m.sem("mean_ready"), m.sem("centred"), m.sem("squared")
        var_ready, rstd_ready, normed = m.sem("var_ready"), m.sem("rstd_ready"), m.sem("normed")
        qk_ready, qk_squared, n2_ready = m.sem("qk_ready"), m.sem("qk_squared"), m.sem("n2_ready")
        rn_ready, unit_ready = m.sem("rn_ready"), m.sem("unit_ready")
        high_ready, low_ready = m.sem("high_ready"), m.sem("low_ready")
        v_ready, v_copied, stored = m.sem("v_ready"), m.sem("v_copied"), m.sem("stored")
        block = s.enter_context(nc.Block())

        @block.sync
        def _(sp):
            sp.dma_start(w[:], w_v).then_inc(w_loaded, 16)
            for g in range(2):
                for h in range(4):
                    sp.dma_start(tcol[32 * h:32 * h + 32, g:g + 1],
                                 temp[4 * g + h:4 * g + h + 1].rearrange("(a b) -> a b", a=1).to_broadcast([32, 1]))\
                      .then_inc(t_loaded, 16)
            with sp.Fori(0, NCH // 2) as i:
                for b in range(2):
                    sp.wait_ge(centred, 2 * i + b + 1)
                    sp.dma_start(xin[:, b], x_v[:, :, bass.ds((2 * i + b) * CH, CH)]).then_inc(x_loaded[b], 16)
            sp.wait_ge(high_ready, 4 * NCH + 1)
            sp.wait_ge(low_ready, 4 * NCH + 1)
            for g in range(4):
                for part in range(2):
                    sp.dma_start(qk_dram[g, part], parts[:, g, part]).then_inc(stored, 16)
            sp.wait_ge(v_copied, 2 * NCH + 1)
            for h in range(HEADS):
                sp.dma_start(v_dram[h], v_sb[:, h].rearrange("p t d -> p (t d)")).then_inc(stored, 16)
            sp.wait_ge(stored, 16 * (8 + HEADS) + 1)

        @block.tensor
        def _(pe):
            pe.wait_ge(w_loaded, 17)
            with pe.Fori(0, NCH // 2) as i:
                for b in range(2):
                    n = 2 * i + b
                    pe.wait_ge(x_loaded[b], 16 * i + 16 + 1)
                    pe.wait_ge(centred, n + 1)
                    for k in range(KC):
                        mm = nc.tensor.matmul(mean_ps[:], ones_mean[:], xin[:, b, k], start=k == 0, stop=k == KC - 1)
                    mm.then_inc(mean_ready, 1)
                    pe.wait_ge(squared, n + 2)
                    pe.wait_ge(sd_ready, n + 1)
                    for k in range(KC):
                        mm = nc.tensor.matmul(var_ps[:], ones_mean[:], sq[:, k], start=k == 0, stop=k == KC - 1)
                    mm.then_inc(var_ready, 1)
                    pe.wait_ge(normed, n + 2)

                    def norm2(g):
                        pe.wait_ge(qk_squared, 4 * n + g + 2)
                        pe.wait_ge(norm_ready, 4 * n + g + 1)
                        nc.tensor.matmul(n2_ps[:], block_ones[:], qsq[:, g % 2], start=True, stop=True)\
                            .then_inc(n2_ready, 1)

                    def values(half):
                        pe.wait_ge(v_copied, 2 * n + 1)
                        for j in range(2):
                            t = 2 * half + j
                            for k in range(KC):
                                mm = nc.tensor.matmul(v_ps[:, half, j], xc[:, b, k, t * P:(t + 1) * P],
                                                      w[:, k, 2 * C:3 * C], start=k == 0, stop=k == KC - 1)
                        mm.then_inc(v_ready, 1)

                    for g in range(4):
                        pe.wait_ge(unit_ready, 4 * n + max(g - 1, 0) + 1)
                        for k in range(KC):
                            mm = nc.tensor.matmul(qk_ps[:, g % 2], w[:, k, g * P:(g + 1) * P], xc[:, b, k],
                                                  start=k == 0, stop=k == KC - 1)
                        mm.then_inc(qk_ready, 1)
                        if g == 0:
                            values(0)
                        if g == 1:
                            values(1)
                        if g >= 1:
                            norm2(g - 1)
                    norm2(3)

        def part_of(g, part, n):
            if g >= 2:
                return parts[:, g, part, bass.ds(n * CH, CH)]
            return parts[:, g, part].rearrange("p (r c) -> p c r", r=16)[:, bass.ds(n * 32, 32), :]

        def unit_of(g):
            return qn[:, g % 2] if g >= 2 else qn[:, g % 2].rearrange("p (c r) -> p c r", r=16)

        def high(act, n, g):
            act.wait_ge(n2_ready, 4 * n + g + 2)
            act.wait_ge(floored, 4 * n + g + 1)
            nc.scalar.activation(norm[:], n2_ps[:], ACT.Sqrt).then_inc(norm_ready, 1)
            act.wait_ge(unit_ready, 4 * n + g + 2)
            act.wait_ge(eps_ready, 2)
            nc.scalar.activation(part_of(g, 0, n), unit_of(g), ACT.Copy).then_inc(high_ready, 1)

        @block.scalar
        def _(act):
            act.wait_ge(eps_ready, 2)
            with act.Fori(0, NCH // 2) as i:
                for b in range(2):
                    n = 2 * i + b
                    act.wait_ge(centred, n + 2)
                    act.wait_ge(var_ready, n + 1)
                    for k in range(KC):
                        a = nc.scalar.activation(sq[:, k], xc[:, b, k], ACT.Square)
                    a.then_inc(squared, 1)
                    act.wait_ge(var_ready, n + 2)
                    act.wait_ge(rstd_ready, n + 1)
                    nc.scalar.activation(sd[:], var_ps[:], ACT.Sqrt, bias=eps[:]).then_inc(sd_ready, 1)
                    for g in range(4):
                        act.wait_ge(qk_ready, 4 * n + g + 2)
                        act.wait_ge(n2_ready, 4 * n + max(g - 1, 0) + 1)
                        nc.scalar.activation(qsq[:, g % 2], qk_ps[:, g % 2], ACT.Square).then_inc(qk_squared, 1)
                        if g in (1, 2):
                            half = g - 1
                            act.wait_ge(v_ready, 2 * n + half + 2)
                            act.wait_ge(eps_ready, 2)
                            for j in range(2):
                                a = nc.scalar.activation(
                                    v_sb[:, :, bass.ds(4 * n + 2 * half + j, 1), :].rearrange("p h o d -> p (h o) d"),
                                    v_ps[:, half, j].rearrange("p (h d) -> p h d", h=HEADS), ACT.Copy)
                            a.then_inc(v_copied, 1)
                        if g >= 1:
                            high(act, n, g - 1)
                    high(act, n, 3)

        @block.vector
        def _(dve):
            dve.memset(eps[:], 1e-6).then_inc(eps_ready, 1)
            dve.wait_ge(t_loaded, 16 * 8 + 1)
            dve.tensor_scalar(scale[:, 0:2], tcol[:], QS, None, ALU.mult).then_inc(scale_ready, 1)
            dve.memset(scale[:, 2:4], KS).then_inc(scale_ready, 1)
            dve.wait_ge(scale_ready, 3)
            with dve.Fori(0, NCH // 2) as i:
                for b in range(2):
                    n = 2 * i + b
                    dve.wait_ge(mean_ready, n + 2)
                    for k in range(KC):
                        d = dve.tensor_tensor(xc[:, b, k], xin[:, b, k], mean_ps[:], ALU.subtract)
                    d.then_inc(centred, 1)
                    dve.wait_ge(sd_ready, n + 2)
                    dve.reciprocal(rstd[:], sd[:]).then_inc(rstd_ready, 1)
                    dve.wait_ge(rstd_ready, n + 2)
                    dve.wait_ge(squared, n + 2)
                    for k in range(KC):
                        d = dve.tensor_tensor(xc[:, b, k], xc[:, b, k], rstd[:], ALU.mult)
                    d.then_inc(normed, 1)
                    for g in range(4):
                        dve.wait_ge(norm_ready, 4 * n + g + 2)
                        dve.tensor_scalar(nm[:], norm[:], 1e-12, None, ALU.max).then_inc(floored, 1)
                        dve.wait_ge(floored, 4 * n + g + 2)
                        dve.reciprocal(rn[:], nm[:]).then_inc(rn_ready, 1)
                        dve.wait_ge(rn_ready, 4 * n + g + 2)
                        dve.wait_ge(low_ready, 4 * n + max(g - 1, 0) + 1)
                        dve.scalar_tensor_tensor(qn[:, g % 2], rn[:], scale[:, g:g + 1], qk_ps[:, g % 2],
                                                 ALU.mult, ALU.mult).then_inc(unit_ready, 1)
                        dve.wait_ge(high_ready, 4 * n + g + 2)
                        dve.wait_ge(unit_ready, 4 * n + g + 2)
                        dve.tensor_tensor(part_of(g, 1, n), unit_of(g), part_of(g, 0, n), ALU.subtract)\
                            .then_inc(low_ready, 1)


def attention_stage(nc, passed, temp, qk_dram, v_dram, attn, stack_ident, den_pick):
    PAIRS = NT // 2
    QUADS = NT // 4
    OCTS = NT // 8
    NQ = 3
    AHEAD = 3
    with ExitStack() as s:
        m = Memory(nc, s, "attention")
        qst = m.sb("q_stack", [P, 2, N], F16)
        kst = m.sb("k_stack", [P, 2, N], F16)
        vb = m.sb("v_head", [P, 2, NT, DH])
        tb = m.sb("temp_all", [P, HEADS])
        nbias = m.sb("neg_bound", [P, HEADS])
        tneg = m.sb("temp_neg", [P, HEADS])
        probs = m.sb("probs", [P, 4, 4, CH])
        half = m.sb("half_sums", [P, 2, 2, CH])
        quad = m.sb("quad_sums", [P, 2, CH])
        octs = m.sb("oct_sums", [P, OCTS, CH])
        oc = m.sb("o_copy", [P, CH])
        dc = m.sb("den_copy", [P, CH])
        rden = m.sb("rden", [P, 4, 1])
        ones32 = m.sb("ones32", [P, DH])
        s_ps = m.ps("s_ps", [P, 2, 2, CH])
        o_ps = m.ps("o_ps", [P, 2, CH])
        den_ps = m.ps("den_ps", [P, CH])
        t_ps = m.ps("t_ps", [P, 4, DH + 1])
        stacks_loaded = [m.sem("stacks_loaded0"), m.sem("stacks_loaded1")]
        temp_loaded, bias_ready, tneg_ready = m.sem("temp_loaded"), m.sem("bias_ready"), m.sem("tneg_ready")
        s_ready, exp_done, pv_done = m.sem("s_ready"), m.sem("exp_done"), m.sem("pv_done", start=4)
        half_done, quad_done, oct_done, den_done = m.sem("half_done", start=4), m.sem("quad_done", start=2), m.sem("oct_done"), m.sem("den_done")
        o_copied, t_ready, attn_done, rden_done = m.sem("o_copied"), m.sem("t_ready"), m.sem("attn_done"), m.sem("rden_done")
        block = s.enter_context(nc.Block())

        @block.sync
        def _(sp):
            sp.dma_start(tb[:], temp.rearrange("(a h) -> a h", a=1).to_broadcast([P, HEADS])).then_inc(temp_loaded, 16)
            for h in range(HEADS):
                b, g, r = h % 2, h // 4, 32 * (h % 4)
                if h >= 2:
                    sp.wait_ge(den_done, (h - 1) * NCH + 1)
                for j in range(4):
                    rows = slice(32 * j, 32 * j + 32)
                    sp.dma_start(qst[rows, b], qk_dram[g, j // 2, r:r + 32]).then_inc(stacks_loaded[b], 16)
                    sp.dma_start(kst[rows, b], qk_dram[2 + g, j % 2, r:r + 32]).then_inc(stacks_loaded[b], 16)
                sp.dma_start(vb[:, b].rearrange("p t d -> p (t d)"), v_dram[h]).then_inc(stacks_loaded[b], 16)

        @block.tensor
        def _(pe):
            def scores(G, u, b, column):
                pe.wait_ge(exp_done, G * PAIRS + u + 1)
                for j in range(2):
                    t = 2 * u + j
                    mm = nc.tensor.matmul(s_ps[:, u % 2, j], kst[:, b, t * P:(t + 1) * P],
                                          qst[:, b, column], start=True, stop=True)
                mm.then_inc(s_ready, 1)

            def values(G, w, b, qb):
                pe.wait_ge(exp_done, G * PAIRS + 2 * w + 4)
                for j in range(4):
                    mm = nc.tensor.matmul(o_ps[32 * j:32 * j + 32, qb], vb[:, b, 4 * w + j], probs[:, w % 4, j],
                                          start=w == 0, stop=w == QUADS - 1, skip_group_check=True)
                mm.then_inc(pv_done, 1)

            def close(G):
                pe.wait_ge(oct_done, (G + 1) * OCTS + 1)
                for j in range(OCTS):
                    mm = nc.tensor.matmul(den_ps[32 * j:32 * j + 32], ones32[:], octs[:, j], start=True, stop=True,
                                          skip_group_check=True)
                mm.then_inc(den_done, 1)

            def turn(G, blk):
                if blk == 0:
                    pe.wait_ge(o_copied, 2 * G + 3)
                    pe.wait_ge(attn_done, G + 1)
                cols = slice(blk * P, (blk + 1) * P)
                nc.tensor.matmul(t_ps[:, blk, 0:DH], oc[:, cols], stack_ident[:], start=True, stop=True,
                                 skip_group_check=True)
                mm = nc.tensor.matmul(t_ps[:, blk, DH:DH + 1], dc[:, cols], den_pick[:], start=True,
                                      stop=True, skip_group_check=True)
                if blk == 3:
                    mm.then_inc(t_ready, 1)

            def group(G, b, qb, column, following, first=False):
                for u in range(AHEAD, PAIRS):
                    scores(G, u, b, column)
                    if u % 2:
                        values(G, (u - 3) // 2, b, qb)
                    if u == 5 and not first:
                        close(G - 1)
                    if u in (8, 9, 11, 13) and not first:
                        turn(G - 1, (8, 9, 11, 13).index(u))
                if following is not None:
                    for u in range(AHEAD - 1):
                        scores(G + 1, u, *following)
                values(G, QUADS - 1, b, qb)
                if following is not None:
                    scores(G + 1, AHEAD - 1, *following)

            def after_first(hp, b, last):
                for qc in range(1, NCH - 1):
                    group((2 * hp + b) * NCH + qc, b, qc % 2, slice(qc * CH, qc * CH + CH),
                          (b, slice(qc * CH + CH, qc * CH + 2 * CH)))
                G = (2 * hp + b + 1) * NCH
                if last:
                    group(G - 1, b, 1, slice(N - CH, N), None)
                    return
                pe.wait_ge(stacks_loaded[1 - b], 16 * 9 * (hp + b + 1) + 1)
                pe.sem_inc(passed, 1)
                group(G - 1, b, 1, slice(N - CH, N), (1 - b, slice(0, CH)))
                group(G, 1 - b, 0, slice(0, CH), (1 - b, slice(CH, 2 * CH)))

            pe.wait_ge(bias_ready, 3)
            pe.wait_ge(stacks_loaded[0], 16 * 9 + 1)
            for u in range(AHEAD):
                scores(0, u, 0, slice(0, CH))
            group(0, 0, 0, slice(0, CH), (0, slice(CH, 2 * CH)), first=True)
            with pe.Fori(0, HEADS // 2 - 1) as hp:
                for b in range(2):
                    after_first(hp, b, False)
            for b in range(2):
                after_first(HEADS // 2 - 1, b, b == 1)
            close(HEADS * NCH - 1)
            for blk in range(4):
                turn(HEADS * NCH - 1, blk)

        @block.scalar
        def _(act):
            act.wait_ge(bias_ready, 3)
            act.sem_inc(exp_done, 1)
            with act.Fori(0, HEADS) as h:
                for qc in range(NCH):
                    G = h * NCH + qc
                    for u in range(PAIRS):
                        w = u // 2
                        act.wait_ge(s_ready, G * PAIRS + u + 2)
                        if u % 2 == 0:
                            act.wait_ge(pv_done, G * QUADS + w + 1)
                            act.wait_ge(half_done, G * QUADS + w + 1)
                        act.sem_inc(passed, 1)
                        nc.scalar.activation(probs[:, w % 4, 2 * (u % 2):2 * (u % 2) + 2], s_ps[:, u % 2], ACT.Exp,
                                             bias=nbias[:, bass.ds(h, 1)], scale=1.0 / (QS * KS)).then_inc(exp_done, 1)

        @block.gpsimd
        def _(pool):
            with pool.Fori(0, HEADS) as h:
                for qc, w in [(qc, w) for qc in range(NCH) for w in range(QUADS)]:
                    G = h * NCH + qc
                    pool.wait_ge(half_done, G * QUADS + w + 5)
                    pool.wait_ge(oct_done, G * OCTS + w // 2 + 1)
                    pool.tensor_tensor(quad[:, w % 2], half[:, w % 2, 0], half[:, w % 2, 1], ALU.add).then_inc(quad_done, 1)
                    if w % 2:
                        pool.wait_ge(quad_done, G * QUADS + w + 3)
                        pool.wait_ge(den_done, G + 1)
                        pool.tensor_tensor(octs[:, w // 2], quad[:, 0], quad[:, 1], ALU.add).then_inc(oct_done, 1)

        @block.vector
        def _(dve):
            dve.memset(ones32[:], 1.0).then_inc(bias_ready, 1)
            dve.wait_ge(temp_loaded, 17)
            dve.tensor_scalar(tneg[:], tb[:], -1.0, None, ALU.mult).then_inc(tneg_ready, 1)
            dve.wait_ge(tneg_ready, 2)
            dve.tensor_tensor(nbias[:], tb[:], tneg[:], ALU.min).then_inc(bias_ready, 1)

            def halves(G, w):
                dve.wait_ge(exp_done, G * PAIRS + 2 * w + 4)
                dve.wait_ge(quad_done, G * QUADS + w + 1)
                dve.tensor_tensor(half[:, w % 2], probs[:, w % 4, 0:2], probs[:, w % 4, 2:4], ALU.add)\
                    .then_inc(half_done, 1)

            def copy_o(G, qb):
                dve.wait_ge(t_ready, G + 1)
                dve.wait_ge(pv_done, (G + 1) * QUADS + 4)
                dve.tensor_copy(oc[:], o_ps[:, qb]).then_inc(o_copied, 1)

            def copy_den(G):
                dve.wait_ge(den_done, G + 2)
                dve.tensor_copy(dc[:], den_ps[:]).then_inc(o_copied, 1)

            def divide(G, h, qc):
                dve.wait_ge(t_ready, G + 2)
                dve.reciprocal(rden[:], t_ps[:, :, DH:DH + 1]).then_inc(rden_done, 1)
                dve.wait_ge(rden_done, G + 2)
                dst = attn[:].rearrange("p k r (h d) -> p r k h d", h=HEADS)[:, 2 * qc:2 * qc + 2, :, bass.ds(h, 1), :]\
                    .rearrange("p r k o d -> p r k (o d)")
                dve.tensor_tensor(dst, t_ps[:, :, 0:DH].rearrange("p (r k) d -> p r k d", r=2),
                                  rden[:].rearrange("p (r k) o -> p r k o", r=2).to_broadcast([P, 2, KC, DH]),
                                  ALU.mult).then_inc(attn_done, 1)

            def group(G, h, qc, qb):
                for w in range(QUADS):
                    halves(G, w)
                    if w == 0:
                        copy_o(G - 1, qb)
                    if w == 2:
                        copy_den(G - 1)
                    if w == 5:
                        divide(G - 1, h, qc)

            def after_first(h):
                for qc in range(NCH - 1):
                    group(h * NCH + qc + 1, h, qc, qc % 2)

            for w in range(QUADS):
                halves(0, w)
            with dve.Fori(0, HEADS - 1) as h:
                after_first(h)
                group((h + 1) * NCH, h, NCH - 1, 1)
            after_first(HEADS - 1)
            copy_o(HEADS * NCH - 1, 1)
            copy_den(HEADS * NCH - 1)
            divide(HEADS * NCH - 1, HEADS - 1, NCH - 1)


def projection_stage(nc, x, wprojT, attn, res):
    with ExitStack() as s:
        m = Memory(nc, s, "projection")
        w = m.sb("wproj_sb", [P, KC, C])
        o_ps = m.ps("proj_ps", [P, 2, KC, CH])
        w_loaded, x_loaded = m.sem("w_loaded"), m.sem("x_loaded")
        projected, added = m.sem("projected"), m.sem("added")
        block = s.enter_context(nc.Block())

        @block.sync
        def _(sp):
            sp.dma_start(w[:], wprojT.rearrange("(k p) o -> p k o", p=P)).then_inc(w_loaded, 16)
            sp.dma_start(res[:], x.rearrange("(k p) n -> p k n", p=P)).then_inc(x_loaded, 16)

        @block.tensor
        def _(pe):
            pe.wait_ge(w_loaded, 17)
            with pe.Fori(0, NCH // 2) as i:
                for b in range(2):
                    n = 2 * i + b
                    pe.wait_ge(added, 2 * i + 1)
                    for o in range(KC):
                        for k in range(KC):
                            mm = nc.tensor.matmul(o_ps[:, b, o], w[:, k, o * P:(o + 1) * P],
                                                  attn[:, k, bass.ds(2 * n, 2), :].rearrange("p r c -> p (r c)"),
                                                  start=k == 0, stop=k == KC - 1)
                    mm.then_inc(projected, 1)

        @block.vector
        def _(dve):
            dve.wait_ge(x_loaded, 17)
            with dve.Fori(0, NCH // 2) as i:
                for b in range(2):
                    n = 2 * i + b
                    dve.wait_ge(projected, n + 2)
                    chunk = res[:, :, bass.ds(n * CH, CH)]
                    dve.tensor_tensor(chunk, chunk, o_ps[:, b], ALU.add).then_inc(added, 1)


def layer_norm_stage(nc, name, src, dst, eps_value, ones_mean, col_sum=None):
    with ExitStack() as s:
        m = Memory(nc, s, name)
        eps = m.sb("ln_eps", [P, 1])
        xc = m.sb("x_centred", [P, 2, KC, CH])
        sq = m.sb("x_squared", [P, 2, KC, CH])
        sd = m.sb("x_deviation", [P, 2, CH])
        rstd = m.sb("x_rstd", [P, 2, CH])
        mean_ps = m.ps("mean_ps", [P, 2, CH])
        var_ps = m.ps("var_ps", [P, 2, CH])
        eps_ready, mean_ready, centred = m.sem("eps_ready"), m.sem("mean_ready"), m.sem("centred")
        squared, var_ready, sd_ready = m.sem("squared"), m.sem("var_ready"), m.sem("sd_ready")
        rstd_ready, normed = m.sem("rstd_ready"), m.sem("normed")
        block = s.enter_context(nc.Block())

        @block.tensor
        def _(pe):
            with pe.Fori(0, NCH // 2) as i:
                for b in range(2):
                    pe.wait_ge(centred, 2 * i + 1)
                    for k in range(KC):
                        mm = nc.tensor.matmul(mean_ps[:, b], ones_mean[:], src[:, k, bass.ds((2 * i + b) * CH, CH)],
                                              start=k == 0, stop=k == KC - 1)
                    mm.then_inc(mean_ready, 1)
                for b in range(2):
                    pe.wait_ge(squared, 2 * i + b + 2)
                    pe.wait_ge(sd_ready, 2 * i + 1)
                    for k in range(KC):
                        mm = nc.tensor.matmul(var_ps[:, b], ones_mean[:], sq[:, b, k], start=k == 0, stop=k == KC - 1)
                    mm.then_inc(var_ready, 1)

        @block.scalar
        def _(act):
            act.wait_ge(eps_ready, 2)
            with act.Fori(0, NCH // 2) as i:
                for b in range(2):
                    act.wait_ge(centred, 2 * i + b + 2)
                    act.wait_ge(var_ready, 2 * i + 1)
                    nc.scalar.activation(sq[:, b], xc[:, b], ACT.Square).then_inc(squared, 1)
                for b in range(2):
                    act.wait_ge(var_ready, 2 * i + b + 2)
                    act.wait_ge(rstd_ready, 2 * i + 1)
                    nc.scalar.activation(sd[:, b], var_ps[:, b], ACT.Sqrt, bias=eps[:]).then_inc(sd_ready, 1)

        @block.vector
        def _(dve):
            dve.memset(eps[:], eps_value).then_inc(eps_ready, 1)
            with dve.Fori(0, NCH // 2) as i:
                for b in range(2):
                    n = 2 * i + b
                    dve.wait_ge(mean_ready, n + 2)
                    dve.wait_ge(normed, 2 * i + 1)
                    dve.tensor_tensor(xc[:, b], src[:, :, bass.ds(n * CH, CH)],
                                      mean_ps[:, b:b + 1].to_broadcast([P, KC, CH]), ALU.subtract).then_inc(centred, 1)
                for b in range(2):
                    n = 2 * i + b
                    dve.wait_ge(sd_ready, n + 2)
                    dve.reciprocal(rstd[:, b], sd[:, b]).then_inc(rstd_ready, 1)
                    dve.wait_ge(centred, n + 2)
                    dve.wait_ge(rstd_ready, n + 2)
                    dve.tensor_tensor(dst[:, :, bass.ds(n * CH, CH)], xc[:, b],
                                      rstd[:, b:b + 1].to_broadcast([P, KC, CH]), ALU.mult).then_inc(normed, 1)
            if col_sum is not None:
                dve.wait_ge(normed, NCH + 1)
                dve.reduce_sum(col_sum[:], dst[:], axis=AX.X).then_inc(normed, 1)


def routing_stage(nc, a, col_sum, top_w, top_i):
    E = 8
    CAPACITY = float(-(-N * 5 // (4 * E)))
    with ExitStack() as s:
        m = Memory(nc, s, "routing")
        wr = m.sb("wr_sb", [P, KC, E])
        br = m.sb("br_sb", [1, E])
        mcol = m.sb("token_mean", [P, KC])
        row = m.sb("route_rows", [1, 12, E])
        one = m.sb("route_scalars", [1, 12])
        ones_row = m.sb("ones_row", [1, P])
        lg_ps = m.ps("logits_ps", [1, E])
        w_ps = m.ps("top_w_ps", [P, 2])
        loaded, mean_ready, logits_ready = m.sem("loaded"), m.sem("mean_ready"), m.sem("logits_ready")
        step, exp_in, exp_out, w_ready, ws_ready = (m.sem(x) for x in ("step", "exp_in", "exp_out", "w_ready", "ws_ready"))
        block = s.enter_context(nc.Block())

        @block.sync
        def _(sp):
            sp.dma_start(wr[:], a["wr"].rearrange("(k p) e -> p k e", p=P)).then_inc(loaded, 16)
            sp.dma_start(br[:], a["br"].rearrange("(a e) -> a e", a=1)).then_inc(loaded, 16)

        @block.tensor
        def _(pe):
            pe.wait_ge(loaded, 33)
            pe.wait_ge(mean_ready, 2)
            for k in range(KC):
                mm = nc.tensor.matmul(lg_ps[:], mcol[:, k:k + 1], wr[:, k], start=k == 0, stop=k == KC - 1)
            mm.then_inc(logits_ready, 1)
            pe.wait_ge(ws_ready, 2)
            nc.tensor.matmul(w_ps[:], ones_row[:], row[:, 9, 0:2], start=True, stop=True).then_inc(w_ready, 1)

        @block.scalar
        def _(act):
            for n, (src, dst, bias, total) in enumerate(((0, 1, 1, 2), (4, 5, 5, 6), (7, 8, 9, 10))):
                act.wait_ge(exp_in, n + 2)
                w = E if n < 2 else 2
                nc.scalar.activation(row[:, dst, 0:w], row[:, src, 0:w], ACT.Exp, bias=one[:, bias:bias + 1],
                                     accum_out=one[:, total:total + 1]).then_inc(exp_out, 1)

        @block.vector
        def _(dve):
            count = [0]

            def chain(ins):
                count[0] += 1
                ins.then_inc(step, 1)
                dve.wait_ge(step, count[0] + 1)

            dve.memset(ones_row[:], 1.0).then_inc(step, 1)
            count[0] += 1
            dve.tensor_scalar(mcol[:], col_sum[:], 1.0 / N, None, ALU.mult).then_inc(mean_ready, 1)
            dve.wait_ge(logits_ready, 2)
            chain(dve.tensor_tensor(row[:, 0], lg_ps[:], br[:], ALU.add))

            def softmax(n, src, dst, neg, total, w):
                chain(dve.reduce_max(one[:, neg - 1:neg], row[:, src, 0:w], axis=AX.X))
                dve.tensor_scalar(one[:, neg:neg + 1], one[:, neg - 1:neg], -1.0, None, ALU.mult).then_inc(exp_in, 1)
                dve.wait_ge(exp_out, n + 2)
                chain(dve.reciprocal(one[:, total + 1:total + 2], one[:, total:total + 1]))
                return dve.tensor_scalar(row[:, dst, 0:w], row[:, dst, 0:w], one[:, total + 1:total + 2], None, ALU.mult)

            chain(softmax(0, 0, 1, 1, 2, E))
            chain(dve.tensor_scalar(row[:, 2], row[:, 1], float(N), None, ALU.mult))
            chain(dve.reciprocal(row[:, 3], row[:, 2]))
            chain(dve.tensor_scalar(row[:, 3], row[:, 3], CAPACITY, 1.0, ALU.mult, ALU.min))
            chain(dve.tensor_tensor(row[:, 4], row[:, 1], row[:, 3], ALU.mult))
            chain(softmax(1, 4, 5, 5, 6, E))
            chain(dve.max(row[:, 7], row[:, 5]))
            chain(dve.max_index(top_i[:], row[:, 7], row[:, 5]))
            chain(softmax(2, 7, 8, 9, 10, 2))
            dve.tensor_copy(row[:, 9, 0:2], row[:, 8, 0:2]).then_inc(ws_ready, 1)
            dve.wait_ge(w_ready, 2)
            dve.tensor_copy(top_w[:], w_ps[:]).then_inc(step, 1)


def expert_stage(nc, a, xn, top_w, top_i, z):
    F = 512
    KF = F // P
    with ExitStack() as s:
        m = Memory(nc, s, "expert")
        w1 = m.sb("w1_sb", [P, 2, KC, F])
        w2 = m.sb("w2_sb", [P, 2, KF, C])
        b1 = m.sb("b1_sb", [P, 2, KF])
        b2 = m.sb("b2_sb", [P, 2, KC])
        b2w = m.sb("b2_weighted", [P, 2, KC])
        b2s = m.sb("b2_sum", [P, KC])
        hid = m.sb("hidden", [P, 4, CH])
        h_ps = m.ps("hidden_ps", [P, 2, CH])
        y_ps = m.ps("y_ps", [P, 2, KC, CH])
        loaded, weighted = m.sem("loaded"), m.sem("weighted")
        h_ready, h_done, y_ready, z_done = m.sem("h_ready"), m.sem("h_done"), m.sem("y_ready"), m.sem("z_done")
        block = s.enter_context(nc.Block())

        @block.sync
        def _(sp):
            for j in range(2):
                e = sp.value_load(top_i[0:1, j:j + 1], min_val=0, max_val=7)
                sp.dma_start(w1[:, j], a["w1"].rearrange("e (k p) f -> p e k f", p=P)[:, bass.ds(e, 1)]
                             .rearrange("p o k f -> p (o k) f")).then_inc(loaded, 16)
                sp.dma_start(w2[:, j], a["w2"].rearrange("e (k p) d -> p e k d", p=P)[:, bass.ds(e, 1)]
                             .rearrange("p o k d -> p (o k) d")).then_inc(loaded, 16)
                sp.dma_start(b1[:, j], a["b1"].rearrange("p (e k) -> p e k", k=KF)[:, bass.ds(e, 1)]
                             .rearrange("p o k -> p (o k)")).then_inc(loaded, 16)
                sp.dma_start(b2[:, j], a["b2"].rearrange("p (e k) -> p e k", k=KC)[:, bass.ds(e, 1)]
                             .rearrange("p o k -> p (o k)")).then_inc(loaded, 16)

        @block.tensor
        def _(pe):
            pe.wait_ge(weighted, 6)
            with pe.Fori(0, NCH // 2) as i:
                for b in range(2):
                    n = 2 * i + b

                    def out(q):
                        pe.wait_ge(h_done, 8 * n + q + 2)
                        for o in range(KC):
                            mm = nc.tensor.matmul(y_ps[:, b, o], w2[:, q // KF, q % KF, o * P:(o + 1) * P], hid[:, q % 4],
                                                  start=q == 0, stop=q == 2 * KF - 1)
                        mm.then_inc(y_ready, 1)

                    for q in range(2 * KF):
                        pe.wait_ge(h_done, 8 * n + max(q - 1, 0) + 1)
                        for k in range(KC):
                            mm = nc.tensor.matmul(h_ps[:, q % 2], w1[:, q // KF, k, (q % KF) * P:(q % KF + 1) * P],
                                                  xn[:, k, bass.ds(n * CH, CH)], start=k == 0, stop=k == KC - 1)
                        mm.then_inc(h_ready, 1)
                        if q == 2:
                            pe.wait_ge(z_done, 2 * i + 1)
                        if q >= 2:
                            out(q - 2)
                    out(2 * KF - 2)
                    out(2 * KF - 1)

        @block.scalar
        def _(act):
            act.wait_ge(loaded, 16 * 8 + 1)
            with act.Fori(0, NCH) as n:
                for q in range(2 * KF):
                    act.wait_ge(h_ready, 8 * n + q + 2)
                    act.wait_ge(y_ready, 8 * n + max(q - 3, 0) + 1)
                    nc.scalar.activation(hid[:, q % 4], h_ps[:, q % 2], ACT.Gelu,
                                         bias=b1[:, q // KF, q % KF:q % KF + 1]).then_inc(h_done, 1)

        @block.vector
        def _(dve):
            dve.wait_ge(loaded, 16 * 8 + 1)
            for j in range(2):
                dve.tensor_scalar(w2[:, j], w2[:, j], top_w[:, j:j + 1], None, ALU.mult).then_inc(weighted, 1)
                dve.tensor_scalar(b2w[:, j], b2[:, j], top_w[:, j:j + 1], None, ALU.mult).then_inc(weighted, 1)
            dve.wait_ge(weighted, 5)
            dve.tensor_tensor(b2s[:], b2w[:, 0], b2w[:, 1], ALU.add).then_inc(weighted, 1)
            dve.wait_ge(weighted, 6)
            with dve.Fori(0, NCH // 2) as i:
                for b in range(2):
                    n = 2 * i + b
                    dve.wait_ge(y_ready, 8 * n + 8 + 1)
                    for o in range(KC):
                        ins = dve.scalar_tensor_tensor(z[:, o, bass.ds(n * CH, CH)], y_ps[:, b, o], b2s[:, o:o + 1],
                                                       xn[:, o, bass.ds(n * CH, CH)], ALU.add, ALU.add)
                    ins.then_inc(z_done, 1)


def affine_residual_stage(nc, a, zn, res):
    with ExitStack() as s:
        m = Memory(nc, s, "affine_residual")
        gb = m.sb("gamma_beta", [P, 2, KC])
        loaded, scaled, added = m.sem("loaded"), m.sem("scaled"), m.sem("added")
        block = s.enter_context(nc.Block())

        @block.sync
        def _(sp):
            sp.dma_start(gb[:, 0], a["gamma"].rearrange("p k -> p k")).then_inc(loaded, 16)
            sp.dma_start(gb[:, 1], a["beta"].rearrange("p k -> p k")).then_inc(loaded, 16)

        @block.vector
        def _(dve):
            dve.wait_ge(loaded, 33)
            with dve.Fori(0, NCH) as n:
                for o in range(KC):
                    c = bass.ds(n * CH, CH)
                    dve.tensor_scalar(zn[:, o, c], zn[:, o, c], gb[:, 0, o:o + 1], gb[:, 1, o:o + 1], ALU.mult, ALU.add)\
                        .then_inc(scaled, 1)
                    dve.wait_ge(scaled, 2 * n + o + 2)
                    dve.tensor_tensor(res[:, o, c], res[:, o, c], zn[:, o, c], ALU.add).then_inc(added, 1)


W = 64
PW = W + 4
NB6 = 6 * PW


def conv_in_stage(nc, a, cn, hpad, hT, gate, ident):
    with ExitStack() as s:
        m = Memory(nc, s, "conv_in")
        w1 = m.sb("cw1_sb", [P, KC, P])
        w2 = m.sb("cw2_sb", [P, P])
        b1 = m.sb("cb1_sb", [P, 1])
        b2 = m.sb("cb2_sb", [P, 1])
        hc = m.sb("h_chunk", [P, 2, CH])
        g0 = m.sb("gate_in", [P, 2, CH])
        h_ps = m.ps("h_ps", [P, 2, CH])
        g_ps = m.ps("g_ps", [P, 2, CH])
        t_ps = m.ps("t_ps", [P, 2, 4, P])
        loaded, cleared, h_ready, h_done = m.sem("loaded"), m.sem("cleared"), m.sem("h_ready"), m.sem("h_done")
        padded, g_ready, relu_done, gate_done = m.sem("padded"), m.sem("g_ready"), m.sem("relu_done"), m.sem("gate_done")
        t_ready, t_done = m.sem("t_ready"), m.sem("t_done")
        block = s.enter_context(nc.Block())

        @block.sync
        def _(sp):
            sp.dma_start(w1[:], a["cw1T"].rearrange("(k p) o -> p k o", p=P)).then_inc(loaded, 16)
            sp.dma_start(w2[:], a["cw2T"]).then_inc(loaded, 16)
            sp.dma_start(b1[:], a["cb1"]).then_inc(loaded, 16)
            sp.dma_start(b2[:], a["cb2"]).then_inc(loaded, 16)

        @block.tensor
        def _(pe):
            pe.wait_ge(loaded, 65)
            with pe.Fori(0, NCH // 2) as i:
                for b in range(2):
                    n = 2 * i + b
                    pe.wait_ge(h_done, 2 * i + 1)
                    for k in range(KC):
                        mm = nc.tensor.matmul(h_ps[:, b], w1[:, k], cn[:, k, bass.ds(n * CH, CH)],
                                              start=k == 0, stop=k == KC - 1)
                    mm.then_inc(h_ready, 1)
                    pe.wait_ge(h_done, n + 2)
                    pe.wait_ge(relu_done, 2 * i + 1)
                    nc.tensor.matmul(g_ps[:, b], w2[:], hc[:, b], start=True, stop=True).then_inc(g_ready, 1)
                    pe.wait_ge(t_done, 2 * i + 1)
                    for j in range(4):
                        mm = nc.tensor.transpose(t_ps[:, b, j], hc[:, b, j * P:(j + 1) * P], ident[:])
                    mm.then_inc(t_ready, 1)

        @block.gpsimd
        def _(pool):
            pool.memset(hpad[:], 0.0).then_inc(cleared, 1)
            pool.memset(hT[:, 0], 0.0).then_inc(cleared, 1)
            pool.memset(hT[:, NT + 1], 0.0).then_inc(cleared, 1)
            pool.wait_ge(cleared, 4)
            with pool.Fori(0, NCH // 2) as i:
                for b in range(2):
                    n = 2 * i + b
                    pool.wait_ge(h_done, n + 2)
                    pool.tensor_copy(hpad[:].rearrange("p (y x) -> p y x", x=PW)[:, bass.ds(8 * n + 2, 8), 2:2 + W],
                                     hc[:, b].rearrange("p (y x) -> p y x", x=W)).then_inc(padded, 1)

        @block.scalar
        def _(act):
            act.wait_ge(loaded, 65)
            with act.Fori(0, NCH // 2) as i:
                for b in range(2):
                    n = 2 * i + b
                    act.wait_ge(h_ready, n + 2)
                    act.wait_ge(padded, 2 * i + 1)
                    act.wait_ge(t_ready, 2 * i + 1)
                    nc.scalar.activation(hc[:, b], h_ps[:, b], ACT.Identity, bias=b1[:]).then_inc(h_done, 1)
                    act.wait_ge(loaded, 65)
                    act.wait_ge(relu_done, n + 2)
                    nc.scalar.activation(gate[:, bass.ds(n * CH, CH)], g0[:, b], ACT.Sigmoid).then_inc(gate_done, 1)

        @block.vector
        def _(dve):
            dve.wait_ge(loaded, 65)
            dve.wait_ge(cleared, 4)
            with dve.Fori(0, NCH // 2) as i:
                for b in range(2):
                    n = 2 * i + b
                    dve.wait_ge(g_ready, n + 2)
                    dve.wait_ge(gate_done, 2 * i + 1)
                    dve.tensor_scalar(g0[:, b], g_ps[:, b], b2[:], 0.0, ALU.add, ALU.max).then_inc(relu_done, 1)
                    dve.wait_ge(t_ready, n + 2)
                    dve.tensor_copy(hT[:, bass.ds(4 * n + 1, 4)], t_ps[:, b]).then_inc(t_done, 1)


def conv_out_stage(nc, a, hpad, hT, gate, res, ident):
    with ExitStack() as s:
        m = Memory(nc, s, "conv_out")
        wo = m.sb("wout_sb", [P, C])
        bo = m.sb("bout_sb", [P, KC])
        mask = m.sb("mask", [P, 6, PW])
        hc = m.sb("h_chunk", [P, 2, 4, P])
        hw = m.sb("hT_window", [P, 2, 6, P])
        sc = m.sb("scores", [P, 2, NB6])
        mx = m.sb("score_max", [P, 2])
        nmx = m.sb("neg_max", [P, 2])
        ex = m.sb("exps", [P, 2, 6, PW])
        den = m.sb("dens", [P, 2])
        rden = m.sb("rdens", [P, 2])
        an = m.sb("weights", [P, 2, 6 * W])
        aT = m.sb("weightsT", [P, 2, 3, P])
        att = m.sb("gated", [P, CH])
        g_ps = m.ps("gram_ps", [P, 2, CH])
        t_ps = m.ps("wT_ps", [P, 2, CH])
        s_ps = m.ps("sample_ps", [P, 4, P])
        o_ps = m.ps("out_ps", [P, KC, CH])
        loaded, masked, staged = m.sem("loaded"), m.sem("masked"), m.sem("staged")
        gram_ready, sc_ready, max_ready, nmax_ready = (m.sem(x) for x in ("gram_ready", "sc_ready", "max_ready", "nmax_ready"))
        ex_ready, rden_ready, an_ready, t_ready = (m.sem(x) for x in ("ex_ready", "rden_ready", "an_ready", "t_ready"))
        aT_ready, s_ready, att_ready, o_ready, added = (m.sem(x) for x in ("aT_ready", "s_ready", "att_ready", "o_ready", "added"))
        block = s.enter_context(nc.Block())

        @block.sync
        def _(sp):
            sp.dma_start(wo[:], a["cwoT"]).then_inc(loaded, 16)
            sp.dma_start(bo[:], a["cbo"]).then_inc(loaded, 16)

        @block.gpsimd
        def _(pool):
            pool.memset(mask[:], 0.0).then_inc(masked, 1)
            for dy in range(2):
                rows = mask[W * dy:W * dy + W]
                for q, (pattern, base, mult) in enumerate((
                        ([[0, 6], [1, PW]], 0, -1), ([[0, 6], [-1, PW]], 4, 1),
                        ([[1, 6], [0, PW]], -dy, 0), ([[-1, 6], [0, PW]], 4 + dy, 0))):
                    pool.wait_ge(masked, 4 * dy + q + 2)
                    pool.affine_select(out=rows, in_=rows, compare_op=ALU.is_ge, fill=-1e30, base=base,
                                       pattern=pattern, channel_multiplier=mult).then_inc(masked, 1)
            pool.wait_ge(masked, 10)
            with pool.Fori(0, NCH // 2) as i:
                for b in range(2):
                    n = 2 * i + b
                    pool.wait_ge(s_ready, 2 * i + 1)
                    pool.tensor_copy(hc[:, b].rearrange("p t (y x) -> p (t y) x", x=W),
                                     hpad[:].rearrange("p (y x) -> p y x", x=PW)[:, bass.ds(8 * n + 2, 8), 2:2 + W])\
                        .then_inc(staged, 1)
                    pool.tensor_copy(hw[:, b], hT[:, bass.ds(4 * n, 6)]).then_inc(staged, 1)

        @block.tensor
        def _(pe):
            pe.wait_ge(loaded, 33)
            with pe.Fori(0, NCH // 2) as i:
                for b in range(2):
                    n = 2 * i + b
                    for half in range(2):
                        H = 2 * n + half
                        pe.wait_ge(staged, 2 * n + 2 + 1)
                        pe.wait_ge(sc_ready, H + 1)
                        for j in range(2):
                            t = 2 * half + j
                            mm = nc.tensor.matmul(g_ps[:, j, 0:NB6], hc[:, b, t],
                                                  hpad[:, bass.ds((8 * n + 2 * t) * PW, NB6)], start=True, stop=True)
                        mm.then_inc(gram_ready, 1)
                        pe.wait_ge(an_ready, H + 2)
                        pe.wait_ge(aT_ready, H + 1)
                        for j in range(2):
                            for q in range(3):
                                mm = nc.tensor.transpose(t_ps[:, j, q * P:(q + 1) * P], an[:, j, q * P:(q + 1) * P], ident[:])
                        mm.then_inc(t_ready, 1)
                        pe.wait_ge(aT_ready, H + 2)
                        if half == 0:
                            pe.wait_ge(att_ready, n + 1)
                        for j in range(2):
                            t = 2 * half + j
                            for q in range(3):
                                mm = nc.tensor.matmul(s_ps[:, t], hw[:, b, t + q], aT[:, j, q], start=q == 0, stop=q == 2,
                                                      skip_group_check=True)
                        if half == 1:
                            mm.then_inc(s_ready, 1)
                    pe.wait_ge(att_ready, n + 2)
                    pe.wait_ge(added, n + 1)
                    for o in range(KC):
                        mm = nc.tensor.matmul(o_ps[:, o], wo[:, o * P:(o + 1) * P], att[:], start=True, stop=True)
                    mm.then_inc(o_ready, 1)

        @block.scalar
        def _(act):
            with act.Fori(0, 2 * NCH) as H:
                act.wait_ge(nmax_ready, H + 2)
                act.wait_ge(an_ready, H + 1)
                for j in range(2):
                    e = nc.scalar.activation(ex[:, j].rearrange("p y x -> p (y x)"), sc[:, j], ACT.Exp,
                                             bias=nmx[:, j:j + 1], accum_out=den[:, j:j + 1])
                e.then_inc(ex_ready, 1)
                act.wait_ge(t_ready, H + 2)
                nc.scalar.activation(aT[:].rearrange("p j q c -> p j (q c)"), t_ps[:, :, 0:3 * P], ACT.Copy)\
                    .then_inc(aT_ready, 1)

        @block.vector
        def _(dve):
            dve.wait_ge(masked, 10)
            dve.wait_ge(loaded, 33)
            with dve.Fori(0, NCH) as n:
                for half in range(2):
                    H = 2 * n + half
                    dve.wait_ge(gram_ready, H + 2)
                    dve.wait_ge(ex_ready, H + 1)
                    dve.scalar_tensor_tensor(sc[:], g_ps[:, :, 0:NB6], float(P) ** -0.5,
                                             mask[:].rearrange("p y x -> p (y x)").rearrange("p (o z) -> p o z", o=1)
                                             .to_broadcast([P, 2, NB6]), ALU.mult, ALU.add).then_inc(sc_ready, 1)
                    dve.wait_ge(sc_ready, H + 2)
                    dve.reduce_max(mx[:], sc[:], axis=AX.X).then_inc(max_ready, 1)
                    dve.wait_ge(max_ready, H + 2)
                    dve.tensor_scalar(nmx[:], mx[:], -1.0, None, ALU.mult).then_inc(nmax_ready, 1)
                    dve.wait_ge(ex_ready, H + 2)
                    dve.reciprocal(rden[:], den[:]).then_inc(rden_ready, 1)
                    dve.wait_ge(rden_ready, H + 2)
                    dve.wait_ge(t_ready, H + 1)
                    for j in range(2):
                        ins = dve.tensor_scalar(an[:, j].rearrange("p (y x) -> p y x", x=W), ex[:, j, :, 2:2 + W],
                                                rden[:, j:j + 1], None, ALU.mult)
                    ins.then_inc(an_ready, 1)
                dve.wait_ge(s_ready, n + 2)
                dve.wait_ge(o_ready, n + 1)
                dve.tensor_tensor(att[:], s_ps[:].rearrange("p t x -> p (t x)"), gate[:, bass.ds(n * CH, CH)], ALU.mult)\
                    .then_inc(att_ready, 1)
                dve.wait_ge(o_ready, n + 2)
                for o in range(KC):
                    c = res[:, o, bass.ds(n * CH, CH)]
                    ins = dve.scalar_tensor_tensor(c, o_ps[:, o], bo[:, o:o + 1], c, ALU.add, ALU.add)
                ins.then_inc(added, 1)


EDGES = 1048576
EC = EDGES // P
BITS = 12
CC = 2048
SEG = 64
KEEP = 16
KEPT = EC * KEEP // SEG
LISTED = 64
TURN = 8
HB = 256
U32 = mybir.dt.uint32
BF16 = mybir.dt.bfloat16
RMAX = bass.bass_isa.ReduceOp.max


def edge_keys_stage(nc, passed, edges, keys_dram, plan):
    e_v = edges.rearrange("t (p c) -> t p c", p=P)
    SEGS = CC // SEG
    with ExitStack() as s:
        m = Memory(nc, s, "keys")
        raw = m.sb("raw", [P, 2, 2, CC], I32)
        sp1 = m.sb("src_plus_1", [P, CC])
        kk = m.sb("key_any", [P, CC])
        kb = m.sb("key_chunk", [P, 2, CC])
        work = m.sb("key_left", [P, CC])
        cand = m.sb("packed", [P, 2, SEGS, KEEP])
        ki = m.sb("packed_int", [P, SEGS * KEEP], I32)
        ksrc = m.sb("packed_src", [P, SEGS * KEEP], I32)
        cl = m.sb("listed_from", [P, SEGS * KEEP])
        l1 = m.sb("list_part", [P, 2, KEEP])
        lc = m.sb("list_parts", [P, EC // CC, 2 * KEEP])
        lf = m.sb("list", [P, LISTED + TURN])
        held = m.sb("list_held", [P, LISTED])
        turns_i = m.sb("turns_int", [P, 2], I32)
        turns_f = m.sb("turns", [P, 1])
        left = m.sb("left_over", [P, EC // CC, 4])
        lmax = m.sb("left_max", [P, 3])
        lall = m.sb("left_all", [P, 3])
        pf = m.sb("plan_f", [P, 4])
        loaded = [m.sem("loaded0"), m.sem("loaded1")]
        step, keyed, packed, stored, done = m.sem("step"), m.sem("keyed"), m.sem("packed"), m.sem("stored"), m.sem("done")
        listed, left_ready, all_ready = m.sem("listed"), m.sem("left_ready"), m.sem("all_ready")
        block = s.enter_context(nc.Block())

        @block.sync
        def _(sp):
            with sp.Fori(0, EC // CC // 2) as i:
                for b in range(2):
                    n = 2 * i + b
                    sp.wait_ge(keyed, 2 * i + 1)
                    for t in range(2):
                        sp.dma_start(raw[:, b, t], e_v[t, :, bass.ds(n * CC, CC)]).then_inc(loaded[b], 16)
            with sp.Fori(0, EC // CC // 2) as i:
                for b in range(2):
                    n = 2 * i + b
                    sp.wait_ge(keyed, n + 2)
                    sp.dma_start(keys_dram[:, bass.ds(n * CC, CC)], kb[:, b]).then_inc(stored, 16)
                    sp.wait_ge(packed, n + 2)
                    sp.dma_start(keys_dram[:, bass.ds(n * (SEGS * KEEP) + EC, SEGS * KEEP)],
                                 cand[:, b].rearrange("p s k -> p (s k)")).then_inc(stored, 16)
            sp.wait_ge(listed, 2)
            sp.dma_start(keys_dram[:, EC + KEPT:EC + KEPT + LISTED + TURN], lf[:]).then_inc(stored, 16)
            sp.wait_ge(stored, 16 * (2 * EC // CC + 1) + 1)

        @block.gpsimd
        def _(pool):
            pool.wait_ge(left_ready, 2)
            pool.partition_all_reduce(lall[:], lmax[:], P, RMAX).then_inc(all_ready, 1)

        @block.vector
        def _(dve):
            STEPS = 3 + 4 * SEGS + 4 + 4 * 2 + 1
            with dve.Fori(0, EC // CC // 2) as i:
                for b in range(2):
                    n = 2 * i + b
                    base = n * STEPS
                    at = [0]

                    def chain(ins):
                        at[0] += 1
                        ins.then_inc(step, 1)
                        dve.wait_ge(step, base + at[0] + 1)
                        dve.sem_inc(passed, 1)

                    dve.wait_ge(loaded[b], 32 * i + 32 + 1)
                    chain(dve.tensor_scalar(sp1[:], raw[:, b, 0], 4095, 1, ALU.min, ALU.add))
                    chain(dve.scalar_tensor_tensor(kk[:], raw[:, b, 1], 4096.0, sp1[:], ALU.mult, ALU.add))
                    dve.wait_ge(stored, 64 * i + 1)
                    dve.scalar_tensor_tensor(kb[:, b], raw[:, b, 1], 4096.0, kk[:], ALU.is_lt, ALU.mult).then_inc(keyed, 1)
                    dve.wait_ge(keyed, n + 2)
                    chain(dve.tensor_copy(work[:], kb[:, b]))
                    for half in range(2):
                        for g in range(SEGS):
                            ins = dve.max(cand[:, b, g, 8 * half:8 * half + 8], work[:, g * SEG:(g + 1) * SEG])
                            at[0] += 1
                            ins.then_inc(step, 1)
                        dve.wait_ge(step, base + at[0] + 1)
                        dve.sem_inc(passed, 1)
                        for g in range(SEGS):
                            part = work[:, g * SEG:(g + 1) * SEG]
                            ins = dve.match_replace(part, cand[:, b, g, 8 * half:8 * half + 8], part, 0.0)
                            at[0] += 1
                            ins.then_inc(step, 1)
                        dve.wait_ge(step, base + at[0] + 1)
                        dve.sem_inc(passed, 1)
                    flat = cand[:, b].rearrange("p s k -> p (s k)")
                    dve.reduce_max(left[:, bass.ds(n, 1), 0:1].rearrange("p a c -> p (a c)"), work[:], axis=AX.X).then_inc(packed, 1)
                    chain(dve.tensor_scalar(ki[:], flat, 1.0, None, ALU.subtract))
                    chain(dve.tensor_scalar(ksrc[:], ki[:], 4095, None, ALU.bitwise_and))
                    chain(dve.scalar_tensor_tensor(cl[:], ksrc[:], 4095.0, flat, ALU.is_lt, ALU.mult))
                    for h in range(2):
                        part = cl[:, h * 256:(h + 1) * 256]
                        for r in range(2):
                            chain(dve.max(l1[:, h, 8 * r:8 * r + 8], part))
                            chain(dve.match_replace(part, l1[:, h, 8 * r:8 * r + 8], part, 0.0))
                    chain(dve.reduce_max(left[:, bass.ds(n, 1), 1:2].rearrange("p a c -> p (a c)"), cl[:], axis=AX.X))
                    chain(dve.tensor_copy(lc[:, bass.ds(n, 1)].rearrange("p a c -> p (a c)"),
                                          l1[:].rearrange("p h k -> p (h k)")))
                    assert at[0] == STEPS, (at[0], STEPS)
            at = [STEPS * (EC // CC)]

            def chain(ins):
                at[0] += 1
                ins.then_inc(step, 1)
                dve.wait_ge(step, at[0] + 1)

            flat = lc[:].rearrange("p n k -> p (n k)")
            chain(dve.memset(lf[:, LISTED:], 0.0))
            for r in range(LISTED // 8):
                chain(dve.max(lf[:, 8 * r:8 * r + 8], flat))
                ins = dve.match_replace(flat, lf[:, 8 * r:8 * r + 8], flat, 0.0)
                if r == LISTED // 8 - 1:
                    ins.then_inc(listed, 1)
                    dve.wait_ge(listed, 2)
                else:
                    chain(ins)
            chain(dve.tensor_scalar(held[:], lf[:, 0:LISTED], 0.0, None, ALU.is_gt))
            chain(dve.tensor_reduce(lmax[:, 2:3], held[:], AX.X, ALU.add))
            chain(dve.reduce_max(lmax[:, 0:1], left[:, :, 0:1].rearrange("p n o -> p (n o)"), axis=AX.X))
            chain(dve.reduce_max(lmax[:, 1:2], left[:, :, 1:2].rearrange("p n o -> p (n o)"), axis=AX.X))
            chain(dve.reduce_max(pf[:, 0:1], flat, axis=AX.X))
            chain(dve.tensor_tensor(pf[:, 1:2], pf[:, 0:1], lmax[:, 1:2], ALU.max))
            dve.tensor_tensor(lmax[:, 1:2], pf[:, 1:2], lmax[:, 0:1], ALU.max).then_inc(left_ready, 1)
            dve.wait_ge(all_ready, 2)
            chain(dve.tensor_scalar(pf[:, 0:2], lall[:, 0:2], 0.0, None, ALU.is_gt))
            dve.tensor_scalar(plan[:, 0:1], pf[:, 0:1], float(-EC), float(EC), ALU.mult, ALU.add).then_inc(done, 1)
            n_fit, n_all = KEPT // HB // 2, EC // HB // 2
            dve.tensor_scalar(plan[:, 1:2], pf[:, 0:1], float(n_all - n_fit), float(n_fit), ALU.mult, ALU.add).then_inc(done, 1)
            start = float(EC + KEPT)
            dve.tensor_scalar(plan[:, 2:3], pf[:, 1:2], -start, start, ALU.mult, ALU.add).then_inc(done, 1)
            chain(dve.tensor_scalar(turns_i[:, 0:1], lall[:, 2:3], float(2 * TURN - 1), None, ALU.add))
            chain(dve.tensor_scalar(turns_i[:, 1:2], turns_i[:, 0:1], (2 * TURN).bit_length() - 1, None, ALU.arith_shift_right))
            chain(dve.tensor_scalar(turns_f[:], turns_i[:, 1:2], 1.0, None, ALU.max))
            dve.scalar_tensor_tensor(plan[:, 3:4], pf[:, 1:2], float(EC // TURN // 2), turns_f[:], ALU.mult, ALU.max)\
                .then_inc(done, 1)


def clamped_count_stage(nc, keys_dram, plan, clamped, ident):
    with ExitStack() as s:
        m = Memory(nc, s, "count")
        kb = m.sb("keys", [P, 2, HB])
        ki = m.sb("key_int", [P, HB], I32)
        dst = m.sb("dst", [P, HB], I32)
        far = m.sb("src_inner", [P, HB], I32)
        push = m.sb("push_out", [P, HB])
        hi_i = m.sb("hi_int", [P, HB], I32)
        lo_i = m.sb("lo_int", [P, HB], I32)
        hi = m.sb("hi", [P, HB], BF16)
        lo = m.sb("lo", [P, HB], BF16)
        iota_i = m.sb("iota_int", [P, 64], I32)
        iota = m.sb("iota", [P, 64, HB], BF16)
        oh = m.sb("one_hot", [P, 2, 64, HB], BF16)
        zero = m.sb("zeros", [P, 64], BF16)
        cs = m.sb("counts", [64, 64])
        c_ps = m.ps("counts_ps", [64, 64])
        o_ps = m.ps("clamped_ps", [P, NT])
        loaded = [m.sem("loaded0"), m.sem("loaded1")]
        iota_ready, step, split, hot, counted = m.sem("iota_ready"), m.sem("step"), m.sem("split"), m.sem("hot"), m.sem("counted")
        opened, closed, copied, spread = m.sem("opened"), m.sem("closed"), m.sem("copied"), m.sem("spread")
        block = s.enter_context(nc.Block())

        @block.sync
        def _(sp):
            start = sp.value_load(plan[0:1, 0:1], min_val=0, max_val=EC)
            turns = sp.value_load(plan[0:1, 1:2], min_val=KEPT // HB // 2, max_val=EC // HB // 2)
            with sp.Fori(0, turns) as i:
                for b in range(2):
                    sp.wait_ge(split, 2 * i + 1)
                    sp.dma_start(kb[:, b], keys_dram[:, bass.ds(start + (2 * i + b) * HB, HB)]).then_inc(loaded[b], 16)

        @block.gpsimd
        def _(pool):
            pool.iota(iota_i[:], pattern=[[1, 64]], base=0, channel_multiplier=0).then_inc(iota_ready, 1)

        @block.tensor
        def _(pe):
            turns = pe.value_load(plan[0:1, 1:2], min_val=KEPT // HB // 2, max_val=EC // HB // 2)
            pe.wait_ge(iota_ready, 4)
            nc.tensor.matmul(c_ps[:], zero[:], zero[:], start=True, stop=False, skip_group_check=True).then_inc(opened, 1)
            pe.wait_ge(opened, 2)
            with pe.Fori(0, turns) as i:
                for b in range(2):
                    n = 2 * i + b
                    pe.wait_ge(hot, 2 * n + 2 + 1)
                    for c in range(HB):
                        mm = nc.tensor.matmul(c_ps[:], oh[:, 0, :, c], oh[:, 1, :, c], start=False, stop=False,
                                              skip_group_check=True)
                    mm.then_inc(counted, 1)
            nc.tensor.matmul(c_ps[:], zero[:], zero[:], start=False, stop=True, skip_group_check=True).then_inc(closed, 1)
            pe.wait_ge(copied, 2)
            v = cs[:].rearrange("p (t o) -> p t o", o=2)
            for o in range(2):
                mm = nc.tensor.matmul(o_ps[64 * o:64 * o + 64], ident[0:64, 0:64], v[:, :, o], start=True, stop=True,
                                      skip_group_check=True)
            mm.then_inc(spread, 1)

        @block.vector
        def _(dve):
            turns = dve.value_load(plan[0:1, 1:2], min_val=KEPT // HB // 2, max_val=EC // HB // 2)
            dve.memset(zero[:], 0.0).then_inc(iota_ready, 1)
            dve.wait_ge(iota_ready, 3)
            dve.tensor_copy(iota[:], iota_i[:].rearrange("p (v o) -> p v o", o=1).to_broadcast([P, 64, HB])).then_inc(iota_ready, 1)
            dve.wait_ge(iota_ready, 4)
            with dve.Fori(0, turns) as i:
                for b in range(2):
                    n = 2 * i + b
                    at = [0]
                    STEPS = 7

                    def chain(ins):
                        at[0] += 1
                        ins.then_inc(step, 1)
                        dve.wait_ge(step, n * STEPS + at[0] + 1)

                    dve.wait_ge(loaded[b], 16 * i + 16 + 1)
                    dve.tensor_scalar(ki[:], kb[:, b], 1.0, None, ALU.subtract).then_inc(split, 1)
                    dve.wait_ge(split, n + 2)
                    dve.tensor_scalar(dst[:], ki[:], BITS, None, ALU.arith_shift_right).then_inc(step, 1)
                    dve.tensor_scalar(far[:], ki[:], 4095, None, ALU.bitwise_and).then_inc(step, 1)
                    at[0] += 2
                    dve.wait_ge(step, n * STEPS + at[0] + 1)
                    dve.tensor_scalar(push[:], far[:], 4095.0, 64.0, ALU.is_lt, ALU.mult).then_inc(step, 1)
                    dve.tensor_scalar(hi_i[:], dst[:], 6, None, ALU.arith_shift_right).then_inc(step, 1)
                    dve.tensor_scalar(lo_i[:], dst[:], 63, None, ALU.bitwise_and).then_inc(step, 1)
                    at[0] += 3
                    dve.wait_ge(step, n * STEPS + at[0] + 1)
                    dve.tensor_tensor(hi[:], hi_i[:], push[:], ALU.add).then_inc(step, 1)
                    dve.tensor_copy(lo[:], lo_i[:]).then_inc(step, 1)
                    at[0] += 2
                    dve.wait_ge(step, n * STEPS + at[0] + 1)
                    dve.wait_ge(counted, n + 1)
                    for q, v in enumerate((lo, hi)):
                        dve.tensor_tensor(oh[:, q], iota[:], v[:].rearrange("p (o c) -> p o c", o=1).to_broadcast([P, 64, HB]),
                                          ALU.is_equal).then_inc(hot, 1)
            dve.wait_ge(closed, 2)
            dve.tensor_copy(cs[:], c_ps[:]).then_inc(copied, 1)
            dve.wait_ge(spread, 2)
            dve.tensor_copy(clamped[:], o_ps[:]).then_inc(copied, 1)


H4 = 4
NE = 4
G20 = H4 + H4 * NE
BIG = 1e30


def node_features_stage(nc, a, xn, feat, adst, node_dram, ident):
    with ExitStack() as s:
        m = Memory(nc, s, "nodes")
        wg = m.sb("w_gat", [P, KC, 16])
        att = m.sb("att", [P, 2, 16])
        hc = m.sb("h_chunk", [16, 2, CH])
        prod = m.sb("products", [P, NT, 16])
        h_ps = m.ps("h_ps", [16, 2, CH])
        t_ps = m.ps("hT_ps", [P, NT, 16])
        loaded, h_ready, h_done, t_ready = m.sem("loaded"), m.sem("h_ready"), m.sem("h_done"), m.sem("t_ready")
        step, feat_ready, stored = m.sem("step"), m.sem("feat_ready"), m.sem("stored")
        block = s.enter_context(nc.Block())

        @block.sync
        def _(sp):
            sp.dma_start(wg[:], a["wgat"].rearrange("(k p) o -> p k o", p=P)).then_inc(loaded, 16)
            sp.dma_start(att[:, 0], a["att_src"].rearrange("(a n) -> a n", a=1).to_broadcast([P, 16])).then_inc(loaded, 16)
            sp.dma_start(att[:, 1], a["att_dst"].rearrange("(a n) -> a n", a=1).to_broadcast([P, 16])).then_inc(loaded, 16)
            sp.wait_ge(feat_ready, 2)
            sp.dma_start(node_dram.rearrange("(t p) f -> p t f", p=P), feat[:]).then_inc(stored, 16)
            sp.wait_ge(stored, 17)

        @block.tensor
        def _(pe):
            pe.wait_ge(loaded, 49)
            for n in range(NCH):
                b = n % 2
                if n >= 2:
                    pe.wait_ge(h_done, n - 1 + 1)
                for k in range(KC):
                    mm = nc.tensor.matmul(h_ps[:, b], wg[:, k], xn[:, k, n * CH:(n + 1) * CH], start=k == 0, stop=k == KC - 1)
                mm.then_inc(h_ready, 1)
                pe.wait_ge(h_done, n + 2)
                for j in range(4):
                    mm = nc.tensor.transpose(t_ps[:, 4 * n + j], hc[:, b, j * P:(j + 1) * P], ident[0:16, 0:16])
                mm.then_inc(t_ready, 1)

        @block.scalar
        def _(act):
            for n in range(NCH):
                act.wait_ge(h_ready, n + 2)
                if n >= 2:
                    act.wait_ge(t_ready, n - 1 + 1)
                nc.scalar.activation(hc[:, n % 2], h_ps[:, n % 2], ACT.Copy).then_inc(h_done, 1)

        @block.vector
        def _(dve):
            at = [0]

            def chain(ins):
                at[0] += 1
                ins.then_inc(step, 1)
                dve.wait_ge(step, at[0] + 1)

            dve.wait_ge(loaded, 49)
            dve.wait_ge(t_ready, NCH + 1)
            chain(dve.tensor_copy(feat[:, :, H4:G20], t_ps[:]))
            for q in range(2):
                chain(dve.tensor_tensor(prod[:], feat[:, :, H4:G20], att[:, q:q + 1].to_broadcast([P, NT, 16]), ALU.mult))
                dst = feat[:, :, 0:H4] if q == 0 else adst[:]
                chain(dve.reduce_sum(dst, prod[:].rearrange("p t (h e) -> p t h e", h=H4), axis=AX.X))
            dve.tensor_copy(prod[:, 0:1], prod[:, 1:2]).then_inc(feat_ready, 1)


def edge_max_stage(nc, passed, keys_dram, plan, feat, node_dram, shift, table, iota128, iota32, ident):
    NX = TURN * (1 + H4)
    with ExitStack() as s:
        m = Memory(nc, s, "emax")
        kb = m.sb("keys", [P, 2, TURN])
        dec = EdgeNumbers(m)
        av = m.sb("gathered", [P, 2, TURN, G20])
        x = m.sb("columns", [P, NX])
        xT = m.sb("columnsT", [NX, P])
        dbc = m.sb("dst_rows", [P, TURN, P])
        lower = m.sb("lower", [P, P])
        val = m.sb("masked", [P, H4, P])
        first = m.sb("earlier", [P, TURN])
        junk = m.sb("junk", [P, P])
        lead = m.sb("leader", [P, TURN])
        best = m.sb("best", [P, TURN, H4])
        ohlo = m.sb("lo_rows", [P, 2, P])
        rhs = m.sb("hi_rows", [P, 2, NT, H4])
        fneg = m.sb("neg_feat", [P, H4])
        fall = m.sb("neg_all", [P, H4])
        x_ps = m.ps("columnsT_ps", [NX, P])
        d_ps = m.ps("dst_rows_ps", [P, TURN, P])
        a_ps = m.ps("a_rows_ps", [P, 2, H4, P])
        s_ps = m.ps("scatter_ps", [P, 2, CH])
        loaded = [m.sem("loaded0"), m.sem("loaded1")]
        gathered = [m.sem("gathered0", 0), m.sem("gathered1", 0)]
        shift_in, shift_out, ready = m.sem("shift_in"), m.sem("shift_out"), m.sem("ready")
        step, decoded, x_ready, xT_ready, xT_done = (m.sem(q) for q in ("step", "decoded", "x_ready", "xT_ready", "xT_done"))
        d_ready, d_done, a_ready, masked = (m.sem(q) for q in ("d_ready", "d_done", "a_ready", "masked"))
        rows_ready, scattered, merged = m.sem("rows_ready"), m.sem("scattered"), m.sem("merged")
        block = s.enter_context(nc.Block())

        @block.sync
        def _(sp):
            load_keys(sp, keys_dram, plan, kb, loaded, decoded)

        @block.gpsimd
        def _(pool):
            turns = pool.value_load(plan[0:1, 3:4], min_val=1, max_val=EC // TURN // 2)
            pool.memset(lower[:], 1.0).then_inc(ready, 1)
            pool.wait_ge(ready, 2)
            pool.affine_select(out=lower[:], in_=lower[:], compare_op=ALU.is_gt, fill=0.0, base=0,
                               pattern=[[-1, P]], channel_multiplier=1).then_inc(ready, 1)
            pool.wait_ge(ready, 3)
            pool.wait_ge(shift_in, 2)
            pool.partition_all_reduce(fall[:], fneg[:], P, RMAX).then_inc(shift_out, 1)

            def gather(n, b):
                pool.wait_ge(decoded, n + 2)
                pool.sem_inc(passed, 1)
                for c in range(TURN):
                    pool.indirect_dma_start(av[:, b, c], None, node_dram,
                                            bass.IndirectOffsetOnAxis(dec.src[:, b, c:c + 1], 0)).then_inc(gathered[b], 16)

            gather(0, 0)
            with pool.Fori(0, turns) as i:
                for b in range(2):
                    gather(2 * i + b + 1, 1 - b)

        @block.tensor
        def _(pe):
            turns = pe.value_load(plan[0:1, 3:4], min_val=1, max_val=EC // TURN // 2)
            with pe.Fori(0, turns) as i:
                for b in range(2):
                    n = 2 * i + b
                    pe.wait_ge(x_ready, n + 2)
                    pe.wait_ge(xT_done, n + 1)
                    pe.sem_inc(passed, 1)
                    nc.tensor.transpose(x_ps[:], x[:], ident[:]).then_inc(xT_ready, 1)
                    pe.wait_ge(xT_done, n + 2)
                    pe.wait_ge(d_done, 2 * n + 1)
                    for c in range(TURN):
                        mm = nc.tensor.matmul(d_ps[:, c], ident[0:NX, c:c + 1].to_broadcast([NX, P]), xT[:], start=True,
                                              stop=True, skip_group_check=True)
                        if c % (TURN // 2) == TURN // 2 - 1:
                            mm.then_inc(d_ready, 1)
                    for c in range(TURN):
                        pe.wait_ge(masked, TURN * n + max(c - 1, 0) + 1)
                        for h in range(H4):
                            q = TURN + H4 * c + h
                            mm = nc.tensor.matmul(a_ps[:, c % 2, h], ident[0:NX, q:q + 1].to_broadcast([NX, P]), xT[:],
                                                  start=True, stop=True, skip_group_check=True)
                        mm.then_inc(a_ready, 1)
                    for c in range(TURN):
                        pe.wait_ge(rows_ready, TURN * n + c + 2)
                        pe.wait_ge(merged, TURN * n + max(c - 1, 0) + 1)
                        nc.tensor.matmul(s_ps[:, c % 2, 0:NT * H4], ohlo[:, c % 2], rhs[:, c % 2].rearrange("p t h -> p (t h)"),
                                         start=True, stop=True, skip_group_check=True).then_inc(scattered, 1)

        @block.scalar
        def _(act):
            turns = act.value_load(plan[0:1, 3:4], min_val=1, max_val=EC // TURN // 2)
            with act.Fori(0, turns) as i:
                for b in range(2):
                    n = 2 * i + b
                    act.wait_ge(xT_ready, n + 2)
                    act.wait_ge(a_ready, TURN * n + 1)
                    nc.scalar.activation(xT[:], x_ps[:], ACT.Copy).then_inc(xT_done, 1)
                    act.wait_ge(masked, TURN * n + 1)
                    for g in range(2):
                        half = slice(g * TURN // 2, (g + 1) * TURN // 2)
                        act.wait_ge(d_ready, 2 * n + g + 2)
                        nc.scalar.activation(dbc[:, half], d_ps[:, half], ACT.Copy).then_inc(d_done, 1)

        def merge(dve, n, c):
            dve.wait_ge(scattered, TURN * n + c + 2)
            dve.wait_ge(merged, TURN * n + c + 1)
            dve.tensor_tensor(table[:].rearrange("p t h -> p (t h)"), table[:].rearrange("p t h -> p (t h)"),
                              s_ps[:, c % 2, 0:NT * H4], ALU.max).then_inc(merged, 1)

        @block.vector
        def _(dve):
            turns = dve.value_load(plan[0:1, 3:4], min_val=1, max_val=EC // TURN // 2)
            at = [0]

            def chain(ins, base=0):
                at[0] += 1
                ins.then_inc(step, 1)
                dve.wait_ge(step, base + at[0] + 1)

            dve.wait_ge(loaded[0], 17)
            dec.decode(dve, 0, 0, kb[:, 0], step, 0, decoded)
            at[0] = EdgeNumbers.STEPS
            chain(dve.memset(table[:], 0.0))
            chain(dve.tensor_reduce(fneg[:], feat[:, :, 0:H4].rearrange("p t h -> p h t"), AX.X, ALU.min))
            dve.tensor_scalar(fneg[:], fneg[:], -1.0, None, ALU.mult).then_inc(shift_in, 1)
            dve.wait_ge(shift_out, 2)
            chain(dve.tensor_scalar(shift[:], fall[:], 1.0, None, ALU.add))
            dve.wait_ge(ready, 3)
            first_steps = at[0]
            STEPS = EdgeNumbers.STEPS + TURN * 3 + 3
            with dve.Fori(0, turns) as i:
                for b in range(2):
                    n = 2 * i + b
                    base = n * STEPS + first_steps
                    dve.wait_ge(gathered[b], 16 * TURN * (i + 1))
                    dve.wait_ge(xT_ready, n + 1)
                    at[0] = 0
                    chain(dve.tensor_copy(x[:, 0:TURN], dec.dst[:, b]), base)
                    dve.tensor_tensor(x[:, TURN:NX].rearrange("p (c h) -> p c h", c=TURN), av[:, b, :, 0:H4],
                                      shift[:].rearrange("p (o h) -> p o h", o=1).to_broadcast([P, TURN, H4]), ALU.add)\
                        .then_inc(x_ready, 1)
                    dve.wait_ge(x_ready, n + 2)
                    dve.wait_ge(loaded[1 - b], 16 * (i + b) + 16 + 1)
                    dec.decode(dve, 1 - b, n + 1, kb[:, 1 - b], step, base + 1, decoded)
                    at[0] += EdgeNumbers.STEPS
                    for c in range(TURN):
                        d = dec.dst[:, b, c:c + 1]
                        if c % (TURN // 2) == 0:
                            dve.wait_ge(d_done, 2 * n + c // (TURN // 2) + 2)
                        dve.wait_ge(a_ready, TURN * n + c + 2)
                        dve.scalar_tensor_tensor(junk[:], dbc[:, c], d, lower[:], ALU.is_equal, ALU.mult,
                                                 accum_out=first[:, c:c + 1]).then_inc(step, 1)
                        at[0] += 1
                        dve.scalar_tensor_tensor(val[:], dbc[:, c:c + 1].to_broadcast([P, H4, P]), d, a_ps[:, c % 2],
                                                 ALU.is_equal, ALU.mult).then_inc(masked, 1)
                        dve.wait_ge(masked, TURN * n + c + 2)
                        dve.reduce_max(best[:, c], val[:], axis=AX.X).then_inc(step, 1)
                        at[0] += 1
                        dve.wait_ge(step, base + at[0] + 1)
                    chain(dve.tensor_scalar(lead[:], first[:], 0.0, None, ALU.is_equal), base)
                    for c in range(TURN):
                        dve.wait_ge(scattered, TURN * n + max(c - 1, 0) + 1)
                        dve.scalar_tensor_tensor(rhs[:, c % 2], iota32[:].rearrange("p (t o) -> p t o", o=1).to_broadcast([P, NT, H4]),
                                                 dec.hi[:, b, c:c + 1],
                                                 best[:, c:c + 1].to_broadcast([P, NT, H4]), ALU.is_equal, ALU.mult)\
                            .then_inc(step, 1)
                        at[0] += 1
                        dve.tensor_scalar(ohlo[:, c % 2], iota128[:], dec.lo[:, b, c:c + 1], lead[:, c:c + 1],
                                          ALU.is_equal, ALU.mult).then_inc(rows_ready, 1)
                        if c:
                            merge(dve, n, c - 1)
                    merge(dve, n, TURN - 1)
                    chain(dve.tensor_copy(junk[:, 0:1], junk[:, 1:2]), base)
                    assert at[0] == STEPS, (at[0], STEPS)
            dve.wait_ge(gathered[0], 16 * TURN * (turns + 1))
            dve.sem_inc(passed, 1)


def load_keys(sp, keys_dram, plan, kb, loaded, decoded):
    start = sp.value_load(plan[0:1, 2:3], min_val=0, max_val=EC + KEPT)
    turns = sp.value_load(plan[0:1, 3:4], min_val=1, max_val=EC // TURN // 2)
    sp.dma_start(kb[:, 0], keys_dram[:, bass.ds(start, TURN)]).then_inc(loaded[0], 16)
    with sp.Fori(0, turns) as i:
        for b in range(2):
            n = 2 * i + b
            sp.wait_ge(decoded, n + 1)
            sp.dma_start(kb[:, 1 - b], keys_dram[:, bass.ds(start + (n + 1) * TURN, TURN)]).then_inc(loaded[1 - b], 16)


class EdgeNumbers:
    STEPS = 9

    def __init__(self, m):
        self.ki = m.sb("key_int", [P, TURN], I32)
        self.di = m.sb("dst_int", [P, TURN], I32)
        self.out = m.sb("not_listed", [P, TURN])
        self.li = m.sb("lo_int", [P, TURN], I32)
        self.dg = m.sb("dst_row", [P, 2, TURN], I32)
        self.src = m.sb("src", [P, 2, TURN], I32)
        self.dst = m.sb("dst", [P, 2, TURN])
        self.lo = m.sb("lo", [P, 2, TURN])
        self.hi = m.sb("hi", [P, 2, TURN])

    def decode(self, dve, b, n, keys, step, base, decoded):
        k = 0

        def then(ins):
            nonlocal k
            k += 1
            ins.then_inc(step, 1)

        def fence():
            dve.wait_ge(step, base + k + 1)

        fence()
        then(dve.tensor_scalar(self.ki[:], keys, 1.0, None, ALU.subtract))
        fence()
        then(dve.tensor_scalar(self.di[:], self.ki[:], BITS, None, ALU.arith_shift_right))
        then(dve.tensor_scalar(self.src[:, b], self.ki[:], 4095, None, ALU.bitwise_and))
        fence()
        then(dve.tensor_scalar(self.out[:], self.src[:, b], 4095.0, -8192.0, ALU.is_equal, ALU.mult))
        then(dve.tensor_scalar(self.li[:], self.di[:], 127, None, ALU.bitwise_and))
        fence()
        then(dve.tensor_tensor(self.dst[:, b], self.di[:], self.out[:], ALU.add))
        then(dve.tensor_copy(self.lo[:, b], self.li[:]))
        fence()
        then(dve.tensor_tensor(self.hi[:, b], self.dst[:, b], self.lo[:, b], ALU.subtract))
        fence()
        then(dve.tensor_scalar(self.hi[:, b], self.hi[:, b], 1.0 / P, None, ALU.mult))
        fence()
        assert k == self.STEPS
        dve.tensor_scalar(self.dg[:, b], self.dst[:, b], 0.0, None, ALU.max).then_inc(decoded, 1)
        dve.wait_ge(decoded, n + 2)


def node_max_stage(nc, feat, adst, shift, table, clamped, last, mx, max_dram, ident):
    with ExitStack() as s:
        m = Memory(nc, s, "nmax")
        l_ps = m.ps("last_ps", [P, G20])
        top = m.sb("top", [P, NT, H4])
        alt = m.sb("alt", [P, NT, H4])
        lsh = m.sb("last_shifted", [P, H4])
        has = m.sb("has_clamped", [P, NT])
        last_ready, step, mx_ready, stored = m.sem("last_ready"), m.sem("step"), m.sem("mx_ready"), m.sem("stored")
        block = s.enter_context(nc.Block())

        @block.tensor
        def _(pe):
            nc.tensor.matmul(l_ps[:], ident[:, P - 1:P].to_broadcast([P, P]), feat[:, NT - 1], start=True, stop=True)\
                .then_inc(last_ready, 1)

        @block.sync
        def _(sp):
            sp.wait_ge(mx_ready, 2)
            sp.dma_start(max_dram.rearrange("(t p) f -> p t f", p=P), mx[:]).then_inc(stored, 16)
            sp.wait_ge(stored, 17)

        @block.vector
        def _(dve):
            at = [0]

            def chain(ins):
                at[0] += 1
                ins.then_inc(step, 1)
                dve.wait_ge(step, at[0] + 1)

            sh = shift[:].rearrange("p (o h) -> p o h", o=1).to_broadcast([P, NT, H4])
            chain(dve.tensor_tensor(top[:], feat[:, :, 0:H4], sh, ALU.add))
            chain(dve.tensor_tensor(top[:], top[:], table[:], ALU.max))
            dve.wait_ge(last_ready, 2)
            chain(dve.tensor_copy(last[:], l_ps[:]))
            chain(dve.tensor_tensor(lsh[:], last[:, 0:H4], shift[:], ALU.add))
            chain(dve.tensor_scalar(has[:], clamped[:], 0.0, None, ALU.is_gt))
            chain(dve.tensor_tensor(alt[:], has[:].rearrange("p (t o) -> p t o", o=1).to_broadcast([P, NT, H4]),
                                    lsh[:].rearrange("p (o h) -> p o h", o=1).to_broadcast([P, NT, H4]), ALU.mult))
            chain(dve.tensor_tensor(top[:], top[:], alt[:], ALU.max))
            chain(dve.tensor_tensor(top[:], top[:], sh, ALU.subtract))
            chain(dve.tensor_tensor(top[:], top[:], adst[:], ALU.add))
            chain(dve.tensor_scalar(alt[:], top[:], 0.2, None, ALU.mult))
            chain(dve.tensor_copy(mx[:, :, 0:H4], adst[:]))
            dve.tensor_tensor(mx[:, :, H4:2 * H4], top[:], alt[:], ALU.max).then_inc(mx_ready, 1)


def edge_sum_stage(nc, passed, keys_dram, plan, node_dram, max_dram, sums, iota128, iota32):
    W5 = 1 + NE
    with ExitStack() as s:
        m = Memory(nc, s, "esum")
        kb = m.sb("keys", [P, 2, TURN])
        dec = EdgeNumbers(m)
        av = m.sb("src_rows", [P, 2, TURN, G20])
        dv = m.sb("dst_rows", [P, 2, TURN, 2 * H4])
        z = m.sb("z", [P, TURN, H4])
        z2 = m.sb("z2", [P, TURN, H4])
        ee = m.sb("exp", [P, 2, TURN, H4])
        msg = m.sb("messages", [P, 2, TURN, H4, W5])
        ohlo = m.sb("lo_rows", [P, 2, P])
        rhs = m.sb("hi_rows", [P, 2, NT, H4 * W5])
        zero = m.sb("zeros", [P, NT // 2 * H4 * W5])
        s_ps = m.ps("sums_ps", [P, 2, CH])
        HALF = NT // 2 * H4 * W5
        loaded = [m.sem("loaded0"), m.sem("loaded1")]
        gathered = [m.sem("gathered0", 0), m.sem("gathered1", 0)]
        step, decoded, x_ready, e_ready, msg_ready = (m.sem(q) for q in ("step", "decoded", "x_ready", "e_ready", "msg_ready"))
        rows_ready, summed, ready, opened, closed = (m.sem(q) for q in ("rows_ready", "summed", "ready", "opened", "closed"))
        block = s.enter_context(nc.Block())

        @block.sync
        def _(sp):
            load_keys(sp, keys_dram, plan, kb, loaded, decoded)

        @block.gpsimd
        def _(pool):
            turns = pool.value_load(plan[0:1, 3:4], min_val=1, max_val=EC // TURN // 2)

            def gather(n, b):
                pool.wait_ge(decoded, n + 2)
                pool.sem_inc(passed, 1)
                for c in range(TURN):
                    pool.indirect_dma_start(av[:, b, c], None, node_dram,
                                            bass.IndirectOffsetOnAxis(dec.src[:, b, c:c + 1], 0)).then_inc(gathered[b], 16)
                    pool.indirect_dma_start(dv[:, b, c], None, max_dram,
                                            bass.IndirectOffsetOnAxis(dec.dg[:, b, c:c + 1], 0)).then_inc(gathered[b], 16)

            gather(0, 0)
            with pool.Fori(0, turns) as i:
                for b in range(2):
                    gather(2 * i + b + 1, 1 - b)

        @block.tensor
        def _(pe):
            turns = pe.value_load(plan[0:1, 3:4], min_val=1, max_val=EC // TURN // 2)
            pe.wait_ge(ready, 2)
            for h in range(2):
                mm = nc.tensor.matmul(s_ps[:, h, 0:HALF], zero[:, 0:P], zero[:], start=True, stop=False, skip_group_check=True)
            mm.then_inc(opened, 1)
            pe.wait_ge(opened, 2)
            with pe.Fori(0, turns) as i:
                for b in range(2):
                    n = 2 * i + b
                    for c in range(TURN):
                        pe.wait_ge(rows_ready, TURN * n + c + 2)
                        for h in range(2):
                            mm = nc.tensor.matmul(s_ps[:, h, 0:HALF], ohlo[:, c % 2],
                                                  rhs[:, c % 2, h * NT // 2:(h + 1) * NT // 2].rearrange("p t f -> p (t f)"),
                                                  start=False, stop=False, skip_group_check=True)
                        mm.then_inc(summed, 1)
            for h in range(2):
                mm = nc.tensor.matmul(s_ps[:, h, 0:HALF], zero[:, 0:P], zero[:], start=False, stop=True, skip_group_check=True)
            mm.then_inc(closed, 1)

        @block.scalar
        def _(act):
            turns = act.value_load(plan[0:1, 3:4], min_val=1, max_val=EC // TURN // 2)
            with act.Fori(0, turns) as i:
                for b in range(2):
                    n = 2 * i + b
                    act.wait_ge(x_ready, n + 2)
                    act.wait_ge(msg_ready, 2 * i + 1)
                    nc.scalar.activation(ee[:, b], z[:], ACT.Exp).then_inc(e_ready, 1)

        @block.vector
        def _(dve):
            turns = dve.value_load(plan[0:1, 3:4], min_val=1, max_val=EC // TURN // 2)
            dve.memset(zero[:], 0.0).then_inc(ready, 1)
            dve.wait_ge(loaded[0], 17)
            dec.decode(dve, 0, 0, kb[:, 0], step, 0, decoded)
            STEPS = 5 + EdgeNumbers.STEPS + TURN
            with dve.Fori(0, turns) as i:
                for b in range(2):
                    n = 2 * i + b
                    at = [0]
                    base = EdgeNumbers.STEPS + n * STEPS

                    def chain(ins):
                        at[0] += 1
                        ins.then_inc(step, 1)
                        dve.wait_ge(step, base + at[0] + 1)

                    dve.wait_ge(gathered[b], 32 * TURN * (i + 1))
                    dve.wait_ge(e_ready, n + 1)
                    chain(dve.tensor_tensor(z[:], av[:, b, :, 0:H4], dv[:, b, :, 0:H4], ALU.add))
                    chain(dve.tensor_scalar(z2[:], z[:], 0.2, None, ALU.mult))
                    chain(dve.tensor_tensor(z[:], z[:], z2[:], ALU.max))
                    chain(dve.tensor_tensor(z[:], z[:], dv[:, b, :, H4:2 * H4], ALU.subtract))
                    dve.tensor_scalar(z[:], z[:], 0.0, None, ALU.min).then_inc(x_ready, 1)
                    dve.wait_ge(loaded[1 - b], 16 * (i + b) + 16 + 1)
                    dve.wait_ge(summed, TURN * n + 1)
                    dec.decode(dve, 1 - b, n + 1, kb[:, 1 - b], step, base + at[0], decoded)
                    at[0] += EdgeNumbers.STEPS
                    dve.wait_ge(e_ready, n + 2)
                    chain(dve.tensor_copy(msg[:, b, :, :, 0:1].rearrange("p c h o -> p c (h o)"), ee[:, b]))
                    dve.tensor_tensor(msg[:, b, :, :, 1:W5], av[:, b, :, H4:G20].rearrange("p c (h e) -> p c h e", h=H4),
                                      ee[:, b].rearrange("p c (h o) -> p c h o", o=1).to_broadcast([P, TURN, H4, NE]), ALU.mult)\
                        .then_inc(msg_ready, 1)
                    dve.wait_ge(msg_ready, n + 2)
                    for c in range(TURN):
                        dve.wait_ge(summed, TURN * n + max(c - 1, 0) + 1)
                        chain(dve.tensor_scalar(ohlo[:, c % 2], iota128[:], dec.lo[:, b, c:c + 1], None, ALU.is_equal))
                        dve.scalar_tensor_tensor(
                            rhs[:, c % 2], iota32[:].rearrange("p (t o) -> p t o", o=1).to_broadcast([P, NT, H4 * W5]),
                            dec.hi[:, b, c:c + 1],
                            msg[:, b, c:c + 1].rearrange("p o h f -> p o (h f)").to_broadcast([P, NT, H4 * W5]),
                            ALU.is_equal, ALU.mult).then_inc(rows_ready, 1)
                    assert at[0] == STEPS, (at[0], STEPS)
            dve.wait_ge(gathered[0], 32 * TURN * (turns + 1))
            dve.sem_inc(passed, 1)
            dve.wait_ge(closed, 2)
            for h in range(2):
                ins = dve.tensor_copy(sums[:, h * NT // 2:(h + 1) * NT // 2].rearrange("p t h f -> p (t h f)"), s_ps[:, h, 0:HALF])
            ins.then_inc(step, 1)


def gate_stage(nc, a, feat, mx, clamped, last, sums, gates, gT, ident):
    W5 = 1 + NE
    with ExitStack() as s:
        m = Memory(nc, s, "gates")
        par = m.sb("params", [P, 3, 16])
        z = m.sb("z", [P, 2, NT, H4])
        z2 = m.sb("z2", [P, 2, NT, H4])
        ee = m.sb("exp", [P, 2, NT, H4])
        tmp = m.sb("tmp", [P, NT, H4, NE])
        agg = m.sb("agg", [P, NT, H4, NE])
        one = m.sb("per_node", [P, 6, NT])
        eps = m.sb("eps", [P, 1])
        sc = m.sb("scores", [P, NT, NE])
        rank = m.sb("rank", [P, NE, NT])
        beat = m.sb("beats", [P, NT])
        t_ps = m.ps("gT_ps", [NE, 2, 4, P])
        loaded, step, z_ready, e_ready = m.sem("loaded"), m.sem("step"), m.sem("z_ready"), m.sem("e_ready")
        var_ready, sd_ready, sc_ready, sm_ready = (m.sem(q) for q in ("var_ready", "sd_ready", "sc_ready", "sm_ready"))
        gates_ready, t_ready, t_done = m.sem("gates_ready"), m.sem("t_ready"), m.sem("t_done")
        block = s.enter_context(nc.Block())

        @block.sync
        def _(sp):
            for q, name in enumerate(("b_gat", "ln_gamma", "ln_beta")):
                sp.dma_start(par[:, q], a[name].rearrange("(a n) -> a n", a=1).to_broadcast([P, 16])).then_inc(loaded, 16)

        @block.scalar
        def _(act):
            act.wait_ge(z_ready, 2)
            nc.scalar.activation(ee[:], z[:], ACT.Exp).then_inc(e_ready, 1)
            act.wait_ge(var_ready, 2)
            nc.scalar.activation(one[:, 2], one[:, 1], ACT.Sqrt, bias=eps[:], scale=1.0 / 16).then_inc(sd_ready, 1)
            act.wait_ge(sc_ready, 2)
            nc.scalar.activation(sc[:], sc[:], ACT.Exp).then_inc(sm_ready, 1)

        @block.tensor
        def _(pe):
            pe.wait_ge(gates_ready, 2)
            for n in range(NCH):
                if n >= 2:
                    pe.wait_ge(t_done, n - 1 + 1)
                for j in range(4):
                    mm = nc.tensor.transpose(t_ps[:, n % 2, j], gates[:, 4 * n + j], ident[:])
                mm.then_inc(t_ready, 1)

        @block.vector
        def _(dve):
            at = [0]

            def chain(ins):
                at[0] += 1
                ins.then_inc(step, 1)
                dve.wait_ge(step, at[0] + 1)

            def wide(v, *shape):
                return v.rearrange("p (t o) -> p t o", o=1).to_broadcast([P, NT, *shape])

            chain(dve.memset(eps[:], 1e-5))
            chain(dve.tensor_tensor(z[:, 0], feat[:, :, 0:H4], mx[:, :, 0:H4], ALU.add))
            chain(dve.tensor_tensor(z[:, 1], last[:, 0:H4].rearrange("p (o h) -> p o h", o=1).to_broadcast([P, NT, H4]),
                                    mx[:, :, 0:H4], ALU.add))
            chain(dve.tensor_scalar(z2[:], z[:], 0.2, None, ALU.mult))
            chain(dve.tensor_tensor(z[:], z[:], z2[:], ALU.max))
            for q in range(2):
                chain(dve.tensor_tensor(z[:, q], z[:, q], mx[:, :, H4:2 * H4], ALU.subtract))
            dve.tensor_scalar(z[:], z[:], 0.0, None, ALU.min).then_inc(z_ready, 1)
            dve.wait_ge(e_ready, 2)
            chain(dve.tensor_tensor(ee[:, 1], ee[:, 1], wide(clamped[:], H4), ALU.mult))
            for q, h in enumerate((feat[:, :, H4:G20].rearrange("p t (h e) -> p t h e", h=H4),
                                   last[:, H4:G20].rearrange("p (o h e) -> p o h e", o=1, h=H4).to_broadcast([P, NT, H4, NE]))):
                chain(dve.tensor_tensor(tmp[:], h, ee[:, q].rearrange("p t (h o) -> p t h o", o=1).to_broadcast([P, NT, H4, NE]), ALU.mult))
                chain(dve.tensor_tensor(agg[:], tmp[:], sums[:, :, :, 1:W5] if q == 0 else agg[:], ALU.add))
            den = sums[:, :, :, 0:1].rearrange("p t h o -> p t (h o)")
            chain(dve.tensor_tensor(z[:, 0], ee[:, 0], den, ALU.add))
            chain(dve.tensor_tensor(z[:, 0], z[:, 0], ee[:, 1], ALU.add))
            chain(dve.tensor_scalar(z[:, 0], z[:, 0], 1e-16, None, ALU.add))
            chain(dve.reciprocal(z[:, 1], z[:, 0]))
            chain(dve.tensor_tensor(agg[:], agg[:], z[:, 1].rearrange("p t (h o) -> p t h o", o=1).to_broadcast([P, NT, H4, NE]), ALU.mult))
            a16 = agg[:].rearrange("p t h e -> p t (h e)")
            t16 = tmp[:].rearrange("p t h e -> p t (h e)")
            dve.wait_ge(loaded, 49)
            chain(dve.tensor_tensor(a16, a16, par[:, 0:1].to_broadcast([P, NT, 16]), ALU.add))
            chain(dve.reduce_sum(one[:, 0], a16, axis=AX.X))
            chain(dve.tensor_scalar(one[:, 0], one[:, 0], 1.0 / 16, None, ALU.mult))
            chain(dve.tensor_tensor(a16, a16, wide(one[:, 0], 16), ALU.subtract))
            chain(dve.tensor_tensor(t16, a16, a16, ALU.mult))
            dve.reduce_sum(one[:, 1], t16, axis=AX.X).then_inc(var_ready, 1)
            dve.wait_ge(sd_ready, 2)
            chain(dve.reciprocal(one[:, 3], one[:, 2]))
            chain(dve.tensor_tensor(a16, a16, wide(one[:, 3], 16), ALU.mult))
            chain(dve.tensor_tensor(a16, a16, par[:, 1:2].to_broadcast([P, NT, 16]), ALU.mult))
            chain(dve.tensor_tensor(a16, a16, par[:, 2:3].to_broadcast([P, NT, 16]), ALU.add))
            chain(dve.reduce_sum(sc[:], agg[:].rearrange("p t h e -> p t e h"), axis=AX.X))
            chain(dve.tensor_scalar(sc[:], sc[:], 1.0 / H4, None, ALU.mult))
            chain(dve.memset(rank[:], 0.0))
            for i in range(NE):
                for j in range(i + 1, NE):
                    chain(dve.tensor_tensor(beat[:], sc[:, :, i], sc[:, :, j], ALU.is_ge))
                    chain(dve.tensor_tensor(rank[:, j], rank[:, j], beat[:], ALU.add))
                    chain(dve.tensor_scalar(beat[:], beat[:], -1.0, 1.0, ALU.mult, ALU.add))
                    chain(dve.tensor_tensor(rank[:, i], rank[:, i], beat[:], ALU.add))
            chain(dve.tensor_scalar(rank[:], rank[:], 2.0, None, ALU.is_lt))
            chain(dve.reduce_max(one[:, 4], sc[:], axis=AX.X))
            dve.tensor_tensor(sc[:], sc[:], wide(one[:, 4], NE), ALU.subtract).then_inc(sc_ready, 1)
            dve.wait_ge(sm_ready, 2)
            chain(dve.tensor_tensor(sc[:], sc[:], rank[:].rearrange("p e t -> p t e"), ALU.mult))
            chain(dve.reduce_sum(one[:, 5], sc[:], axis=AX.X))
            chain(dve.reciprocal(one[:, 0], one[:, 5]))
            dve.tensor_tensor(gates[:], sc[:], wide(one[:, 0], NE), ALU.mult).then_inc(gates_ready, 1)
            for n in range(NCH):
                dve.wait_ge(t_ready, n + 2)
                dve.tensor_copy(gT[:, n * CH:(n + 1) * CH], t_ps[:, n % 2].rearrange("p j c -> p (j c)")).then_inc(t_done, 1)


def gated_expert_stage(nc, passed, a, xn, gT, res, out, ident):
    F = 512
    KF = F // P
    with ExitStack() as s:
        m = Memory(nc, s, "moe")
        w1 = m.sb("w1_sb", [P, NE, KC, F])
        w2 = m.sb("w2_sb", [P, NE, KF, C])
        b1 = m.sb("b1_sb", [P, NE, KF])
        b2 = m.sb("b2_sb", [NE, C])
        hid = m.sb("hidden", [P, 2, CH])
        gh = m.sb("gated_hidden", [P, 4, CH])
        gb = m.sb("gate_rows", [P, 2, CH])
        h_ps = m.ps("hidden_ps", [P, 2, CH])
        g_ps = m.ps("gate_ps", [P, CH])
        y_ps = m.ps("y_ps", [P, 2, KC, CH])
        loaded, g_ready, g_done = m.sem("loaded"), m.sem("g_ready"), m.sem("g_done")
        h_ready, h_done, gated, y_ready = m.sem("h_ready"), m.sem("h_done"), m.sem("gated"), m.sem("y_ready")
        added, stored = m.sem("added"), m.sem("stored")
        o_v = out.rearrange("(k p) n -> p k n", p=P)
        block = s.enter_context(nc.Block())
        Q = NE * KF

        @block.sync
        def _(sp):
            sp.dma_start(w1[:], a["ew1"].rearrange("e (k p) f -> p e k f", p=P)).then_inc(loaded, 16)
            sp.dma_start(w2[:], a["ew2"].rearrange("e (k p) d -> p e k d", p=P)).then_inc(loaded, 16)
            sp.dma_start(b1[:].rearrange("p e k -> p (e k)"), a["eb1"]).then_inc(loaded, 16)
            sp.dma_start(b2[:], a["eb2"]).then_inc(loaded, 16)
            with sp.Fori(0, NCH) as n:
                sp.wait_ge(added, n + 2)
                sp.dma_start(o_v[:, :, bass.ds(n * CH, CH)], res[:, :, bass.ds(n * CH, CH)]).then_inc(stored, 16)
            sp.wait_ge(stored, 16 * NCH + 1)

        @block.tensor
        def _(pe):
            pe.wait_ge(loaded, 65)
            with pe.Fori(0, NCH // 2) as i:
                for b in range(2):
                    n = 2 * i + b
                    cols = bass.ds(n * CH, CH)

                    def out_tile(q):
                        pe.wait_ge(gated, Q * n + q + 2)
                        for o in range(KC):
                            mm = nc.tensor.matmul(y_ps[:, b, o], w2[:, q // KF, q % KF, o * P:(o + 1) * P], gh[:, q % 4],
                                                  start=False, stop=q == Q - 1)
                        mm.then_inc(y_ready, 1)

                    for q in range(Q):
                        e = q // KF
                        if q % KF == 0:
                            pe.wait_ge(g_done, NE * n + e + 1)
                            pe.sem_inc(passed, 1)
                            nc.tensor.matmul(g_ps[:], ident[0:NE, e:e + 1].to_broadcast([NE, P]), gT[:, cols],
                                             start=True, stop=True).then_inc(g_ready, 1)
                        pe.wait_ge(h_done, Q * n + max(q - 1, 0) + 1)
                        for k in range(KC):
                            mm = nc.tensor.matmul(h_ps[:, q % 2], w1[:, e, k, (q % KF) * P:(q % KF + 1) * P],
                                                  xn[:, k, cols], start=k == 0, stop=k == KC - 1)
                        mm.then_inc(h_ready, 1)
                        if q == 2:
                            pe.wait_ge(added, 2 * i + 1)
                            pe.sem_inc(passed, 1)
                            for o in range(KC):
                                nc.tensor.matmul(y_ps[:, b, o], b2[:, o * P:(o + 1) * P], gT[:, cols], start=True, stop=False)
                        if q >= 2:
                            out_tile(q - 2)
                    out_tile(Q - 2)
                    out_tile(Q - 1)

        @block.scalar
        def _(act):
            act.wait_ge(loaded, 65)
            with act.Fori(0, NCH) as n:
                for q in range(Q):
                    if q % KF == 0:
                        e = q // KF
                        act.wait_ge(g_ready, NE * n + e + 2)
                        act.wait_ge(gated, Q * n + max(q - KF, 0) + 1)
                        nc.scalar.activation(gb[:, e % 2], g_ps[:], ACT.Copy).then_inc(g_done, 1)
                    act.wait_ge(h_ready, Q * n + q + 2)
                    act.wait_ge(gated, Q * n + max(q - 1, 0) + 1)
                    nc.scalar.activation(hid[:, q % 2], h_ps[:, q % 2], ACT.Gelu,
                                         bias=b1[:, q // KF, q % KF:q % KF + 1]).then_inc(h_done, 1)

        @block.vector
        def _(dve):
            with dve.Fori(0, NCH // 2) as i:
                for b in range(2):
                    n = 2 * i + b
                    for q in range(Q):
                        e = q // KF
                        dve.wait_ge(g_done, NE * n + e + 2)
                        dve.wait_ge(h_done, Q * n + q + 2)
                        dve.wait_ge(y_ready, Q * n + max(q - 3, 0) + 1)
                        dve.tensor_tensor(gh[:, q % 4], hid[:, q % 2], gb[:, e % 2], ALU.mult).then_inc(gated, 1)
                    dve.wait_ge(y_ready, Q * n + Q + 1)
                    c = res[:, :, bass.ds(n * CH, CH)]
                    dve.tensor_tensor(c, c, y_ps[:, b], ALU.add).then_inc(added, 1)


def program(nc, a, out, stop=None):
    with ExitStack() as s:
        m = Memory(nc, s, "program")
        passed = nc.alloc_semaphore(name="passed")
        Memory.spent = []
        ones_mean = m.sb("ones_mean", [P, P])
        block_ones = m.sb("block_ones", [P, P])
        ident = m.sb("ident", [P, P])
        stack_ident = m.sb("stack_ident", [P, DH])
        den_pick = m.sb("den_pick", [P, 1])
        col_sum = m.sb("col_sum", [P, KC])
        top_w = m.sb("top_w", [P, 2])
        top_i = m.sb("top_i", [1, 8], mybir.dt.uint32)
        qk_dram = nc.dram_tensor("qk_scratch", [4, 2, P, N], F16, kind="Internal").ap()
        v_dram = nc.dram_tensor("v_scratch", [HEADS, P, NT * DH], F32, kind="Internal").ap()
        iota128 = m.sb("iota128", [P, P])
        iota32 = m.sb("iota32", [P, NT])
        plan = m.sb("plan", [P, 4], I32)
        clamped = m.sb("clamped", [P, NT])
        keys_dram = nc.dram_tensor("keys_scratch", [P, 2 * EC + KEPT + TURN], F32, kind="Internal").ap()
        node_dram = nc.dram_tensor("node_scratch", [N, G20], F32, kind="Internal").ap()
        max_dram = nc.dram_tensor("max_scratch", [N, 2 * H4], F32, kind="Internal").ap()
        fill_constants(nc, ones_mean, block_ones, ident, stack_ident, den_pick)
        iotas(nc, iota128, iota32)
        edge_keys_stage(nc, passed, a["edges"], keys_dram, plan)
        clamped_count_stage(nc, keys_dram, plan, clamped, ident)
        if stop != "skip":
            qkv_stage(nc, a["x"], a["wqkvT"], a["temp"], qk_dram, v_dram, ones_mean, block_ones)
        res = m.sb("residual", [P, KC, N])
        with nc.sbuf_tensor("attn", [P, KC, 16, C], F32) as attn:
            if stop != "skip":
                attention_stage(nc, passed, a["temp"], qk_dram, v_dram, attn, stack_ident, den_pick)
            else:
                load(nc, attn, a["attn"])
            projection_stage(nc, a["x"], a["wprojT"], attn, res)
        with nc.sbuf_tensor("normed", [P, KC, N], F32) as xn:
            layer_norm_stage(nc, "ln_ffn", res, xn, 1e-5, ones_mean, col_sum)
            routing_stage(nc, a, col_sum, top_w, top_i)
            with nc.sbuf_tensor("expert_sum", [P, KC, N], F32) as z:
                expert_stage(nc, a, xn, top_w, top_i, z)
                layer_norm_stage(nc, "ln_out", z, z, 1e-5, ones_mean)
                affine_residual_stage(nc, a, z, res)
        with nc.sbuf_tensor("h_padded", [P, PW * PW], F32) as hpad, \
                nc.sbuf_tensor("h_transposed", [P, NT + 2, P], F32) as hT, \
                nc.sbuf_tensor("gate", [P, N], F32) as gate:
            with nc.sbuf_tensor("conv_normed", [P, KC, N], F32) as cn:
                layer_norm_stage(nc, "ln_conv", res, cn, 1e-6, ones_mean)
                conv_in_stage(nc, a, cn, hpad, hT, gate, ident)
            conv_out_stage(nc, a, hpad, hT, gate, res, ident)
        Memory.clear_semaphores(nc)
        with nc.sbuf_tensor("graph_normed", [P, KC, N], F32) as xn, ExitStack() as gs:
            g = Memory(nc, gs, "graph")
            layer_norm_stage(nc, "ln_graph", res, xn, 1e-5, ones_mean)
            feat = g.sb("feat", [P, NT, G20])
            adst = g.sb("adst", [P, NT, H4])
            shift = g.sb("shift", [P, H4])
            table = g.sb("table", [P, NT, H4])
            last = g.sb("last", [P, G20])
            mx = g.sb("mx", [P, NT, 2 * H4])
            sums = g.sb("sums", [P, NT, H4, 1 + NE])
            gates = g.sb("gates", [P, NT, NE])
            gT = g.sb("gT", [NE, N])
            node_features_stage(nc, a, xn, feat, adst, node_dram, ident)
            edge_max_stage(nc, passed, keys_dram, plan, feat, node_dram, shift, table, iota128, iota32, ident)
            node_max_stage(nc, feat, adst, shift, table, clamped, last, mx, max_dram, ident)
            edge_sum_stage(nc, passed, keys_dram, plan, node_dram, max_dram, sums, iota128, iota32)
            gate_stage(nc, a, feat, mx, clamped, last, sums, gates, gT, ident)
            gated_expert_stage(nc, passed, a, xn, gT, res, out, ident)


def iotas(nc, iota128, iota32):
    with ExitStack() as s:
        m = Memory(nc, s, "iotas")
        i128 = m.sb("i128", [P, P], I32)
        made, copied = m.sem("made"), m.sem("copied")
        block = s.enter_context(nc.Block())

        @block.gpsimd
        def _(pool):
            pool.iota(i128[:], pattern=[[1, P]], base=0, channel_multiplier=0).then_inc(made, 1)

        @block.vector
        def _(dve):
            dve.wait_ge(made, 2)
            dve.tensor_copy(iota128[:], i128[:]).then_inc(copied, 1)
            dve.tensor_copy(iota32[:], i128[:, 0:NT]).then_inc(copied, 1)


def load(nc, dst, src):
    with ExitStack() as s:
        sem = Memory(nc, s, "load").sem("load_sem")
        block = s.enter_context(nc.Block())

        @block.sync
        def _(sp):
            sp.dma_start(dst[:], src).then_inc(sem, 16)
            sp.wait_ge(sem, 17)


def store(nc, out, src):
    with ExitStack() as s:
        stored = Memory(nc, s, "store").sem("stored")
        block = s.enter_context(nc.Block())

        @block.sync
        def _(sp):
            sp.dma_start(out.rearrange("(k p) n -> p k n", p=P), src).then_inc(stored, 16)
            sp.wait_ge(stored, 17)


def layout(z):
    import numpy as np

    def cols(v, per):
        return np.ascontiguousarray(v.reshape(-1, per, P).transpose(2, 0, 1).reshape(P, -1))

    T = lambda v: np.ascontiguousarray(v.T)
    return {
        "x": np.ascontiguousarray(z["x"].reshape(C, N)),
        "wqkvT": T(z["L0_conv_w_qkv"]), "wprojT": T(z["L0_conv_w_proj"]),
        "temp": np.ascontiguousarray(z["L0_conv_temperature"].reshape(HEADS)),
        "wr": z["L0_ffn_Wr"], "br": z["L0_ffn_br"], "w1": z["L0_ffn_W1"], "w2": z["L0_ffn_W2"],
        "b1": cols(z["L0_ffn_b1"], 4), "b2": cols(z["L0_ffn_b2"], 2),
        "gamma": cols(z["L0_ffn_gamma"], 2), "beta": cols(z["L0_ffn_beta"], 2),
        "cw1T": T(z["L1_conv_W1"]), "cb1": cols(z["L1_conv_b1"], 1),
        "cw2T": T(z["L1_conv_W2"]), "cb2": cols(z["L1_conv_b2"], 1),
        "wgat": z["L1_ffn_W_gat"], "att_src": z["L1_ffn_att_src"].reshape(16), "att_dst": z["L1_ffn_att_dst"].reshape(16),
        "b_gat": z["L1_ffn_b_gat"], "ln_gamma": z["L1_ffn_ln_gamma"], "ln_beta": z["L1_ffn_ln_beta"],
        "ew1": z["L1_ffn_W1"], "ew2": z["L1_ffn_W2"], "eb1": cols(z["L1_ffn_b1"], 4), "eb2": z["L1_ffn_b2"],
        "edges": z["L1_ffn_edge_index"],
        "cwoT": T(z["L1_conv_Wout"]), "cbo": cols(z["L1_conv_bout"], 2),
    }


def kernel(**inputs):
    import numpy as np
    import concourse.bacc as bacc
    from concourse.bass_utils import run_bass_kernel_spmd

    nc = bacc.Bacc("TRN2", target_bir_lowering=False, num_devices=1)
    arrays = {f"in_{k}": np.ascontiguousarray(v) for k, v in layout({k: np.asarray(v) for k, v in inputs.items()}).items()}
    aps = {k[3:]: nc.dram_tensor(k, v.shape, mybir.dt.from_np(v.dtype), kind="ExternalInput").ap()
           for k, v in arrays.items()}
    out = nc.dram_tensor("out_dram", [C, N], F32, kind="ExternalOutput").ap()
    program(nc, aps, out)
    r = run_bass_kernel_spmd(nc, [arrays], core_ids=[0])
    return r.results[0]["out_dram"].reshape(1, C, 64, 64)
```

```python
import concourse.bass as bass
from concourse import mybir
from contextlib import ExitStack

F32 = mybir.dt.float32
F16 = mybir.dt.float16
I32 = mybir.dt.int32
BF16 = mybir.dt.bfloat16
RMAX = bass.bass_isa.ReduceOp.max
ALU = mybir.AluOpType
ACT = mybir.ActivationFunctionType
AX = mybir.AxisListType

P = 128
C = 256
KC = C // P
N = 4096
CH = 512
NCH = N // CH
NT = N // P
HEADS = 8
DH = C // HEADS
QS, KS = 16.0, 1024.0


class Memory:

    spent = []

    def __init__(self, nc, stack, stage):
        self.nc, self.stack, self.stage = nc, stack, stage

    def sb(self, name, shape, dt=F32):
        return self.stack.enter_context(self.nc.sbuf_tensor(f"{self.stage}_{name}", shape, dt))

    def ps(self, name, shape, dt=F32):
        return self.stack.enter_context(self.nc.psum_tensor(f"{self.stage}_{name}", shape, dt))

    def sem(self, name, start=1):
        sem = self.nc.alloc_semaphore(name=f"{self.stage}_{name}")
        if start:
            self.nc.sync.sem_inc(sem, start)
        self.spent.append(sem)
        return sem

    @classmethod
    def clear_semaphores(cls, nc):
        nc.all_engine_barrier()
        nc.clear_and_free_semaphores(cls.spent)
        nc.all_engine_barrier()
        cls.spent = []


def fill_constants(nc, ones_mean, block_ones, ident, stack_ident):
    with ExitStack() as s:
        filled = Memory(nc, s, "fill_constants").sem("const_filled")
        block = s.enter_context(nc.Block())

        @block.gpsimd
        def _(pool):
            pool.memset(ones_mean[:], 1.0 / C).then_inc(filled, 1)
            pool.memset(block_ones[:], 1.0).then_inc(filled, 1)
            pool.memset(ident[:], 0.0).then_inc(filled, 1)
            pool.memset(stack_ident[:], 0.0).then_inc(filled, 1)
            pool.wait_ge(filled, 5)
            v = block_ones[:].rearrange("p (g j) -> p g j", g=4)
            pool.affine_select(out=v, in_=v, compare_op=ALU.is_ge, fill=0.0, base=0,
                               pattern=[[-32, 4], [0, 32]], channel_multiplier=1).then_inc(filled, 1)
            pool.wait_ge(filled, 6)
            pool.affine_select(out=v, in_=v, compare_op=ALU.is_ge, fill=0.0, base=31,
                               pattern=[[32, 4], [0, 32]], channel_multiplier=-1).then_inc(filled, 1)
            pool.affine_select(out=ident[:], in_=ident[:], compare_op=ALU.not_equal, fill=1.0, base=0,
                               pattern=[[-1, P]], channel_multiplier=1).then_inc(filled, 1)
            for j in range(4):
                pool.affine_select(out=stack_ident[:], in_=stack_ident[:], compare_op=ALU.not_equal, fill=1.0,
                                   base=-32 * j, pattern=[[-1, DH]], channel_multiplier=1).then_inc(filled, 1)
                pool.wait_ge(filled, 9 + j)


def qkv_stage(nc, x, wqkvT, temp, qk_dram, v_dram, ones_mean, block_ones, ident):
    x_v = x.rearrange("(k p) n -> p k n", p=P)
    w_v = wqkvT.rearrange("(k p) o -> p k o", p=P)
    TILES = CH // P
    GH = P // DH
    with ExitStack() as s:
        m = Memory(nc, s, "qkv")
        w = m.sb("wqkv_sb", [P, KC, 3 * C])
        xin = m.sb("x_in", [P, 2, KC, CH])
        xc = m.sb("x_centred", [P, 2, KC, CH])
        sq = m.sb("x_squared", [P, KC, CH])
        rstd = m.sb("x_rstd", [P, TILES])
        sd = m.sb("x_deviation", [P, TILES])
        eps = m.sb("ln_eps", [P, 1])
        norm = m.sb("qk_norm", [P, 2, TILES, GH])
        nm = m.sb("qk_norm_floored", [P, TILES, GH])
        raw = m.sb("qk_raw", [P, 4, CH])
        qsq = m.sb("qk_squared", [P, 2, CH])
        rn = m.sb("qk_rnorm", [P, TILES, GH])
        rs = m.sb("qk_rnorm_scaled", [P, TILES, GH])
        rx = m.sb("qk_rnorm_by_channel", [P, 2, TILES, P])
        qn = m.sb("qk_unit", [P, 2, CH])
        tb = m.sb("temp_all", [P, HEADS])
        scale = m.sb("qk_scale", [P, 4, GH])
        parts = m.sb("qk_parts", [P, 4, 2, N], F16)
        v_sb = m.sb("v_sb", [P, HEADS, NT, DH])
        mean_ps = m.ps("mean_ps", [P, CH])
        var_ps = m.ps("var_ps", [P, CH])
        qk_ps = m.ps("qk_ps", [P, 2, CH])
        n2_ps = m.ps("n2_ps", [P, CH])
        u_ps = m.ps("rnorm_ps", [P, CH])
        r_ps = m.ps("rstd_ps", [P, CH])
        v_ps = m.ps("v_ps", [P, 2, C])
        w_loaded, t_loaded = m.sem("w_loaded"), m.sem("t_loaded")
        x_loaded = [m.sem("x_loaded0"), m.sem("x_loaded1")]
        scale_ready = m.sem("scale_ready")
        eps_ready, sd_ready = m.sem("eps_ready"), m.sem("sd_ready")
        norm_ready, floored = m.sem("norm_ready", start=2), m.sem("floored", start=2)
        mean_ready, centred, squared = m.sem("mean_ready"), m.sem("centred"), m.sem("squared")
        var_ready, rstd_ready, normed = m.sem("var_ready"), m.sem("rstd_ready"), m.sem("normed")
        raw_ready, rstd_spread = m.sem("raw_ready", start=2), m.sem("rstd_spread")
        rs_ready, scaled, rn_spread = m.sem("rs_ready"), m.sem("scaled", start=2), m.sem("rn_spread", start=2)
        qk_ready, qk_squared, n2_ready = m.sem("qk_ready"), m.sem("qk_squared"), m.sem("n2_ready", start=2)
        rn_ready, unit_ready = m.sem("rn_ready"), m.sem("unit_ready", start=4)
        high_ready, low_ready = m.sem("high_ready"), m.sem("low_ready", start=2)
        v_ready, v_copied, stored = m.sem("v_ready"), m.sem("v_copied"), m.sem("stored")
        block = s.enter_context(nc.Block())

        @block.sync
        def _(sp):
            sp.dma_start(w[:], w_v).then_inc(w_loaded, 16)
            sp.dma_start(tb[:], temp.rearrange("(a h) -> a h", a=1).to_broadcast([P, HEADS])).then_inc(t_loaded, 16)

            def load_x(n):
                sp.dma_start(xin[:, n % 2], x_v[:, :, n * CH:(n + 1) * CH]).then_inc(x_loaded[n % 2], 16)

            def store_kv(n):
                sp.wait_ge(high_ready, 4 * n + 4 + 1)
                sp.wait_ge(low_ready, 4 * n + 4 + 2)
                cols = slice(n * CH, (n + 1) * CH)
                for g in range(2, 4):
                    for part in range(2):
                        sp.dma_start(qk_dram[g, part, :, cols], parts[:, g, part, cols]).then_inc(stored, 16)
                sp.wait_ge(v_copied, 2 * n + 2 + 1)
                sp.dma_start(v_dram[:, :, n * 4 * DH:(n + 1) * 4 * DH].rearrange("h p c -> p h c"),
                             v_sb[:, :, 4 * n:4 * n + 4, :].rearrange("p h t d -> p h (t d)")).then_inc(stored, 16)

            for n in range(2):
                load_x(n)
            for n in range(NCH):
                if n + 2 < NCH:
                    sp.wait_ge(centred, n + 2)
                    load_x(n + 2)
                if n >= 1:
                    store_kv(n - 1)
            store_kv(NCH - 1)
            for g in range(2):
                for part in range(2):
                    sp.dma_start(qk_dram[g, part], parts[:, g, part]).then_inc(stored, 16)
            sp.wait_ge(stored, 16 * (5 * NCH + 4) + 1)

        @block.tensor
        def _(pe):
            head_ones = block_ones[:].rearrange("p (h d) -> p h d", h=GH)[:, :, 0:1].rearrange("p h o -> p (h o)")

            def mean(n, b, i):
                pe.wait_ge(x_loaded[b], 16 * i + 16 + 1)
                pe.wait_ge(centred, n + 1)
                for k in range(KC):
                    mm = nc.tensor.matmul(mean_ps[:], ones_mean[:], xin[:, b, k], start=k == 0, stop=k == KC - 1)
                mm.then_inc(mean_ready, 1)

            def variance(n):
                pe.wait_ge(squared, n + 2)
                pe.wait_ge(sd_ready, n + 1)
                for t in range(TILES):
                    for k in range(KC):
                        mm = nc.tensor.matmul(var_ps[:, t:t + 1], sq[:, k, t * P:(t + 1) * P], ones_mean[:, 0:1],
                                              start=k == 0, stop=k == KC - 1, skip_group_check=True)
                mm.then_inc(var_ready, 1)

            def spread_rstd(n):
                pe.wait_ge(rstd_ready, n + 2)
                pe.wait_ge(normed, n + 1)
                for t in range(TILES):
                    mm = nc.tensor.matmul(r_ps[:, t * P:(t + 1) * P], rstd[:, t:t + 1].to_broadcast([P, P]), ident[:],
                                          start=True, stop=True, skip_group_check=True)
                mm.then_inc(rstd_spread, 1)

            def product(n, b, g):
                pe.wait_ge(raw_ready, 4 * n + g + 1)
                for k in range(KC):
                    mm = nc.tensor.matmul(qk_ps[:, g % 2], w[:, k, g * P:(g + 1) * P], xc[:, b, k],
                                          start=k == 0, stop=k == KC - 1)
                mm.then_inc(qk_ready, 1)

            def norm2(n, g):
                pe.wait_ge(qk_squared, 4 * n + g + 2)
                pe.wait_ge(norm_ready, 4 * n + g + 2)
                for t in range(TILES):
                    mm = nc.tensor.matmul(n2_ps[:, t * GH:(t + 1) * GH], qsq[:, g % 2, t * P:(t + 1) * P], head_ones,
                                          start=True, stop=True, skip_group_check=True)
                mm.then_inc(n2_ready, 1)

            def spread(n, g):
                pe.wait_ge(scaled, 4 * n + g + 3)
                pe.wait_ge(unit_ready, 4 * n + g + 4)
                for t in range(TILES):
                    mm = nc.tensor.matmul(u_ps[:, t * P:(t + 1) * P], rx[:, g % 2, t], ident[:],
                                          start=True, stop=True, skip_group_check=True)
                mm.then_inc(rn_spread, 1)

            def values(n, b, half):
                pe.wait_ge(v_copied, 2 * n + half + 1)
                for j in range(2):
                    t = 2 * half + j
                    for k in range(KC):
                        mm = nc.tensor.matmul(v_ps[:, j], xc[:, b, k, t * P:(t + 1) * P],
                                              w[:, k, 2 * C:3 * C], start=k == 0, stop=k == KC - 1)
                mm.then_inc(v_ready, 1)

            def chunk(n, b, i, following, first=False):
                pe.wait_ge(normed, n + 2)
                product(n, b, 0)
                if not first:
                    spread(n - 1, 3)
                if following:
                    mean(n + 1, 1 - b, i + b)
                product(n, b, 1)
                values(n, b, 0)
                norm2(n, 0)
                product(n, b, 2)
                norm2(n, 1)
                spread(n, 0)
                if following:
                    variance(n + 1)
                product(n, b, 3)
                norm2(n, 2)
                spread(n, 1)
                values(n, b, 1)
                if following:
                    spread_rstd(n + 1)
                norm2(n, 3)
                spread(n, 2)

            pe.wait_ge(w_loaded, 17)
            mean(0, 0, 0)
            variance(0)
            spread_rstd(0)
            chunk(0, 0, 0, True, first=True)
            with pe.Fori(0, NCH // 2 - 1) as i:
                chunk(2 * i + 1, 1, i, True)
                chunk(2 * i + 2, 0, i + 1, True)
            chunk(NCH - 1, 1, NCH // 2 - 1, False)
            spread(NCH - 1, 3)

        def part_of(g, part, n):
            if g >= 2:
                return parts[:, g, part, bass.ds(n * CH, CH)]
            return parts[:, g, part].rearrange("p (r c) -> p c r", r=16)[:, bass.ds(n * 32, 32), :]

        def unit_of(g):
            return qn[:, g % 2] if g >= 2 else qn[:, g % 2].rearrange("p (c r) -> p c r", r=16)

        @block.gpsimd
        def _(pool):
            def square_x(n, b):
                pool.wait_ge(centred, n + 2)
                pool.wait_ge(var_ready, n + 1)
                pool.tensor_tensor(sq[:], xc[:, b], xc[:, b], ALU.mult).then_inc(squared, 1)

            def square(n, g):
                pool.wait_ge(raw_ready, 4 * n + g + 3)
                pool.wait_ge(n2_ready, 4 * n + g + 1)
                pool.tensor_tensor(qsq[:, g % 2], raw[:, g], raw[:, g], ALU.mult).then_inc(qk_squared, 1)

            def chunk(n, b, following):
                square(n, 0)
                square(n, 1)
                if following:
                    square_x(n + 1, 1 - b)
                square(n, 2)
                square(n, 3)

            square_x(0, 0)
            with pool.Fori(0, NCH // 2 - 1) as i:
                for b in range(2):
                    chunk(2 * i + b, b, True)
            for b in range(2):
                chunk(NCH - 2 + b, b, b == 0)

        @block.scalar
        def _(act):
            def deviation(n):
                act.wait_ge(var_ready, n + 2)
                act.wait_ge(rstd_ready, n + 1)
                nc.scalar.activation(sd[:], var_ps[:, 0:TILES], ACT.Sqrt, bias=eps[:]).then_inc(sd_ready, 1)

            def length(n, g):
                act.wait_ge(n2_ready, 4 * n + g + 3)
                act.wait_ge(floored, 4 * n + g + 1)
                nc.scalar.activation(norm[:, g % 2].rearrange("p t h -> p (t h)"), n2_ps[:, 0:TILES * GH], ACT.Sqrt)\
                    .then_inc(norm_ready, 1)

            def high(n, g):
                act.wait_ge(unit_ready, 4 * n + g + 5)
                nc.scalar.activation(part_of(g, 0, n), unit_of(g), ACT.Copy).then_inc(high_ready, 1)

            def copy_values(n, half):
                act.wait_ge(v_ready, 2 * n + half + 2)
                for j in range(2):
                    a = nc.scalar.activation(
                        v_sb[:, :, bass.ds(4 * n + 2 * half + j, 1), :].rearrange("p h o d -> p (h o) d"),
                        v_ps[:, j].rearrange("p (h d) -> p h d", h=HEADS), ACT.Copy)
                a.then_inc(v_copied, 1)

            def copy_raw(n, g):
                act.wait_ge(qk_ready, 4 * n + g + 2)
                act.wait_ge(unit_ready, 4 * n + g + 1)
                nc.scalar.activation(raw[:, g], qk_ps[:, g % 2], ACT.Copy).then_inc(raw_ready, 1)

            def chunk(n, following, first=False):
                copy_raw(n, 0)
                if not first:
                    high(n - 1, 3)
                copy_raw(n, 1)
                copy_values(n, 0)
                length(n, 0)
                length(n, 1)
                copy_raw(n, 2)
                high(n, 0)
                if following:
                    deviation(n + 1)
                copy_raw(n, 3)
                high(n, 1)
                length(n, 2)
                copy_values(n, 1)
                length(n, 3)
                high(n, 2)

            act.wait_ge(eps_ready, 2)
            deviation(0)
            chunk(0, True, first=True)
            with act.Fori(0, NCH // 2 - 1) as i:
                for o in range(2):
                    chunk(2 * i + 1 + o, True)
            chunk(NCH - 1, False)
            high(NCH - 1, 3)

        @block.vector
        def _(dve):
            def centre(n, b):
                dve.wait_ge(mean_ready, n + 2)
                for k in range(KC):
                    d = dve.tensor_tensor(xc[:, b, k], xin[:, b, k], mean_ps[:], ALU.subtract)
                d.then_inc(centred, 1)

            def invert(n):
                dve.wait_ge(sd_ready, n + 2)
                dve.wait_ge(rstd_spread, n + 1)
                dve.reciprocal(rstd[:], sd[:]).then_inc(rstd_ready, 1)

            def normalise(n, b):
                dve.wait_ge(rstd_spread, n + 2)
                dve.wait_ge(squared, n + 2)
                for k in range(KC):
                    d = dve.tensor_tensor(xc[:, b, k], xc[:, b, k], r_ps[:], ALU.mult)
                d.then_inc(normed, 1)

            def rnorm(n, g):
                dve.wait_ge(norm_ready, 4 * n + g + 3)
                dve.tensor_scalar(nm[:], norm[:, g % 2], 1e-12, None, ALU.max).then_inc(floored, 1)
                dve.wait_ge(floored, 4 * n + g + 3)
                dve.reciprocal(rn[:], nm[:]).then_inc(rn_ready, 1)
                dve.wait_ge(rn_ready, 4 * n + g + 2)
                dve.tensor_tensor(rs[:], rn[:], scale[:, g:g + 1].to_broadcast([P, TILES, GH]), ALU.mult)\
                    .then_inc(rs_ready, 1)
                dve.wait_ge(rs_ready, 4 * n + g + 2)
                dve.wait_ge(rn_spread, 4 * n + g + 1)
                dve.tensor_copy(rx[:, g % 2].rearrange("p t (h d) -> p (t h) d", h=GH),
                                rs[:].rearrange("p t (h o) -> p (t h) o", o=1).to_broadcast([P, TILES * GH, DH]))\
                    .then_inc(scaled, 1)

            def unit(n, g):
                dve.wait_ge(rn_spread, 4 * n + g + 3)
                dve.wait_ge(low_ready, 4 * n + g + 1)
                dve.tensor_tensor(qn[:, g % 2], raw[:, g], u_ps[:], ALU.mult).then_inc(unit_ready, 1)

            def low(n, g):
                dve.wait_ge(high_ready, 4 * n + g + 2)
                dve.wait_ge(unit_ready, 4 * n + g + 5)
                dve.tensor_tensor(part_of(g, 1, n), unit_of(g), part_of(g, 0, n), ALU.subtract)\
                    .then_inc(low_ready, 1)

            def chunk(n, b, following):
                if following:
                    dve.wait_ge(v_ready, 2 * n + 1)
                    centre(n + 1, 1 - b)
                rnorm(n, 0)
                rnorm(n, 1)
                unit(n, 0)
                if following:
                    invert(n + 1)
                unit(n, 1)
                low(n, 0)
                rnorm(n, 2)
                low(n, 1)
                if following:
                    normalise(n + 1, 1 - b)
                rnorm(n, 3)
                unit(n, 2)
                unit(n, 3)
                low(n, 2)
                low(n, 3)

            dve.memset(eps[:], 1e-6).then_inc(eps_ready, 1)
            dve.wait_ge(t_loaded, 17)
            dve.tensor_scalar(scale[:, 0:2].rearrange("p g h -> p (g h)"), tb[:], QS, None, ALU.mult).then_inc(scale_ready, 1)
            dve.memset(scale[:, 2:4], KS).then_inc(scale_ready, 1)
            dve.wait_ge(scale_ready, 3)
            centre(0, 0)
            invert(0)
            normalise(0, 0)
            with dve.Fori(0, NCH // 2 - 1) as i:
                for b in range(2):
                    chunk(2 * i + b, b, True)
            for b in range(2):
                chunk(NCH - 2 + b, b, b == 0)


def attention_stage(nc, passed, temp, qk_dram, v_dram, attn, stack_ident):
    PAIRS = NT // 2
    QUADS = NT // 4
    OCTS = NT // 8
    AHEAD = 3
    PLACE = [u % 3 for u in range(PAIRS - 1)] + [1]
    AGO = [next(d for d in range(1, PAIRS) if PLACE[(u - d) % PAIRS] == PLACE[u]) for u in range(PAIRS)]
    with ExitStack() as s:
        m = Memory(nc, s, "attention")
        qst = m.sb("q_stack", [P, 2, N], F16)
        kst = m.sb("k_stack", [P, 2, N], F16)
        vb = m.sb("v_head", [P, 2, NT, DH])
        tb = m.sb("temp_all", [P, HEADS])
        nbias = m.sb("neg_bound", [P, HEADS])
        tneg = m.sb("temp_neg", [P, HEADS])
        probs = m.sb("probs", [P, 4, 4, CH])
        half = m.sb("half_sums", [P, 2, 2, CH])
        quad = m.sb("quad_sums", [P, 2, CH])
        octs = m.sb("oct_sums", [P, 2, OCTS, CH])
        sum2 = m.sb("two_sums", [P, OCTS // 2, CH])
        dsum = m.sb("den_by_partition", [P, CH])
        oc = m.sb("o_copy", [P, CH])
        rden = m.sb("rden", [P, 4, 1])
        ones = m.sb("ones", [P, 1])
        s_ps = m.ps("s_ps", [P, 3, 2, CH])
        o_ps = m.ps("o_ps", [P, CH])
        t_ps = m.ps("t_ps", [P, 4, DH + 1])
        stacks_loaded = [m.sem("stacks_loaded0"), m.sem("stacks_loaded1")]
        temp_loaded, bias_ready, tneg_ready = m.sem("temp_loaded"), m.sem("bias_ready"), m.sem("tneg_ready")
        s_ready, exp_done, pv_done = m.sem("s_ready"), m.sem("exp_done", start=4), m.sem("pv_done", start=4)
        half_done, quad_done, oct_done = m.sem("half_done", start=4), m.sem("quad_done", start=2), m.sem("oct_done")
        octs_used, den_done = m.sem("octs_used", start=2), m.sem("den_done")
        o_copied, t_ready, attn_done, rden_done = m.sem("o_copied"), m.sem("t_ready"), m.sem("attn_done"), m.sem("rden_done")
        block = s.enter_context(nc.Block())

        @block.sync
        def _(sp):
            sp.dma_start(tb[:], temp.rearrange("(a h) -> a h", a=1).to_broadcast([P, HEADS])).then_inc(temp_loaded, 16)
            for h in range(HEADS):
                b, g, r = h % 2, h // 4, 32 * (h % 4)
                if h >= 2:
                    sp.wait_ge(o_copied, (h - 1) * NCH + 1)
                for j in range(4):
                    rows = slice(32 * j, 32 * j + 32)
                    sp.dma_start(qst[rows, b], qk_dram[g, j // 2, r:r + 32]).then_inc(stacks_loaded[b], 16)
                    sp.dma_start(kst[rows, b], qk_dram[2 + g, j % 2, r:r + 32]).then_inc(stacks_loaded[b], 16)
                sp.dma_start(vb[:, b].rearrange("p t d -> p (t d)"), v_dram[h]).then_inc(stacks_loaded[b], 16)

        @block.tensor
        def _(pe):
            def scores(G, u, b, column):
                pe.wait_ge(exp_done, G * PAIRS + u - AGO[u] + 5)
                for j in range(2):
                    t = 2 * u + j
                    mm = nc.tensor.matmul(s_ps[:, PLACE[u], j], kst[:, b, t * P:(t + 1) * P],
                                          qst[:, b, column], start=True, stop=True)
                mm.then_inc(s_ready, 1)

            def values(G, w, b):
                pe.wait_ge(exp_done, G * PAIRS + 2 * w + 6)
                if w == 0:
                    pe.wait_ge(o_copied, G + 1)
                for j in range(4):
                    mm = nc.tensor.matmul(o_ps[32 * j:32 * j + 32], vb[:, b, 4 * w + j], probs[:, w % 4, j],
                                          start=w == 0, stop=w == QUADS - 1, skip_group_check=True)
                mm.then_inc(pv_done, 1)

            def turn(G, blk):
                if blk == 0:
                    pe.wait_ge(o_copied, G + 2)
                    pe.wait_ge(den_done, G + 2)
                    pe.wait_ge(attn_done, G + 1)
                cols = slice(blk * P, (blk + 1) * P)
                nc.tensor.matmul(t_ps[:, blk, 0:DH], oc[:, cols], stack_ident[:], start=True, stop=True,
                                 skip_group_check=True)
                mm = nc.tensor.matmul(t_ps[:, blk, DH:DH + 1], dsum[:, cols], ones[:], start=True,
                                      stop=True, skip_group_check=True)
                if blk == 3:
                    mm.then_inc(t_ready, 1)

            def group(G, b, column, following, first=False):
                for u in range(AHEAD, PAIRS):
                    scores(G, u, b, column)
                    if u % 2:
                        values(G, (u - 3) // 2, b)
                    if u in (8, 10, 12, 14) and not first:
                        turn(G - 1, u // 2 - 4)
                if following is not None:
                    for u in range(AHEAD - 1):
                        scores(G + 1, u, *following)
                values(G, QUADS - 1, b)
                if following is not None:
                    scores(G + 1, AHEAD - 1, *following)

            def after_first(hp, b, last):
                for qc in range(1, NCH - 1):
                    group((2 * hp + b) * NCH + qc, b, slice(qc * CH, qc * CH + CH),
                          (b, slice(qc * CH + CH, qc * CH + 2 * CH)))
                G = (2 * hp + b + 1) * NCH
                if last:
                    group(G - 1, b, slice(N - CH, N), None)
                    return
                pe.wait_ge(stacks_loaded[1 - b], 16 * 9 * (hp + b + 1) + 1)
                pe.sem_inc(passed, 1)
                group(G - 1, b, slice(N - CH, N), (1 - b, slice(0, CH)))
                group(G, 1 - b, slice(0, CH), (1 - b, slice(CH, 2 * CH)))

            pe.wait_ge(bias_ready, 3)
            pe.wait_ge(stacks_loaded[0], 16 * 9 + 1)
            for u in range(AHEAD):
                scores(0, u, 0, slice(0, CH))
            group(0, 0, slice(0, CH), (0, slice(CH, 2 * CH)), first=True)
            with pe.Fori(0, HEADS // 2 - 1) as hp:
                for b in range(2):
                    after_first(hp, b, False)
            for b in range(2):
                after_first(HEADS // 2 - 1, b, b == 1)
            for blk in range(4):
                turn(HEADS * NCH - 1, blk)

        @block.scalar
        def _(act):
            act.wait_ge(bias_ready, 3)
            with act.Fori(0, HEADS) as h:
                for qc in range(NCH):
                    G = h * NCH + qc
                    for u in range(PAIRS):
                        w = u // 2
                        act.wait_ge(s_ready, G * PAIRS + u + 2)
                        if u % 2 == 0:
                            act.wait_ge(pv_done, G * QUADS + w + 1)
                            act.wait_ge(half_done, G * QUADS + w + 1)
                        act.sem_inc(passed, 1)
                        nc.scalar.activation(probs[:, w % 4, 2 * (u % 2):2 * (u % 2) + 2], s_ps[:, PLACE[u]], ACT.Exp,
                                             bias=nbias[:, bass.ds(h, 1)], scale=1.0 / (QS * KS)).then_inc(exp_done, 1)

        @block.gpsimd
        def _(pool):
            with pool.Fori(0, HEADS) as h:
                for qc, w in [(qc, w) for qc in range(NCH) for w in range(QUADS)]:
                    G = h * NCH + qc
                    pool.wait_ge(half_done, G * QUADS + w + 5)
                    pool.wait_ge(oct_done, G * OCTS + w // 2 + 1)
                    pool.tensor_tensor(quad[:, w % 2], half[:, w % 2, 0], half[:, w % 2, 1], ALU.add).then_inc(quad_done, 1)
                    if w % 2:
                        pool.wait_ge(quad_done, G * QUADS + w + 3)
                        pool.wait_ge(octs_used, G + 1)
                        pool.tensor_tensor(octs[:, qc % 2, w // 2], quad[:, 0], quad[:, 1], ALU.add).then_inc(oct_done, 1)

        @block.vector
        def _(dve):
            dve.memset(ones[:], 1.0).then_inc(bias_ready, 1)
            dve.wait_ge(temp_loaded, 17)
            dve.tensor_scalar(tneg[:], tb[:], -1.0, None, ALU.mult).then_inc(tneg_ready, 1)
            dve.wait_ge(tneg_ready, 2)
            dve.tensor_tensor(nbias[:], tb[:], tneg[:], ALU.min).then_inc(bias_ready, 1)

            def halves(G, w):
                dve.wait_ge(exp_done, G * PAIRS + 2 * w + 6)
                dve.wait_ge(quad_done, G * QUADS + w + 1)
                dve.tensor_tensor(half[:, w % 2], probs[:, w % 4, 0:2], probs[:, w % 4, 2:4], ALU.add)\
                    .then_inc(half_done, 1)

            def copy_o(G):
                dve.wait_ge(t_ready, G + 1)
                dve.wait_ge(pv_done, (G + 1) * QUADS + 4)
                dve.tensor_copy(oc[:], o_ps[:]).then_inc(o_copied, 1)

            def add_octs(G, parity):
                dve.wait_ge(oct_done, (G + 1) * OCTS + 1)
                dve.tensor_tensor(sum2[:], octs[:, parity, 0:2], octs[:, parity, 2:4], ALU.add).then_inc(octs_used, 1)
                dve.wait_ge(octs_used, G + 3)
                dve.wait_ge(t_ready, G + 1)
                dve.tensor_tensor(dsum[:], sum2[:, 0], sum2[:, 1], ALU.add).then_inc(den_done, 1)

            def divide(G, h, qc):
                dve.wait_ge(t_ready, G + 2)
                dve.reciprocal(rden[:], t_ps[:, :, DH:DH + 1]).then_inc(rden_done, 1)
                dve.wait_ge(rden_done, G + 2)
                dst = attn[:].rearrange("p k r (h d) -> p r k h d", h=HEADS)[:, 2 * qc:2 * qc + 2, :, bass.ds(h, 1), :]\
                    .rearrange("p r k o d -> p r k (o d)")
                dve.tensor_tensor(dst, t_ps[:, :, 0:DH].rearrange("p (r k) d -> p r k d", r=2),
                                  rden[:].rearrange("p (r k) o -> p r k o", r=2).to_broadcast([P, 2, KC, DH]),
                                  ALU.mult).then_inc(attn_done, 1)

            def group(G, h, qc):
                copy_o(G - 1)
                for w in range(QUADS):
                    halves(G, w)
                    if w == 1:
                        add_octs(G - 1, qc % 2)
                divide(G - 1, h, qc)

            def after_first(h):
                for qc in range(NCH - 1):
                    group(h * NCH + qc + 1, h, qc)

            for w in range(QUADS):
                halves(0, w)
            with dve.Fori(0, HEADS - 1) as h:
                after_first(h)
                group((h + 1) * NCH, h, NCH - 1)
            after_first(HEADS - 1)
            copy_o(HEADS * NCH - 1)
            add_octs(HEADS * NCH - 1, 1)
            divide(HEADS * NCH - 1, HEADS - 1, NCH - 1)


def projection_stage(nc, x, wprojT, attn, res):
    with ExitStack() as s:
        m = Memory(nc, s, "projection")
        w = m.sb("wproj_sb", [P, KC, C])
        o_ps = m.ps("proj_ps", [P, 2, KC, CH])
        w_loaded, x_loaded = m.sem("w_loaded"), m.sem("x_loaded")
        projected, added = m.sem("projected"), m.sem("added")
        block = s.enter_context(nc.Block())

        @block.sync
        def _(sp):
            sp.dma_start(w[:], wprojT.rearrange("(k p) o -> p k o", p=P)).then_inc(w_loaded, 16)
            sp.dma_start(res[:], x.rearrange("(k p) n -> p k n", p=P)).then_inc(x_loaded, 16)

        @block.tensor
        def _(pe):
            pe.wait_ge(w_loaded, 17)
            with pe.Fori(0, NCH // 2) as i:
                for b in range(2):
                    n = 2 * i + b
                    pe.wait_ge(added, 2 * i + 1)
                    for o in range(KC):
                        for k in range(KC):
                            mm = nc.tensor.matmul(o_ps[:, b, o], w[:, k, o * P:(o + 1) * P],
                                                  attn[:, k, bass.ds(2 * n, 2), :].rearrange("p r c -> p (r c)"),
                                                  start=k == 0, stop=k == KC - 1)
                    mm.then_inc(projected, 1)

        @block.vector
        def _(dve):
            dve.wait_ge(x_loaded, 17)
            with dve.Fori(0, NCH // 2) as i:
                for b in range(2):
                    n = 2 * i + b
                    dve.wait_ge(projected, n + 2)
                    chunk = res[:, :, bass.ds(n * CH, CH)]
                    dve.tensor_tensor(chunk, chunk, o_ps[:, b], ALU.add).then_inc(added, 1)


def layer_norm_stage(nc, name, src, dst, eps_value, ones_mean, ident, col_sum=None, affine=None):
    TILES = CH // P
    with ExitStack() as s:
        m = Memory(nc, s, name)
        eps = m.sb("ln_eps", [P, 1])
        xc = m.sb("x_centred", [P, 4, KC, CH])
        sq = m.sb("x_squared", [P, 2, KC, CH])
        sd = m.sb("x_deviation", [P, 2, TILES])
        rstd = m.sb("x_rstd", [P, 2, TILES])
        sums = m.sb("chunk_sums", [P, KC, NCH])
        gb = m.sb("gamma_beta", [P, 2, KC])
        scaled = m.sb("x_scaled", [P, 2, KC, CH])
        mean_ps = m.ps("mean_ps", [P, 2, CH])
        var_ps = m.ps("var_ps", [P, 2, CH])
        r_ps = m.ps("rstd_ps", [P, 2, CH])
        eps_ready, mean_ready, centred, squared, var_ready, sd_ready, rstd_ready, spread, normed, loaded, scaled_ready = (
            m.sem(q, 0) for q in ("eps_ready", "mean_ready", "centred", "squared", "var_ready", "sd_ready", "rstd_ready",
                                  "spread", "normed", "loaded", "scaled_ready"))
        block = s.enter_context(nc.Block())

        if affine is not None:
            @block.sync
            def _(sp):
                for q in range(2):
                    sp.dma_start(gb[:, q], affine[q]).then_inc(loaded, 16)

        def columns(n):
            return slice(n * CH, (n + 1) * CH)

        def pipeline(first, second, third):
            for n in range(-2, NCH):
                if n + 2 < NCH:
                    first(n + 2)
                if 0 <= n + 1 < NCH:
                    second(n + 1)
                if n >= 0:
                    third(n)

        @block.tensor
        def _(pe):
            def mean(n):
                if n >= 2:
                    pe.wait_ge(centred, n - 1)
                for k in range(KC):
                    mm = nc.tensor.matmul(mean_ps[:, n % 2], ones_mean[:], src[:, k, columns(n)],
                                          start=k == 0, stop=k == KC - 1)
                mm.then_inc(mean_ready, 1)

            def variance(n):
                pe.wait_ge(squared, n + 1)
                if n >= 2:
                    pe.wait_ge(sd_ready, n - 1)
                for t in range(TILES):
                    for k in range(KC):
                        mm = nc.tensor.matmul(var_ps[:, n % 2, t:t + 1], sq[:, n % 2, k, t * P:(t + 1) * P],
                                              ones_mean[:, 0:1], start=k == 0, stop=k == KC - 1, skip_group_check=True)
                mm.then_inc(var_ready, 1)

            def spread_out(n):
                pe.wait_ge(rstd_ready, n + 1)
                if n >= 2:
                    pe.wait_ge(normed, n - 1)
                for t in range(TILES):
                    mm = nc.tensor.matmul(r_ps[:, n % 2, t * P:(t + 1) * P], rstd[:, n % 2, t:t + 1].to_broadcast([P, P]),
                                          ident[:], start=True, stop=True, skip_group_check=True)
                mm.then_inc(spread, 1)

            pipeline(mean, variance, spread_out)

        @block.gpsimd
        def _(pool):
            for n in range(NCH):
                pool.wait_ge(centred, n + 1)
                if n >= 2:
                    pool.wait_ge(var_ready, n - 1)
                pool.tensor_tensor(sq[:, n % 2], xc[:, n % 4], xc[:, n % 4], ALU.mult).then_inc(squared, 1)

        @block.scalar
        def _(act):
            act.wait_ge(eps_ready, 1)
            for n in range(NCH):
                act.wait_ge(var_ready, n + 1)
                if n >= 2:
                    act.wait_ge(rstd_ready, n - 1)
                nc.scalar.activation(sd[:, n % 2], var_ps[:, n % 2, 0:TILES], ACT.Sqrt, bias=eps[:]).then_inc(sd_ready, 1)

        @block.vector
        def _(dve):
            def centre(n):
                dve.wait_ge(mean_ready, n + 1)
                if n >= 4:
                    dve.wait_ge(squared, n - 3)
                    dve.wait_ge(normed, n - 3)
                dve.tensor_tensor(xc[:, n % 4], src[:, :, columns(n)],
                                  mean_ps[:, n % 2:n % 2 + 1].to_broadcast([P, KC, CH]), ALU.subtract).then_inc(centred, 1)

            def invert(n):
                dve.wait_ge(sd_ready, n + 1)
                if n >= 2:
                    dve.wait_ge(spread, n - 1)
                dve.reciprocal(rstd[:, n % 2], sd[:, n % 2]).then_inc(rstd_ready, 1)

            def scale(n):
                dve.wait_ge(spread, n + 1)
                dve.wait_ge(centred, n + 1)
                if affine is not None:
                    if n == 0:
                        dve.wait_ge(loaded, 32)
                    for k in range(KC):
                        dve.scalar_tensor_tensor(scaled[:, n % 2, k], xc[:, n % 4, k], gb[:, 0, k:k + 1], r_ps[:, n % 2],
                                                 ALU.mult, ALU.mult).then_inc(scaled_ready, 1)
                    for k in range(KC):
                        dve.wait_ge(scaled_ready, 2 * n + k + 1)
                        c = dst[:, k, columns(n)]
                        ins = dve.scalar_tensor_tensor(c, scaled[:, n % 2, k], gb[:, 1, k:k + 1], c, ALU.add, ALU.add)
                    ins.then_inc(normed, 1)
                    return
                if col_sum is None:
                    dve.tensor_tensor(dst[:, :, columns(n)], xc[:, n % 4],
                                      r_ps[:, n % 2:n % 2 + 1].to_broadcast([P, KC, CH]), ALU.mult).then_inc(normed, 1)
                    return
                for k in range(KC):
                    ins = dve.scalar_tensor_tensor(dst[:, k, columns(n)], xc[:, n % 4, k], 1.0, r_ps[:, n % 2],
                                                   ALU.mult, ALU.mult, accum_out=sums[:, k, n:n + 1])
                ins.then_inc(normed, 1)

            dve.memset(eps[:], eps_value).then_inc(eps_ready, 1)
            pipeline(centre, invert, scale)
            if col_sum is not None:
                dve.wait_ge(normed, NCH)
                dve.reduce_sum(col_sum[:], sums[:], axis=AX.X).then_inc(normed, 1)


def routing_stage(nc, a, col_sum, top_w, top_i):
    E = 8
    CAPACITY = float(-(-N * 5 // (4 * E)))
    with ExitStack() as s:
        m = Memory(nc, s, "routing")
        wr = m.sb("wr_sb", [P, KC, E])
        br = m.sb("br_sb", [1, E])
        mcol = m.sb("token_mean", [P, KC])
        row = m.sb("route_rows", [1, 12, E])
        one = m.sb("route_scalars", [1, 12])
        ones_row = m.sb("ones_row", [1, P])
        lg_ps = m.ps("logits_ps", [1, E])
        w_ps = m.ps("top_w_ps", [P, 2])
        loaded, mean_ready, logits_ready = m.sem("loaded"), m.sem("mean_ready"), m.sem("logits_ready")
        step, exp_in, exp_out, w_ready, ws_ready = (m.sem(x) for x in ("step", "exp_in", "exp_out", "w_ready", "ws_ready"))
        block = s.enter_context(nc.Block())

        @block.sync
        def _(sp):
            sp.dma_start(wr[:], a["wr"].rearrange("(k p) e -> p k e", p=P)).then_inc(loaded, 16)
            sp.dma_start(br[:], a["br"].rearrange("(a e) -> a e", a=1)).then_inc(loaded, 16)

        @block.tensor
        def _(pe):
            pe.wait_ge(loaded, 33)
            pe.wait_ge(mean_ready, 2)
            for k in range(KC):
                mm = nc.tensor.matmul(lg_ps[:], mcol[:, k:k + 1], wr[:, k], start=k == 0, stop=k == KC - 1)
            mm.then_inc(logits_ready, 1)
            pe.wait_ge(ws_ready, 2)
            nc.tensor.matmul(w_ps[:], ones_row[:], row[:, 9, 0:2], start=True, stop=True).then_inc(w_ready, 1)

        @block.scalar
        def _(act):
            for n, (src, dst, bias, total) in enumerate(((0, 1, 1, 2), (4, 5, 5, 6), (7, 8, 9, 10))):
                act.wait_ge(exp_in, n + 2)
                w = E if n < 2 else 2
                nc.scalar.activation(row[:, dst, 0:w], row[:, src, 0:w], ACT.Exp, bias=one[:, bias:bias + 1],
                                     accum_out=one[:, total:total + 1]).then_inc(exp_out, 1)

        @block.vector
        def _(dve):
            count = [0]

            def chain(ins):
                count[0] += 1
                ins.then_inc(step, 1)
                dve.wait_ge(step, count[0] + 1)

            dve.memset(ones_row[:], 1.0).then_inc(step, 1)
            count[0] += 1
            dve.tensor_scalar(mcol[:], col_sum[:], 1.0 / N, None, ALU.mult).then_inc(mean_ready, 1)
            dve.wait_ge(logits_ready, 2)
            chain(dve.tensor_tensor(row[:, 0], lg_ps[:], br[:], ALU.add))

            def softmax(n, src, dst, neg, total, w):
                chain(dve.reduce_max(one[:, neg - 1:neg], row[:, src, 0:w], axis=AX.X))
                dve.tensor_scalar(one[:, neg:neg + 1], one[:, neg - 1:neg], -1.0, None, ALU.mult).then_inc(exp_in, 1)
                dve.wait_ge(exp_out, n + 2)
                chain(dve.reciprocal(one[:, total + 1:total + 2], one[:, total:total + 1]))
                return dve.tensor_scalar(row[:, dst, 0:w], row[:, dst, 0:w], one[:, total + 1:total + 2], None, ALU.mult)

            chain(softmax(0, 0, 1, 1, 2, E))
            chain(dve.tensor_scalar(row[:, 2], row[:, 1], float(N), None, ALU.mult))
            chain(dve.reciprocal(row[:, 3], row[:, 2]))
            chain(dve.tensor_scalar(row[:, 3], row[:, 3], CAPACITY, 1.0, ALU.mult, ALU.min))
            chain(dve.tensor_tensor(row[:, 4], row[:, 1], row[:, 3], ALU.mult))
            chain(softmax(1, 4, 5, 5, 6, E))
            chain(dve.max(row[:, 7], row[:, 5]))
            chain(dve.max_index(top_i[:], row[:, 7], row[:, 5]))
            chain(softmax(2, 7, 8, 9, 10, 2))
            dve.tensor_copy(row[:, 9, 0:2], row[:, 8, 0:2]).then_inc(ws_ready, 1)
            dve.wait_ge(w_ready, 2)
            dve.tensor_copy(top_w[:], w_ps[:]).then_inc(step, 1)


EDGES = 1048576
EC = EDGES // P
BITS = 12
CC = EC // NCH
SEG = 64
KEEP = 16
SEGS = CC // SEG
KEPT = SEGS * KEEP
LISTED = 64
TURN = 8
GATHER_SEMS = 4
HB = 64
HBLOCKS = KEPT // HB


class Histogram:

    def __init__(self, m):
        self.dst = m.sb("hist_dst", [P, KEPT], I32)
        self.push = m.sb("hist_push_out", [P, KEPT])
        self.hi_i = m.sb("hist_hi_int", [P, KEPT], I32)
        self.lo_i = m.sb("hist_lo_int", [P, KEPT], I32)
        self.hi = m.sb("hist_hi", [P, KEPT], BF16)
        self.lo = m.sb("hist_lo", [P, KEPT], BF16)
        self.iota_i = m.sb("hist_iota_int", [P, 64], I32)
        self.iota = m.sb("hist_iota", [P, 64, HB], BF16)
        self.oh = m.sb("hist_one_hot", [P, 2, 2, 64, HB], BF16)
        self.zero = m.sb("hist_zeros", [P, 64], BF16)
        self.c_ps = m.ps("hist_counts_ps", [64, 64])
        self.iota_ready, self.split = m.sem("iota_ready"), m.sem("hist_split")
        self.hot, self.counted = m.sem("hist_hot"), m.sem("hist_counted", start=2)
        self.opened, self.closed = m.sem("hist_opened"), m.sem("hist_closed")

    SPLIT = 6

    def constants(self, dve):
        dve.memset(self.zero[:], 0.0).then_inc(self.iota_ready, 1)
        dve.wait_ge(self.iota_ready, 3)
        dve.tensor_copy(self.iota[:], self.iota_i[:].rearrange("p (v o) -> p v o", o=1).to_broadcast([P, 64, HB]))\
            .then_inc(self.iota_ready, 1)
        dve.wait_ge(self.iota_ready, 4)

    def parts(self, dve, n, cols, ki, src):
        done = [0]

        def then(ins):
            done[0] += 1
            ins.then_inc(self.split, 1)

        def fence():
            dve.wait_ge(self.split, self.SPLIT * n + done[0] + 1)

        fence()
        w = slice(0, cols)
        then(dve.tensor_scalar(self.dst[:, w], ki, BITS, None, ALU.arith_shift_right))
        then(dve.tensor_scalar(self.push[:, w], src, 4095.0, 64.0, ALU.is_lt, ALU.mult))
        fence()
        then(dve.tensor_scalar(self.hi_i[:, w], self.dst[:, w], 6, None, ALU.arith_shift_right))
        then(dve.tensor_scalar(self.lo_i[:, w], self.dst[:, w], 63, None, ALU.bitwise_and))
        fence()
        then(dve.tensor_tensor(self.hi[:, w], self.hi_i[:, w], self.push[:, w], ALU.add))
        then(dve.tensor_copy(self.lo[:, w], self.lo_i[:, w]))
        fence()

    def rows(self, dve, k, place, at=None):
        at = place if at is None else at
        dve.wait_ge(self.counted, k + 1)
        for q, v in enumerate((self.lo, self.hi)):
            dve.tensor_tensor(self.oh[:, place % 2, q], self.iota[:],
                              v[:, at * HB:(at + 1) * HB].rearrange("p (o c) -> p o c", o=1).to_broadcast([P, 64, HB]),
                              ALU.is_equal).then_inc(self.hot, 1)

    def open(self, nc, pe):
        pe.wait_ge(self.iota_ready, 4)
        nc.tensor.matmul(self.c_ps[:], self.zero[:], self.zero[:], start=True, stop=False, skip_group_check=True)\
            .then_inc(self.opened, 1)
        pe.wait_ge(self.opened, 2)

    def count(self, nc, pe, k, place):
        pe.wait_ge(self.hot, 2 * k + 2 + 1)
        for c in range(HB):
            mm = nc.tensor.matmul(self.c_ps[:], self.oh[:, place % 2, 0, :, c], self.oh[:, place % 2, 1, :, c],
                                  start=False, stop=False, skip_group_check=True)
        mm.then_inc(self.counted, 1)

    def close(self, nc):
        nc.tensor.matmul(self.c_ps[:], self.zero[:], self.zero[:], start=False, stop=True, skip_group_check=True)\
            .then_inc(self.closed, 1)


def expert_stage(nc, passed, a, xn, top_w, top_i, keys_dram, plan, counts):
    F = 512
    KF = F // P
    e_v = a["edges"].rearrange("t (p c) -> t p c", p=P)
    with ExitStack() as s:
        m = Memory(nc, s, "expert")
        w1 = m.sb("w1_sb", [P, 2, KC, F])
        w2 = m.sb("w2_sb", [P, 2, KF, C])
        b1 = m.sb("b1_sb", [P, 2, KF])
        b2 = m.sb("b2_sb", [P, 2, KC])
        b2w = m.sb("b2_weighted", [P, 2, KC])
        b2s = m.sb("b2_sum", [P, KC])
        hid = m.sb("hidden", [P, 4, CH])
        h_ps = m.ps("hidden_ps", [P, 2, CH])
        y_ps = m.ps("y_ps", [P, 2, KC, CH])
        raw = m.sb("raw", [P, 2, 2, CC], I32)
        sp1 = m.sb("src_plus_1", [P, CC])
        kk = m.sb("key_any", [P, CC])
        kb = m.sb("key_chunk", [P, 2, CC])
        work = m.sb("key_left", [P, CC])
        cand = m.sb("packed", [P, SEGS, KEEP])
        ki = m.sb("packed_int", [P, KEPT], I32)
        ksrc = m.sb("packed_src", [P, KEPT], I32)
        cl = m.sb("listed_from", [P, KEPT])
        lc = m.sb("list_parts", [P, NCH, KEEP])
        l1 = m.sb("list_part", [P, KEEP])
        lf = m.sb("list", [P, LISTED + TURN])
        held = m.sb("list_held", [P, LISTED])
        turns_i = m.sb("turns_int", [P, 2], I32)
        turns_f = m.sb("turns", [P, 1])
        left = m.sb("left_over", [P, NCH, 2])
        lmax = m.sb("left_max", [P, 3])
        lall = m.sb("left_all", [P, 3])
        pf = m.sb("plan_f", [P, 2])
        hist = Histogram(m)
        loaded, weighted = m.sem("loaded"), m.sem("weighted")
        h_ready, h_done, y_ready = m.sem("h_ready"), m.sem("h_done"), m.sem("y_ready")
        z_done = m.sem("z_done", start=2)
        edges_loaded = [m.sem("edges_loaded0"), m.sem("edges_loaded1")]
        stored = [m.sem("stored0"), m.sem("stored1")]
        step, keyed, listed = m.sem("step"), m.sem("keyed"), m.sem("listed")
        left_ready, all_ready, done = m.sem("left_ready"), m.sem("all_ready"), m.sem("done")
        block = s.enter_context(nc.Block())

        @block.sync
        def _(sp):
            def load_edges(n, b):
                for t in range(2):
                    sp.dma_start(raw[:, b, t], e_v[t, :, bass.ds(n * CC, CC)]).then_inc(edges_loaded[b], 16)

            def store_keys(n, b):
                sp.wait_ge(keyed, n + 2)
                sp.dma_start(keys_dram[:, bass.ds(n * CC, CC)], kb[:, b]).then_inc(stored[b], 16)

            for j in range(2):
                e = sp.value_load(top_i[0:1, j:j + 1], min_val=0, max_val=7)
                sp.dma_start(w1[:, j], a["w1"].rearrange("e (k p) f -> p e k f", p=P)[:, bass.ds(e, 1)]
                             .rearrange("p o k f -> p (o k) f")).then_inc(loaded, 16)
                sp.dma_start(w2[:, j], a["w2"].rearrange("e (k p) d -> p e k d", p=P)[:, bass.ds(e, 1)]
                             .rearrange("p o k d -> p (o k) d")).then_inc(loaded, 16)
                sp.dma_start(b1[:, j], a["b1"].rearrange("p (e k) -> p e k", k=KF)[:, bass.ds(e, 1)]
                             .rearrange("p o k -> p (o k)")).then_inc(loaded, 16)
                sp.dma_start(b2[:, j], a["b2"].rearrange("p (e k) -> p e k", k=KC)[:, bass.ds(e, 1)]
                             .rearrange("p o k -> p (o k)")).then_inc(loaded, 16)
            for b in range(2):
                load_edges(b, b)
            with sp.Fori(0, NCH // 2 - 1) as i:
                for b in range(2):
                    store_keys(2 * i + b, b)
                    load_edges(2 * i + b + 2, b)
            for b in range(2):
                store_keys(NCH - 2 + b, b)
            sp.wait_ge(listed, 2)
            sp.dma_start(keys_dram[:, EC:EC + LISTED + TURN], lf[:]).then_inc(stored[0], 16)
            sp.wait_ge(stored[0], 16 * (NCH // 2 + 1) + 1)
            sp.wait_ge(stored[1], 16 * NCH // 2 + 1)

        @block.tensor
        def _(pe):
            hist.open(nc, pe)
            pe.wait_ge(weighted, 6)
            with pe.Fori(0, NCH // 2) as i:
                for b in range(2):
                    n = 2 * i + b

                    def out(q):
                        pe.wait_ge(h_done, 8 * n + q + 2)
                        for o in range(KC):
                            mm = nc.tensor.matmul(y_ps[:, b, o], w2[:, q // KF, q % KF, o * P:(o + 1) * P], hid[:, q % 4],
                                                  start=q == 0, stop=q == 2 * KF - 1)
                        mm.then_inc(y_ready, 1)

                    for q in range(2 * KF):
                        pe.wait_ge(h_done, 8 * n + max(q - 1, 0) + 1)
                        for k in range(KC):
                            mm = nc.tensor.matmul(h_ps[:, q % 2], w1[:, q // KF, k, (q % KF) * P:(q % KF + 1) * P],
                                                  xn[:, k, bass.ds(n * CH, CH)], start=k == 0, stop=k == KC - 1)
                        mm.then_inc(h_ready, 1)
                        if q == 2:
                            pe.wait_ge(z_done, n + 1)
                        if q >= 2:
                            out(q - 2)
                        if q >= 2 * KF - HBLOCKS + 1:
                            place = q - (2 * KF - HBLOCKS + 1)
                            hist.count(nc, pe, HBLOCKS * n + place, place)
                    out(2 * KF - 2)
                    out(2 * KF - 1)
                    hist.count(nc, pe, HBLOCKS * n + HBLOCKS - 1, HBLOCKS - 1)
            hist.close(nc)

        @block.scalar
        def _(act):
            act.wait_ge(loaded, 16 * 8 + 1)
            with act.Fori(0, NCH) as n:
                for q in range(2 * KF):
                    act.wait_ge(h_ready, 8 * n + q + 2)
                    act.wait_ge(y_ready, 8 * n + max(q - 3, 0) + 1)
                    nc.scalar.activation(hid[:, q % 4], h_ps[:, q % 2], ACT.Gelu,
                                         bias=b1[:, q // KF, q % KF:q % KF + 1]).then_inc(h_done, 1)

        @block.gpsimd
        def _(pool):
            pool.iota(hist.iota_i[:], pattern=[[1, 64]], base=0, channel_multiplier=0).then_inc(hist.iota_ready, 1)
            pool.wait_ge(left_ready, 2)
            pool.partition_all_reduce(lall[:], lmax[:], P, RMAX).then_inc(all_ready, 1)

        @block.vector
        def _(dve):
            STEPS = 2 + 3 * SEGS + 4 + 2 * 2 + 2
            at = [0, 0]

            def then(ins):
                at[0] += 1
                ins.then_inc(step, 1)

            def chain(ins):
                then(ins)
                dve.wait_ge(step, at[1] + at[0] + 1)
                dve.sem_inc(passed, 1)

            def keys(n, b, i):
                at[:] = [0, n * STEPS]
                dve.wait_ge(edges_loaded[b], 32 * i + 32 + 1)
                chain(dve.tensor_scalar(sp1[:], raw[:, b, 0], 4095, 1, ALU.min, ALU.add))
                chain(dve.scalar_tensor_tensor(kk[:], raw[:, b, 1], 4096.0, sp1[:], ALU.mult, ALU.add))
                dve.wait_ge(stored[b], 16 * i + 1)
                dve.scalar_tensor_tensor(kb[:, b], raw[:, b, 1], 4096.0, kk[:], ALU.is_lt, ALU.mult).then_inc(keyed, 1)
                dve.wait_ge(keyed, n + 2)
                dve.sem_inc(passed, 1)
                for g in range(SEGS):
                    then(dve.max(cand[:, g, 0:8], kb[:, b, g * SEG:(g + 1) * SEG]))
                dve.wait_ge(step, at[1] + at[0] + 1)
                dve.sem_inc(passed, 1)
                for g in range(SEGS):
                    part = slice(g * SEG, (g + 1) * SEG)
                    then(dve.match_replace(work[:, part], cand[:, g, 0:8], kb[:, b, part], 0.0))
                dve.wait_ge(step, at[1] + at[0] + 1)
                dve.sem_inc(passed, 1)
                for g in range(SEGS):
                    then(dve.max(cand[:, g, 8:16], work[:, g * SEG:(g + 1) * SEG]))
                dve.wait_ge(step, at[1] + at[0] + 1)
                dve.sem_inc(passed, 1)
                flat = cand[:].rearrange("p s k -> p (s k)")
                then(dve.reduce_max(left[:, bass.ds(n, 1), 0:1].rearrange("p a c -> p (a c)"),
                                    cand[:, :, KEEP - 1:KEEP].rearrange("p s o -> p (s o)"), axis=AX.X))
                chain(dve.tensor_scalar(ki[:], flat, 1.0, None, ALU.subtract))
                chain(dve.tensor_scalar(ksrc[:], ki[:], 4095, None, ALU.bitwise_and))
                chain(dve.scalar_tensor_tensor(cl[:], ksrc[:], 4095.0, flat, ALU.is_lt, ALU.mult))
                for r in range(2):
                    chain(dve.max(l1[:, 8 * r:8 * r + 8], cl[:]))
                    chain(dve.match_replace(cl[:], l1[:, 8 * r:8 * r + 8], cl[:], 0.0))
                chain(dve.reduce_max(left[:, bass.ds(n, 1), 1:2].rearrange("p a c -> p (a c)"), cl[:], axis=AX.X))
                chain(dve.tensor_copy(lc[:, bass.ds(n, 1)].rearrange("p a k -> p (a k)"), l1[:]))
                assert at[0] == STEPS, (at[0], STEPS)

            hist.constants(dve)
            dve.wait_ge(loaded, 16 * 8 + 1)
            for j in range(2):
                dve.tensor_scalar(w2[:, j], w2[:, j], top_w[:, j:j + 1], None, ALU.mult).then_inc(weighted, 1)
                dve.tensor_scalar(b2w[:, j], b2[:, j], top_w[:, j:j + 1], None, ALU.mult).then_inc(weighted, 1)
            dve.wait_ge(weighted, 5)
            dve.tensor_tensor(b2s[:], b2w[:, 0], b2w[:, 1], ALU.add).then_inc(weighted, 1)
            dve.wait_ge(weighted, 6)

            def add_output(n, b):
                dve.wait_ge(y_ready, 8 * n + 8 + 1)
                for o in range(KC):
                    c = xn[:, o, bass.ds(n * CH, CH)]
                    ins = dve.scalar_tensor_tensor(c, y_ps[:, b, o], b2s[:, o:o + 1], c, ALU.add, ALU.add)
                ins.then_inc(z_done, 1)

            def rows(n):
                hist.parts(dve, n, KEPT, ki[:], ksrc[:])
                for place in range(HBLOCKS):
                    hist.rows(dve, HBLOCKS * n + place, place)

            keys(0, 0, 0)
            rows(0)
            with dve.Fori(0, NCH // 2 - 1) as i:
                for b in (1, 0):
                    n = 2 * i + 2 - b
                    keys(n, b, i + 1 - b)
                    add_output(n - 1, 1 - b)
                    rows(n)
            keys(NCH - 1, 1, NCH // 2 - 1)
            add_output(NCH - 2, 0)
            rows(NCH - 1)
            add_output(NCH - 1, 1)

            at[:] = [0, STEPS * NCH]
            flat = lc[:].rearrange("p n k -> p (n k)")
            chain(dve.memset(lf[:, LISTED:], 0.0))
            for r in range(LISTED // 8):
                chain(dve.max(lf[:, 8 * r:8 * r + 8], flat))
                ins = dve.match_replace(flat, lf[:, 8 * r:8 * r + 8], flat, 0.0)
                if r == LISTED // 8 - 1:
                    ins.then_inc(listed, 1)
                    dve.wait_ge(listed, 2)
                else:
                    chain(ins)
            chain(dve.tensor_scalar(held[:], lf[:, 0:LISTED], 0.0, None, ALU.is_gt))
            chain(dve.tensor_reduce(lmax[:, 2:3], held[:], AX.X, ALU.add))
            chain(dve.reduce_max(lmax[:, 0:1], left[:, :, 0:1].rearrange("p n o -> p (n o)"), axis=AX.X))
            chain(dve.reduce_max(lmax[:, 1:2], left[:, :, 1:2].rearrange("p n o -> p (n o)"), axis=AX.X))
            chain(dve.reduce_max(pf[:, 0:1], flat, axis=AX.X))
            chain(dve.tensor_tensor(pf[:, 1:2], pf[:, 0:1], lmax[:, 1:2], ALU.max))
            dve.tensor_tensor(lmax[:, 1:2], pf[:, 1:2], lmax[:, 0:1], ALU.max).then_inc(left_ready, 1)
            dve.wait_ge(hist.closed, 2)
            dve.tensor_copy(counts[:], hist.c_ps[:]).then_inc(done, 1)
            dve.wait_ge(all_ready, 2)
            chain(dve.tensor_scalar(pf[:, 0:2], lall[:, 0:2], 0.0, None, ALU.is_gt))
            dve.tensor_copy(plan[:, 0:1], pf[:, 0:1]).then_inc(done, 1)
            dve.tensor_scalar(plan[:, 1:2], pf[:, 0:1], float(EC // HB // 2 - 1), 1.0, ALU.mult, ALU.add).then_inc(done, 1)
            start = float(EC)
            dve.tensor_scalar(plan[:, 2:3], pf[:, 1:2], -start, start, ALU.mult, ALU.add).then_inc(done, 1)
            chain(dve.tensor_scalar(turns_i[:, 0:1], lall[:, 2:3], float(2 * TURN - 1), None, ALU.add))
            chain(dve.tensor_scalar(turns_i[:, 1:2], turns_i[:, 0:1], (2 * TURN).bit_length() - 1, None, ALU.arith_shift_right))
            chain(dve.tensor_scalar(turns_f[:], turns_i[:, 1:2], 2.0, None, ALU.max))
            dve.scalar_tensor_tensor(plan[:, 3:4], pf[:, 1:2], float(EC // TURN // 2), turns_f[:], ALU.mult, ALU.max)\
                .then_inc(done, 1)


W = 64
PW = W + 4
NB6 = 6 * PW


def conv_in_stage(nc, a, cn, h, hpad, hT, gate, ident):
    with ExitStack() as s:
        m = Memory(nc, s, "conv_in")
        w1 = m.sb("cw1_sb", [P, KC, P])
        w2 = m.sb("cw2_sb", [P, P])
        b1 = m.sb("cb1_sb", [P, 1])
        b2 = m.sb("cb2_sb", [P, 1])
        g0 = m.sb("gate_in", [P, 2, CH])
        h_ps = m.ps("h_ps", [P, 2, CH])
        g_ps = m.ps("g_ps", [P, 2, CH])
        t_ps = m.ps("t_ps", [P, 2, 4, P])
        loaded, cleared, h_ready, h_done = m.sem("loaded"), m.sem("cleared"), m.sem("h_ready"), m.sem("h_done", start=2)
        padded, g_ready = m.sem("padded", start=2), m.sem("g_ready")
        relu_done, gate_done = m.sem("relu_done", start=2), m.sem("gate_done", start=2)
        t_ready, t_done = m.sem("t_ready", start=2), m.sem("t_done", start=2)
        block = s.enter_context(nc.Block())

        @block.sync
        def _(sp):
            sp.dma_start(w1[:], a["cw1T"].rearrange("(k p) o -> p k o", p=P)).then_inc(loaded, 16)
            sp.dma_start(w2[:], a["cw2T"]).then_inc(loaded, 16)
            sp.dma_start(b1[:], a["cb1"]).then_inc(loaded, 16)
            sp.dma_start(b2[:], a["cb2"]).then_inc(loaded, 16)

        def pipeline(eng, step):
            for n in range(NCH):
                step(n, n % 2, n + 1 < NCH)

        def columns(n):
            return slice(n * CH, (n + 1) * CH)

        @block.tensor
        def _(pe):
            def h_of(n, b):
                pe.wait_ge(h_done, n + 1)
                for k in range(KC):
                    mm = nc.tensor.matmul(h_ps[:, b], w1[:, k], cn[:, k, columns(n)],
                                          start=k == 0, stop=k == KC - 1)
                mm.then_inc(h_ready, 1)

            def step(n, b, following):
                if following:
                    h_of(n + 1, 1 - b)
                pe.wait_ge(h_done, n + 3)
                pe.wait_ge(relu_done, n + 1)
                nc.tensor.matmul(g_ps[:, b], w2[:], h[:, columns(n)], start=True, stop=True).then_inc(g_ready, 1)
                pe.wait_ge(t_done, n + 1)
                for j in range(4):
                    mm = nc.tensor.transpose(t_ps[:, b, j], h[:, n * CH + j * P:n * CH + (j + 1) * P], ident[:])
                mm.then_inc(t_ready, 1)

            pe.wait_ge(loaded, 65)
            h_of(0, 0)
            pipeline(pe, step)

        @block.gpsimd
        def _(pool):
            pool.memset(hpad[:], 0.0).then_inc(cleared, 1)
            pool.memset(hT[:, 0], 0.0).then_inc(cleared, 1)
            pool.memset(hT[:, NT + 1], 0.0).then_inc(cleared, 1)
            pool.wait_ge(cleared, 4)
            with pool.Fori(0, NCH // 2) as i:
                for b in range(2):
                    n = 2 * i + b
                    pool.wait_ge(h_done, n + 3)
                    pool.tensor_copy(hpad[:].rearrange("p (y x) -> p y x", x=PW)[:, bass.ds(8 * n + 2, 8), 2:2 + W],
                                     h[:, bass.ds(n * CH, CH)].rearrange("p (y x) -> p y x", x=W)).then_inc(padded, 1)

        @block.scalar
        def _(act):
            act.wait_ge(cleared, 4)
            with act.Fori(0, NCH // 2) as i:
                for b in range(2):
                    n = 2 * i + b
                    act.wait_ge(relu_done, n + 3)
                    nc.scalar.activation(gate[:, bass.ds(n * CH, CH)], g0[:, b], ACT.Sigmoid).then_inc(gate_done, 1)
                    act.wait_ge(t_ready, n + 3)
                    nc.scalar.activation(hT[:, bass.ds(4 * n + 1, 4)], t_ps[:, b], ACT.Copy).then_inc(t_done, 1)

        @block.vector
        def _(dve):
            def biased(n, b):
                dve.wait_ge(h_ready, n + 2)
                dve.tensor_scalar(h[:, columns(n)], h_ps[:, b], b1[:], None, ALU.add).then_inc(h_done, 1)

            def step(n, b, following):
                if following:
                    biased(n + 1, 1 - b)
                dve.wait_ge(g_ready, n + 2)
                dve.wait_ge(gate_done, n + 1)
                dve.tensor_scalar(g0[:, b], g_ps[:, b], b2[:], 0.0, ALU.add, ALU.max).then_inc(relu_done, 1)

            dve.wait_ge(loaded, 65)
            biased(0, 0)
            pipeline(dve, step)


def conv_out_stage(nc, a, h, hpad, hT, gate, res, ident):
    with ExitStack() as s:
        m = Memory(nc, s, "conv_out")
        wo = m.sb("wout_sb", [P, C])
        bo = m.sb("bout_sb", [P, KC])
        mask = m.sb("mask", [P, 6, PW])
        sc = m.sb("scores", [P, 2, 2, NB6])
        mx = m.sb("score_max", [P, 2])
        nmx = m.sb("neg_max", [P, 2, 2])
        ex = m.sb("exps", [P, 2, 2, 6, PW])
        den = m.sb("dens", [P, 2, 2])
        rden = m.sb("rdens", [P, 2, 2])
        an = m.sb("weights", [P, 2, 6 * W])
        aT = m.sb("weightsT", [P, 2, 3, P])
        att = m.sb("gated", [P, CH])
        g_ps = m.ps("gram_ps", [P, 2, CH])
        t_ps = m.ps("wT_ps", [P, 2, CH])
        s_ps = m.ps("sample_ps", [P, 4, P])
        o_ps = m.ps("out_ps", [P, KC, CH])
        loaded, masked = m.sem("loaded"), m.sem("masked")
        gram_ready, sc_ready, max_ready, nmax_ready = (m.sem(x) for x in ("gram_ready", "sc_ready", "max_ready", "nmax_ready"))
        ex_ready, an_ready = m.sem("ex_ready", start=2), m.sem("an_ready", start=2)
        rden_ready, t_ready = m.sem("rden_ready"), m.sem("t_ready")
        s_ready = m.sem("s_ready", start=2)
        aT_ready, att_ready, o_ready, added = (m.sem(x) for x in ("aT_ready", "att_ready", "o_ready", "added"))
        block = s.enter_context(nc.Block())

        def pipeline(step):
            for H in range(2 * NCH):
                step(H // 2, H % 2)

        @block.sync
        def _(sp):
            sp.dma_start(wo[:], a["cwoT"]).then_inc(loaded, 16)
            sp.dma_start(bo[:], a["cbo"]).then_inc(loaded, 16)

        @block.gpsimd
        def _(pool):
            pool.memset(mask[:], 0.0).then_inc(masked, 1)
            for dy in range(2):
                rows = mask[W * dy:W * dy + W]
                for q, (pattern, base, mult) in enumerate((
                        ([[0, 6], [1, PW]], 0, -1), ([[0, 6], [-1, PW]], 4, 1),
                        ([[1, 6], [0, PW]], -dy, 0), ([[-1, 6], [0, PW]], 4 + dy, 0))):
                    pool.wait_ge(masked, 4 * dy + q + 2)
                    pool.affine_select(out=rows, in_=rows, compare_op=ALU.is_ge, fill=-1e30, base=base,
                                       pattern=pattern, channel_multiplier=mult).then_inc(masked, 1)
            pool.wait_ge(masked, 10)

        @block.tensor
        def _(pe):
            def gram(H):
                pe.wait_ge(sc_ready, H + 1)
                for j in range(2):
                    row = 4 * H + 2 * j
                    mm = nc.tensor.matmul(g_ps[:, j, 0:NB6], h[:, row * W:(row + 2) * W], hpad[:, row * PW:row * PW + NB6],
                                          start=True, stop=True)
                mm.then_inc(gram_ready, 1)

            def out(n):
                pe.wait_ge(att_ready, n + 2)
                pe.wait_ge(added, n + 1)
                for o in range(KC):
                    mm = nc.tensor.matmul(o_ps[:, o], wo[:, o * P:(o + 1) * P], att[:], start=True, stop=True)
                mm.then_inc(o_ready, 1)

            def step(n, half):
                H = 2 * n + half
                if H + 2 < 2 * NCH:
                    gram(H + 2)
                pe.wait_ge(an_ready, H + 3)
                pe.wait_ge(aT_ready, H + 1)
                for j in range(2):
                    for q in range(3):
                        mm = nc.tensor.transpose(t_ps[:, j, q * P:(q + 1) * P], an[:, j, q * P:(q + 1) * P], ident[:])
                mm.then_inc(t_ready, 1)
                pe.wait_ge(aT_ready, H + 2)
                if half == 0:
                    pe.wait_ge(att_ready, n + 1)
                for j in range(2):
                    for q in range(3):
                        mm = nc.tensor.matmul(s_ps[:, 2 * half + j], hT[:, 2 * H + j + q], aT[:, j, q], start=q == 0,
                                              stop=q == 2, skip_group_check=True)
                if half == 1:
                    mm.then_inc(s_ready, 1)
                if half == 0 and n > 0:
                    out(n - 1)

            pe.wait_ge(loaded, 33)
            gram(0)
            gram(1)
            pipeline(step)
            out(NCH - 1)

        @block.scalar
        def _(act):
            def exps(H, hb):
                act.wait_ge(nmax_ready, H + 2)
                act.wait_ge(an_ready, H + 1)
                for j in range(2):
                    e = nc.scalar.activation(ex[:, hb, j].rearrange("p y x -> p (y x)"), sc[:, hb, j], ACT.Exp,
                                             bias=nmx[:, hb, j:j + 1], accum_out=den[:, hb, j:j + 1])
                e.then_inc(ex_ready, 1)

            def step(n, half):
                H = 2 * n + half
                if H + 1 < 2 * NCH:
                    exps(H + 1, 1 - half)
                act.wait_ge(t_ready, H + 2)
                nc.scalar.activation(aT[:].rearrange("p j q c -> p j (q c)"), t_ps[:, :, 0:3 * P], ACT.Copy)\
                    .then_inc(aT_ready, 1)

            exps(0, 0)
            pipeline(step)

        @block.vector
        def _(dve):
            def score(H, hb):
                dve.wait_ge(gram_ready, H + 2)
                dve.wait_ge(ex_ready, H + 1)
                dve.scalar_tensor_tensor(sc[:, hb], g_ps[:, :, 0:NB6], float(P) ** -0.5,
                                         mask[:].rearrange("p y x -> p (y x)").rearrange("p (o z) -> p o z", o=1)
                                         .to_broadcast([P, 2, NB6]), ALU.mult, ALU.add).then_inc(sc_ready, 1)
                dve.wait_ge(sc_ready, H + 2)
                dve.reduce_max(mx[:], sc[:, hb], axis=AX.X).then_inc(max_ready, 1)
                dve.wait_ge(max_ready, H + 2)
                dve.tensor_scalar(nmx[:, hb], mx[:], -1.0, None, ALU.mult).then_inc(nmax_ready, 1)

            def gated(n):
                dve.wait_ge(s_ready, n + 3)
                dve.wait_ge(o_ready, n + 1)
                dve.tensor_tensor(att[:], s_ps[:].rearrange("p t x -> p (t x)"), gate[:, bass.ds(n * CH, CH)], ALU.mult)\
                    .then_inc(att_ready, 1)

            def add(n):
                dve.wait_ge(o_ready, n + 2)
                for o in range(KC):
                    c = res[:, o, bass.ds(n * CH, CH)]
                    ins = dve.scalar_tensor_tensor(c, o_ps[:, o], bo[:, o:o + 1], c, ALU.add, ALU.add)
                ins.then_inc(added, 1)

            def step(n, half):
                H = 2 * n + half
                if H + 1 < 2 * NCH:
                    score(H + 1, 1 - half)
                dve.wait_ge(ex_ready, H + 3)
                dve.reciprocal(rden[:, half], den[:, half]).then_inc(rden_ready, 1)
                dve.wait_ge(rden_ready, H + 2)
                dve.wait_ge(t_ready, H + 1)
                for j in range(2):
                    ins = dve.tensor_scalar(an[:, j].rearrange("p (y x) -> p y x", x=W), ex[:, half, j, :, 2:2 + W],
                                            rden[:, half, j:j + 1], None, ALU.mult)
                ins.then_inc(an_ready, 1)
                if half == 0 and n > 0:
                    gated(n - 1)
                if half == 1 and n > 0:
                    add(n - 1)

            dve.wait_ge(masked, 10)
            dve.wait_ge(loaded, 33)
            score(0, 0)
            pipeline(step)
            gated(NCH - 1)
            add(NCH - 1)


H4 = 4
NE = 4
G20 = H4 + H4 * NE
BIG = 1e30


class ClampedCount:
    MAXT = EC // HB // 2

    def __init__(self, nc, m, keys_dram, plan, counts, clamped, ident):
        self.nc, self.keys_dram, self.plan, self.counts, self.clamped, self.ident = nc, keys_dram, plan, counts, clamped, ident
        self.kb = m.sb("keys", [P, 2, HB])
        self.ki = m.sb("key_int", [P, HB], I32)
        self.src = m.sb("src", [P, HB], I32)
        self.full = m.sb("full_flag", [P, 1])
        self.packed = m.sb("packed_flag", [P, 1])
        self.cs = m.sb("counts_blend", [64, 64])
        self.o_ps = m.ps("clamped_ps", [P, NT])
        self.hist = Histogram(m)
        self.loaded = [m.sem("loaded0"), m.sem("loaded1")]
        self.step, self.flags, self.copied, self.spread = m.sem("step"), m.sem("flags"), m.sem("copied"), m.sem("spread")

    def turns(self, eng):
        return eng.value_load(self.plan[0:1, 1:2], min_val=1, max_val=self.MAXT)

    def sync(self, sp):
        with sp.Fori(0, self.turns(sp)) as i:
            for b in range(2):
                sp.wait_ge(self.step, 4 * i + 1)
                sp.dma_start(self.kb[:, b], self.keys_dram[:, bass.ds((2 * i + b) * HB, HB)]).then_inc(self.loaded[b], 16)

    def gpsimd(self, pool):
        pool.iota(self.hist.iota_i[:], pattern=[[1, 64]], base=0, channel_multiplier=0).then_inc(self.hist.iota_ready, 1)

    def tensor(self, pe):
        nc, hist = self.nc, self.hist
        turns = self.turns(pe)
        hist.open(nc, pe)
        with pe.Fori(0, turns) as i:
            for b in range(2):
                hist.count(nc, pe, 2 * i + b, b)
        hist.close(nc)
        pe.wait_ge(self.copied, 3)
        v = self.cs[:].rearrange("p (t o) -> p t o", o=2)
        for o in range(2):
            mm = nc.tensor.matmul(self.o_ps[64 * o:64 * o + 64], self.ident[0:64, 0:64], v[:, :, o], start=True, stop=True,
                                  skip_group_check=True)
        mm.then_inc(self.spread, 1)

    def vector(self, dve):
        hist, full, packed, counts, ki, src = self.hist, self.full, self.packed, self.counts, self.ki, self.src
        turns = self.turns(dve)
        hist.constants(dve)
        dve.tensor_copy(full[:], self.plan[:, 0:1]).then_inc(self.flags, 1)
        dve.wait_ge(self.flags, 2)
        dve.tensor_scalar(packed[:], full[:], -1.0, 1.0, ALU.mult, ALU.add).then_inc(self.flags, 1)
        with dve.Fori(0, turns) as i:
            for b in range(2):
                n = 2 * i + b
                dve.wait_ge(self.loaded[b], 16 * i + 16 + 1)
                dve.tensor_scalar(ki[:], self.kb[:, b], 1.0, None, ALU.subtract).then_inc(self.step, 1)
                dve.wait_ge(self.step, 2 * n + 2)
                dve.tensor_scalar(src[:], ki[:], 4095, None, ALU.bitwise_and).then_inc(self.step, 1)
                dve.wait_ge(self.step, 2 * n + 3)
                hist.parts(dve, n, HB, ki[:], src[:])
                hist.rows(dve, n, b, at=0)
        dve.wait_ge(hist.closed, 2)
        dve.wait_ge(self.flags, 3)
        dve.tensor_scalar(counts[:], counts[:], packed[0:64], None, ALU.mult).then_inc(self.copied, 1)
        dve.wait_ge(self.copied, 2)
        dve.scalar_tensor_tensor(self.cs[:], hist.c_ps[:], full[0:64], counts[:], ALU.mult, ALU.add).then_inc(self.copied, 1)
        dve.wait_ge(self.spread, 2)
        dve.tensor_copy(self.clamped[:], self.o_ps[:]).then_inc(self.copied, 1)


def node_features_stage(nc, a, xn, feat, adst, node_dram, keys_dram, plan, counts, clamped, ident):
    with ExitStack() as s:
        m = Memory(nc, s, "nodes")
        wg = m.sb("w_gat", [P, KC, 16])
        att = m.sb("att", [P, 2, 16])
        hc = m.sb("h_chunk", [16, 2, CH])
        prod = m.sb("products", [P, NT, 16])
        h_ps = m.ps("h_ps", [16, 2, CH])
        t_ps = m.ps("hT_ps", [P, NT, 16])
        loaded, h_ready, h_done, t_ready = m.sem("loaded"), m.sem("h_ready"), m.sem("h_done"), m.sem("t_ready")
        step, feat_ready, stored = m.sem("step"), m.sem("feat_ready"), m.sem("stored")
        clamped_count = ClampedCount(nc, Memory(nc, s, "count"), keys_dram, plan, counts, clamped, ident)
        block = s.enter_context(nc.Block())

        @block.gpsimd
        def _(pool):
            clamped_count.gpsimd(pool)

        @block.sync
        def _(sp):
            sp.dma_start(wg[:], a["wgat"].rearrange("(k p) o -> p k o", p=P)).then_inc(loaded, 16)
            sp.dma_start(att[:, 0], a["att_src"].rearrange("(a n) -> a n", a=1).to_broadcast([P, 16])).then_inc(loaded, 16)
            sp.dma_start(att[:, 1], a["att_dst"].rearrange("(a n) -> a n", a=1).to_broadcast([P, 16])).then_inc(loaded, 16)
            clamped_count.sync(sp)
            sp.wait_ge(feat_ready, 2)
            sp.dma_start(node_dram.rearrange("(t p) f -> p t f", p=P), feat[:]).then_inc(stored, 16)
            sp.wait_ge(stored, 17)

        @block.tensor
        def _(pe):
            def h_of(n):
                if n >= 2:
                    pe.wait_ge(h_done, n)
                for k in range(KC):
                    mm = nc.tensor.matmul(h_ps[:, n % 2], wg[:, k], xn[:, k, n * CH:(n + 1) * CH],
                                          start=k == 0, stop=k == KC - 1)
                mm.then_inc(h_ready, 1)

            pe.wait_ge(loaded, 49)
            h_of(0)
            for n in range(NCH):
                if n + 1 < NCH:
                    h_of(n + 1)
                pe.wait_ge(h_done, n + 2)
                for j in range(4):
                    mm = nc.tensor.transpose(t_ps[:, 4 * n + j], hc[:, n % 2, j * P:(j + 1) * P], ident[0:16, 0:16])
                mm.then_inc(t_ready, 1)
            clamped_count.tensor(pe)

        @block.scalar
        def _(act):
            for n in range(NCH):
                act.wait_ge(h_ready, n + 2)
                if n >= 2:
                    act.wait_ge(t_ready, n)
                nc.scalar.activation(hc[:, n % 2], h_ps[:, n % 2], ACT.Copy).then_inc(h_done, 1)

        @block.vector
        def _(dve):
            at = [0]

            def chain(ins):
                at[0] += 1
                ins.then_inc(step, 1)
                dve.wait_ge(step, at[0] + 1)

            clamped_count.vector(dve)
            dve.wait_ge(loaded, 49)
            dve.wait_ge(t_ready, NCH + 1)
            chain(dve.tensor_copy(feat[:, :, H4:G20], t_ps[:]))
            for q in range(2):
                chain(dve.tensor_tensor(prod[:], feat[:, :, H4:G20], att[:, q:q + 1].to_broadcast([P, NT, 16]), ALU.mult))
                dst = feat[:, :, 0:H4] if q == 0 else adst[:]
                chain(dve.reduce_sum(dst, prod[:].rearrange("p t (h e) -> p t h e", h=H4), axis=AX.X))
            dve.tensor_copy(prod[:, 0:1], prod[:, 1:2]).then_inc(feat_ready, 1)


def edge_max_stage(nc, passed, keys_dram, plan, feat, node_dram, shift, table, iota128, iota32, ident):
    NX = TURN * (1 + H4)
    with ExitStack() as s:
        m = Memory(nc, s, "emax")
        kb = m.sb("keys", [P, 2, TURN])
        dec = EdgeNumbers(m)
        av = m.sb("gathered", [P, 2, TURN, G20])
        x = m.sb("columns", [P, 2, NX])
        dbc = m.sb("dst_rows", [P, 2, TURN, P])
        lower = m.sb("lower", [P, P])
        val = m.sb("masked", [P, H4, P])
        first = m.sb("earlier", [P, TURN])
        junk = m.sb("junk", [P, P])
        lead = m.sb("leader", [P, TURN])
        best = m.sb("best", [P, TURN, H4])
        ohlo = m.sb("lo_rows", [P, 2, P])
        rhs = m.sb("hi_rows", [P, 2, NT, H4])
        fneg = m.sb("neg_feat", [P, H4])
        fall = m.sb("neg_all", [P, H4])
        d_ps = m.ps("dst_rows_ps", [P, TURN, P])
        a_ps = m.ps("a_rows_ps", [P, 2, H4, P])
        s_ps = m.ps("scatter_ps", [P, 2, CH])
        loaded = [m.sem("loaded0"), m.sem("loaded1")]
        gathered = [[m.sem(f"gathered{b}{g}", 0) for g in range(GATHER_SEMS)] for b in range(2)]
        shift_in, shift_out, ready = m.sem("shift_in"), m.sem("shift_out"), m.sem("ready")
        step, decoded, x_ready = m.sem("step"), m.sem("decoded"), m.sem("x_ready")
        d_ready, d_done, a_ready, masked = (m.sem(q) for q in ("d_ready", "d_done", "a_ready", "masked"))
        rows_ready, scattered, merged = m.sem("rows_ready"), m.sem("scattered"), m.sem("merged")
        block = s.enter_context(nc.Block())

        @block.sync
        def _(sp):
            load_keys(sp, keys_dram, plan, kb, loaded, decoded)

        @block.gpsimd
        def _(pool):
            turns = pool.value_load(plan[0:1, 3:4], min_val=2, max_val=EC // TURN // 2)
            pool.memset(lower[:], 1.0).then_inc(ready, 1)
            pool.wait_ge(ready, 2)
            pool.affine_select(out=lower[:], in_=lower[:], compare_op=ALU.is_gt, fill=0.0, base=0,
                               pattern=[[-1, P]], channel_multiplier=1).then_inc(ready, 1)
            pool.wait_ge(ready, 3)
            pool.wait_ge(shift_in, 2)
            pool.partition_all_reduce(fall[:], fneg[:], P, RMAX).then_inc(shift_out, 1)

            def gather(n, b):
                pool.wait_ge(decoded, n + 2)
                pool.sem_inc(passed, 1)
                for c in range(TURN):
                    pool.indirect_dma_start(av[:, b, c], None, node_dram,
                                            bass.IndirectOffsetOnAxis(dec.src[:, b, c:c + 1], 0)).then_inc(gathered[b][c % GATHER_SEMS], 16)

            gather(0, 0)
            with pool.Fori(0, turns) as i:
                for b in range(2):
                    gather(2 * i + b + 1, 1 - b)

        @block.tensor
        def _(pe):
            turns = pe.value_load(plan[0:1, 3:4], min_val=2, max_val=EC // TURN // 2)

            def dst_row(n, b, c):
                if c == 0:
                    pe.wait_ge(x_ready, n + 2)
                    pe.wait_ge(d_done, 2 * n + 1)
                mm = nc.tensor.matmul(d_ps[:, c], x[:, b, c:c + 1].to_broadcast([P, P]), ident[:], start=True,
                                      stop=True, skip_group_check=True)
                if c % (TURN // 2) == TURN // 2 - 1:
                    mm.then_inc(d_ready, 1)

            def a_rows(n, b, c):
                for h in range(H4):
                    q = TURN + H4 * c + h
                    mm = nc.tensor.matmul(a_ps[:, c % 2, h], x[:, b, q:q + 1].to_broadcast([P, P]), ident[:],
                                          start=True, stop=True, skip_group_check=True)
                mm.then_inc(a_ready, 1)

            for c in range(TURN):
                dst_row(0, 0, c)
            for c in range(2):
                a_rows(0, 0, c)
            with pe.Fori(0, turns) as i:
                for b in range(2):
                    n = 2 * i + b
                    for c in range(2, TURN):
                        pe.wait_ge(masked, TURN * n + c)
                        a_rows(n, b, c)
                    for c in range(TURN):
                        pe.wait_ge(rows_ready, TURN * n + c + 2)
                        pe.wait_ge(merged, TURN * n + max(c - 1, 0) + 1)
                        nc.tensor.matmul(s_ps[:, c % 2, 0:NT * H4], ohlo[:, c % 2], rhs[:, c % 2].rearrange("p t h -> p (t h)"),
                                         start=True, stop=True, skip_group_check=True).then_inc(scattered, 1)
                        dst_row(n + 1, 1 - b, c)
                    for c in range(2):
                        pe.wait_ge(masked, TURN * (n + 1) + c)
                        a_rows(n + 1, 1 - b, c)

        @block.scalar
        def _(act):
            turns = act.value_load(plan[0:1, 3:4], min_val=2, max_val=EC // TURN // 2)

            def copy_rows(n, b):
                for g in range(2):
                    half = slice(g * TURN // 2, (g + 1) * TURN // 2)
                    act.wait_ge(d_ready, 2 * n + g + 2)
                    nc.scalar.activation(dbc[:, b, half], d_ps[:, half], ACT.Copy).then_inc(d_done, 1)

            copy_rows(0, 0)
            with act.Fori(0, turns) as i:
                for b in range(2):
                    n = 2 * i + b
                    act.wait_ge(masked, TURN * n + 1)
                    act.sem_inc(passed, 1)
                    copy_rows(n + 1, 1 - b)

        def merge(dve, n, c):
            dve.wait_ge(scattered, TURN * n + c + 2)
            dve.wait_ge(merged, TURN * n + c + 1)
            dve.tensor_tensor(table[:].rearrange("p t h -> p (t h)"), table[:].rearrange("p t h -> p (t h)"),
                              s_ps[:, c % 2, 0:NT * H4], ALU.max).then_inc(merged, 1)

        @block.vector
        def _(dve):
            turns = dve.value_load(plan[0:1, 3:4], min_val=2, max_val=EC // TURN // 2)
            at = [0]

            def chain(ins, base=0):
                at[0] += 1
                ins.then_inc(step, 1)
                dve.wait_ge(step, base + at[0] + 1)

            dve.wait_ge(loaded[0], 17)
            dec.decode(dve, 0, 0, kb[:, 0], step, 0, decoded)
            at[0] = EdgeNumbers.STEPS
            chain(dve.memset(table[:], 0.0))
            chain(dve.tensor_reduce(fneg[:], feat[:, :, 0:H4].rearrange("p t h -> p h t"), AX.X, ALU.min))
            dve.tensor_scalar(fneg[:], fneg[:], -1.0, None, ALU.mult).then_inc(shift_in, 1)
            dve.wait_ge(shift_out, 2)
            chain(dve.tensor_scalar(shift[:], fall[:], 1.0, None, ALU.add))
            dve.wait_ge(ready, 3)

            def columns(n, b, count, base):
                for gathers in gathered[b]:
                    dve.wait_ge(gathers, 16 * TURN // GATHER_SEMS * count)
                chain(dve.tensor_copy(x[:, b, 0:TURN], dec.dst[:, b]), base)
                dve.tensor_tensor(x[:, b, TURN:NX].rearrange("p (c h) -> p c h", c=TURN), av[:, b, :, 0:H4],
                                  shift[:].rearrange("p (o h) -> p o h", o=1).to_broadcast([P, TURN, H4]), ALU.add)\
                    .then_inc(x_ready, 1)

            columns(0, 0, 1, 0)
            first_steps = at[0]
            STEPS = EdgeNumbers.STEPS + TURN * 3 + 3
            with dve.Fori(0, turns) as i:
                for b in range(2):
                    n = 2 * i + b
                    base = n * STEPS + first_steps
                    dve.wait_ge(loaded[1 - b], 16 * (i + b) + 16 + 1)
                    dec.decode(dve, 1 - b, n + 1, kb[:, 1 - b], step, base, decoded)
                    at[0] = EdgeNumbers.STEPS
                    for c in range(TURN):
                        d = dec.dst[:, b, c:c + 1]
                        if c % (TURN // 2) == 0:
                            dve.wait_ge(d_done, 2 * n + c // (TURN // 2) + 2)
                        dve.wait_ge(a_ready, TURN * n + c + 2)
                        dve.scalar_tensor_tensor(junk[:], dbc[:, b, c], d, lower[:], ALU.is_equal, ALU.mult,
                                                 accum_out=first[:, c:c + 1]).then_inc(step, 1)
                        at[0] += 1
                        dve.scalar_tensor_tensor(val[:], dbc[:, b, c:c + 1].to_broadcast([P, H4, P]), d, a_ps[:, c % 2],
                                                 ALU.is_equal, ALU.mult).then_inc(masked, 1)
                        dve.wait_ge(masked, TURN * n + c + 2)
                        dve.reduce_max(best[:, c], val[:], axis=AX.X).then_inc(step, 1)
                        at[0] += 1
                        dve.wait_ge(step, base + at[0] + 1)
                    chain(dve.tensor_scalar(lead[:], first[:], 0.0, None, ALU.is_equal), base)
                    columns(n + 1, 1 - b, i + 1 + b, base)
                    for c in range(TURN):
                        dve.wait_ge(scattered, TURN * n + max(c - 1, 0) + 1)
                        dve.scalar_tensor_tensor(rhs[:, c % 2], iota32[:].rearrange("p (t o) -> p t o", o=1).to_broadcast([P, NT, H4]),
                                                 dec.hi[:, b, c:c + 1],
                                                 best[:, c:c + 1].to_broadcast([P, NT, H4]), ALU.is_equal, ALU.mult)\
                            .then_inc(step, 1)
                        at[0] += 1
                        dve.tensor_scalar(ohlo[:, c % 2], iota128[:], dec.lo[:, b, c:c + 1], lead[:, c:c + 1],
                                          ALU.is_equal, ALU.mult).then_inc(rows_ready, 1)
                        if c:
                            merge(dve, n, c - 1)
                    merge(dve, n, TURN - 1)
                    chain(dve.tensor_copy(junk[:, 0:1], junk[:, 1:2]), base)
                    assert at[0] == STEPS, (at[0], STEPS)


def load_keys(sp, keys_dram, plan, kb, loaded, decoded):
    start = sp.value_load(plan[0:1, 2:3], min_val=0, max_val=EC)
    turns = sp.value_load(plan[0:1, 3:4], min_val=2, max_val=EC // TURN // 2)
    sp.dma_start(kb[:, 0], keys_dram[:, bass.ds(start, TURN)]).then_inc(loaded[0], 16)
    with sp.Fori(0, turns) as i:
        for b in range(2):
            n = 2 * i + b
            sp.wait_ge(decoded, n + 1)
            sp.dma_start(kb[:, 1 - b], keys_dram[:, bass.ds(start + (n + 1) * TURN, TURN)]).then_inc(loaded[1 - b], 16)


class EdgeNumbers:
    STEPS = 9

    def __init__(self, m):
        self.ki = m.sb("key_int", [P, TURN], I32)
        self.di = m.sb("dst_int", [P, TURN], I32)
        self.out = m.sb("not_listed", [P, TURN])
        self.li = m.sb("lo_int", [P, TURN], I32)
        self.dg = m.sb("dst_row", [P, 2, TURN], I32)
        self.src = m.sb("src", [P, 2, TURN], I32)
        self.dst = m.sb("dst", [P, 2, TURN])
        self.lo = m.sb("lo", [P, 2, TURN])
        self.hi = m.sb("hi", [P, 2, TURN])

    def decode(self, dve, b, n, keys, step, base, decoded):
        k = 0

        def then(ins):
            nonlocal k
            k += 1
            ins.then_inc(step, 1)

        def fence():
            dve.wait_ge(step, base + k + 1)

        fence()
        then(dve.tensor_scalar(self.ki[:], keys, 1.0, None, ALU.subtract))
        fence()
        then(dve.tensor_scalar(self.di[:], self.ki[:], BITS, None, ALU.arith_shift_right))
        then(dve.tensor_scalar(self.src[:, b], self.ki[:], 4095, None, ALU.bitwise_and))
        fence()
        then(dve.tensor_scalar(self.out[:], self.src[:, b], 4095.0, -8192.0, ALU.is_equal, ALU.mult))
        then(dve.tensor_scalar(self.li[:], self.di[:], 127, None, ALU.bitwise_and))
        fence()
        then(dve.tensor_tensor(self.dst[:, b], self.di[:], self.out[:], ALU.add))
        then(dve.tensor_copy(self.lo[:, b], self.li[:]))
        fence()
        then(dve.tensor_tensor(self.hi[:, b], self.dst[:, b], self.lo[:, b], ALU.subtract))
        fence()
        then(dve.tensor_scalar(self.hi[:, b], self.hi[:, b], 1.0 / P, None, ALU.mult))
        fence()
        assert k == self.STEPS
        dve.tensor_scalar(self.dg[:, b], self.dst[:, b], 0.0, None, ALU.max).then_inc(decoded, 1)
        dve.wait_ge(decoded, n + 2)


def node_max_stage(nc, feat, adst, shift, table, clamped, last, mx, max_dram, ident):
    with ExitStack() as s:
        m = Memory(nc, s, "nmax")
        l_ps = m.ps("last_ps", [P, G20])
        top = m.sb("top", [P, NT, H4])
        alt = m.sb("alt", [P, NT, H4])
        lsh = m.sb("last_shifted", [P, H4])
        has = m.sb("has_clamped", [P, NT])
        last_ready, step, mx_ready, stored = m.sem("last_ready"), m.sem("step"), m.sem("mx_ready"), m.sem("stored")
        block = s.enter_context(nc.Block())

        @block.tensor
        def _(pe):
            nc.tensor.matmul(l_ps[:], ident[:, P - 1:P].to_broadcast([P, P]), feat[:, NT - 1], start=True, stop=True)\
                .then_inc(last_ready, 1)

        @block.sync
        def _(sp):
            sp.wait_ge(mx_ready, 2)
            sp.dma_start(max_dram.rearrange("(t p) f -> p t f", p=P), mx[:]).then_inc(stored, 16)
            sp.wait_ge(stored, 17)

        @block.vector
        def _(dve):
            at = [0]

            def chain(ins):
                at[0] += 1
                ins.then_inc(step, 1)
                dve.wait_ge(step, at[0] + 1)

            sh = shift[:].rearrange("p (o h) -> p o h", o=1).to_broadcast([P, NT, H4])
            chain(dve.tensor_tensor(top[:], feat[:, :, 0:H4], sh, ALU.add))
            chain(dve.tensor_tensor(top[:], top[:], table[:], ALU.max))
            dve.wait_ge(last_ready, 2)
            chain(dve.tensor_copy(last[:], l_ps[:]))
            chain(dve.tensor_tensor(lsh[:], last[:, 0:H4], shift[:], ALU.add))
            chain(dve.tensor_scalar(has[:], clamped[:], 0.0, None, ALU.is_gt))
            chain(dve.tensor_tensor(alt[:], has[:].rearrange("p (t o) -> p t o", o=1).to_broadcast([P, NT, H4]),
                                    lsh[:].rearrange("p (o h) -> p o h", o=1).to_broadcast([P, NT, H4]), ALU.mult))
            chain(dve.tensor_tensor(top[:], top[:], alt[:], ALU.max))
            chain(dve.tensor_tensor(top[:], top[:], sh, ALU.subtract))
            chain(dve.tensor_tensor(top[:], top[:], adst[:], ALU.add))
            chain(dve.tensor_scalar(alt[:], top[:], 0.2, None, ALU.mult))
            chain(dve.tensor_copy(mx[:, :, 0:H4], adst[:]))
            dve.tensor_tensor(mx[:, :, H4:2 * H4], top[:], alt[:], ALU.max).then_inc(mx_ready, 1)


def edge_sum_stage(nc, passed, a, experts, keys_dram, plan, node_dram, max_dram, sums, iota128, iota32):
    W5 = 1 + NE
    with ExitStack() as s:
        m = Memory(nc, s, "esum")
        kb = m.sb("keys", [P, 2, TURN])
        dec = EdgeNumbers(m)
        av = m.sb("src_rows", [P, 2, TURN, G20])
        dv = m.sb("dst_rows", [P, 2, TURN, 2 * H4])
        z = m.sb("z", [P, TURN, H4])
        z2 = m.sb("z2", [P, TURN, H4])
        ee = m.sb("exp", [P, 2, TURN, H4])
        msg = m.sb("messages", [P, 2, TURN, H4, W5])
        ohlo = m.sb("lo_rows", [P, 2, P])
        rhs = m.sb("hi_rows", [P, 2, NT, H4 * W5])
        zero = m.sb("zeros", [P, NT // 2 * H4 * W5])
        s_ps = m.ps("sums_ps", [P, 2, CH])
        HALF = NT // 2 * H4 * W5
        loaded = [m.sem("loaded0"), m.sem("loaded1")]
        gathered = [[m.sem(f"gathered{b}{g}", 0) for g in range(GATHER_SEMS)] for b in range(2)]
        step, decoded, x_ready, e_ready, msg_ready = (m.sem(q) for q in ("step", "decoded", "x_ready", "e_ready", "msg_ready"))
        rows_ready, summed, ready, opened, closed = (m.sem(q) for q in ("rows_ready", "summed", "ready", "opened", "closed"))
        block = s.enter_context(nc.Block())

        @block.sync
        def _(sp):
            load_keys(sp, keys_dram, plan, kb, loaded, decoded)
            experts.load(sp, a)

        @block.gpsimd
        def _(pool):
            turns = pool.value_load(plan[0:1, 3:4], min_val=2, max_val=EC // TURN // 2)

            def gather(n, b):
                pool.wait_ge(decoded, n + 2)
                pool.sem_inc(passed, 1)
                for c in range(TURN):
                    pool.indirect_dma_start(av[:, b, c], None, node_dram,
                                            bass.IndirectOffsetOnAxis(dec.src[:, b, c:c + 1], 0)).then_inc(gathered[b][c % GATHER_SEMS], 16)
                    pool.indirect_dma_start(dv[:, b, c], None, max_dram,
                                            bass.IndirectOffsetOnAxis(dec.dg[:, b, c:c + 1], 0)).then_inc(gathered[b][c % GATHER_SEMS], 16)

            for b in range(2):
                gather(b, b)
            with pool.Fori(1, turns) as i:
                for b in range(2):
                    gather(2 * i + b, b)

        @block.tensor
        def _(pe):
            turns = pe.value_load(plan[0:1, 3:4], min_val=2, max_val=EC // TURN // 2)
            pe.wait_ge(ready, 2)
            for h in range(2):
                mm = nc.tensor.matmul(s_ps[:, h, 0:HALF], zero[:, 0:P], zero[:], start=True, stop=False, skip_group_check=True)
            mm.then_inc(opened, 1)
            pe.wait_ge(opened, 2)
            with pe.Fori(0, turns) as i:
                for b in range(2):
                    n = 2 * i + b
                    for c in range(TURN):
                        pe.wait_ge(rows_ready, TURN * n + c + 2)
                        for h in range(2):
                            mm = nc.tensor.matmul(s_ps[:, h, 0:HALF], ohlo[:, c % 2],
                                                  rhs[:, c % 2, h * NT // 2:(h + 1) * NT // 2].rearrange("p t f -> p (t f)"),
                                                  start=False, stop=False, skip_group_check=True)
                        mm.then_inc(summed, 1)
            for h in range(2):
                mm = nc.tensor.matmul(s_ps[:, h, 0:HALF], zero[:, 0:P], zero[:], start=False, stop=True, skip_group_check=True)
            mm.then_inc(closed, 1)

        @block.scalar
        def _(act):
            turns = act.value_load(plan[0:1, 3:4], min_val=2, max_val=EC // TURN // 2)
            with act.Fori(0, turns) as i:
                for b in range(2):
                    n = 2 * i + b
                    act.wait_ge(x_ready, n + 2)
                    act.wait_ge(msg_ready, 2 * i + 1)
                    nc.scalar.activation(ee[:, b], z[:], ACT.Exp).then_inc(e_ready, 1)

        @block.vector
        def _(dve):
            turns = dve.value_load(plan[0:1, 3:4], min_val=2, max_val=EC // TURN // 2)
            dve.memset(zero[:], 0.0).then_inc(ready, 1)
            dve.wait_ge(loaded[0], 17)
            dec.decode(dve, 0, 0, kb[:, 0], step, 0, decoded)
            STEPS = 5 + EdgeNumbers.STEPS + TURN
            with dve.Fori(0, turns) as i:
                for b in range(2):
                    n = 2 * i + b
                    at = [0]
                    base = EdgeNumbers.STEPS + n * STEPS

                    def chain(ins):
                        at[0] += 1
                        ins.then_inc(step, 1)
                        dve.wait_ge(step, base + at[0] + 1)

                    for gathers in gathered[b]:
                        dve.wait_ge(gathers, 32 * TURN // GATHER_SEMS * (i + 1))
                    dve.wait_ge(e_ready, n + 1)
                    chain(dve.tensor_tensor(z[:], av[:, b, :, 0:H4], dv[:, b, :, 0:H4], ALU.add))
                    chain(dve.tensor_scalar(z2[:], z[:], 0.2, None, ALU.mult))
                    chain(dve.tensor_tensor(z[:], z[:], z2[:], ALU.max))
                    chain(dve.tensor_tensor(z[:], z[:], dv[:, b, :, H4:2 * H4], ALU.subtract))
                    dve.tensor_scalar(z[:], z[:], 0.0, None, ALU.min).then_inc(x_ready, 1)
                    dve.wait_ge(loaded[1 - b], 16 * (i + b) + 16 + 1)
                    dve.wait_ge(summed, TURN * n + 1)
                    dec.decode(dve, 1 - b, n + 1, kb[:, 1 - b], step, base + at[0], decoded)
                    at[0] += EdgeNumbers.STEPS
                    dve.wait_ge(e_ready, n + 2)
                    chain(dve.tensor_copy(msg[:, b, :, :, 0:1].rearrange("p c h o -> p c (h o)"), ee[:, b]))
                    dve.tensor_tensor(msg[:, b, :, :, 1:W5], av[:, b, :, H4:G20].rearrange("p c (h e) -> p c h e", h=H4),
                                      ee[:, b].rearrange("p c (h o) -> p c h o", o=1).to_broadcast([P, TURN, H4, NE]), ALU.mult)\
                        .then_inc(msg_ready, 1)
                    dve.wait_ge(msg_ready, n + 2)
                    for c in range(TURN):
                        dve.wait_ge(summed, TURN * n + max(c - 1, 0) + 1)
                        chain(dve.tensor_scalar(ohlo[:, c % 2], iota128[:], dec.lo[:, b, c:c + 1], None, ALU.is_equal))
                        dve.scalar_tensor_tensor(
                            rhs[:, c % 2], iota32[:].rearrange("p (t o) -> p t o", o=1).to_broadcast([P, NT, H4 * W5]),
                            dec.hi[:, b, c:c + 1],
                            msg[:, b, c:c + 1].rearrange("p o h f -> p o (h f)").to_broadcast([P, NT, H4 * W5]),
                            ALU.is_equal, ALU.mult).then_inc(rows_ready, 1)
                    assert at[0] == STEPS, (at[0], STEPS)
            dve.wait_ge(closed, 2)
            for h in range(2):
                ins = dve.tensor_copy(sums[:, h * NT // 2:(h + 1) * NT // 2].rearrange("p t h f -> p (t h f)"), s_ps[:, h, 0:HALF])
            ins.then_inc(step, 1)


def gate_stage(nc, a, feat, mx, clamped, last, sums, gates, gT, gates_dram, ident):
    W5 = 1 + NE
    with ExitStack() as s:
        m = Memory(nc, s, "gates")
        par = m.sb("params", [P, 3, 16])
        z = m.sb("z", [P, 2, NT, H4])
        z2 = m.sb("z2", [P, 2, NT, H4])
        ee = m.sb("exp", [P, 2, NT, H4])
        tmp = m.sb("tmp", [P, NT, H4, NE])
        agg = m.sb("agg", [P, NT, H4, NE])
        one = m.sb("per_node", [P, 6, NT])
        eps = m.sb("eps", [P, 1])
        sc = m.sb("scores", [P, NT, NE])
        rank = m.sb("rank", [P, NE, NT])
        beat = m.sb("beats", [P, NT])
        t_ps = m.ps("gT_ps", [NE, 2, 4, P])
        loaded, step, z_ready, e_ready = m.sem("loaded"), m.sem("step"), m.sem("z_ready"), m.sem("e_ready")
        var_ready, sd_ready, sc_ready, sm_ready = (m.sem(q) for q in ("var_ready", "sd_ready", "sc_ready", "sm_ready"))
        gates_ready, t_ready, t_done = m.sem("gates_ready"), m.sem("t_ready"), m.sem("t_done")
        stored = m.sem("stored")
        block = s.enter_context(nc.Block())

        @block.sync
        def _(sp):
            for q, name in enumerate(("b_gat", "ln_gamma", "ln_beta")):
                sp.dma_start(par[:, q], a[name].rearrange("(a n) -> a n", a=1).to_broadcast([P, 16])).then_inc(loaded, 16)
            sp.wait_ge(t_done, NCH + 1)
            sp.dma_start(gates_dram, gT[:]).then_inc(stored, 16)
            sp.wait_ge(stored, 17)

        @block.scalar
        def _(act):
            act.wait_ge(z_ready, 2)
            nc.scalar.activation(ee[:], z[:], ACT.Exp).then_inc(e_ready, 1)
            act.wait_ge(var_ready, 2)
            nc.scalar.activation(one[:, 2], one[:, 1], ACT.Sqrt, bias=eps[:], scale=1.0 / 16).then_inc(sd_ready, 1)
            act.wait_ge(sc_ready, 2)
            nc.scalar.activation(sc[:], sc[:], ACT.Exp).then_inc(sm_ready, 1)

        @block.tensor
        def _(pe):
            pe.wait_ge(gates_ready, 2)
            for n in range(NCH):
                if n >= 2:
                    pe.wait_ge(t_done, n)
                for j in range(4):
                    mm = nc.tensor.transpose(t_ps[:, n % 2, j], gates[:, 4 * n + j], ident[:])
                mm.then_inc(t_ready, 1)

        @block.vector
        def _(dve):
            at = [0]

            def chain(ins):
                at[0] += 1
                ins.then_inc(step, 1)
                dve.wait_ge(step, at[0] + 1)

            def wide(v, *shape):
                return v.rearrange("p (t o) -> p t o", o=1).to_broadcast([P, NT, *shape])

            chain(dve.memset(eps[:], 1e-5))
            chain(dve.tensor_tensor(z[:, 0], feat[:, :, 0:H4], mx[:, :, 0:H4], ALU.add))
            chain(dve.tensor_tensor(z[:, 1], last[:, 0:H4].rearrange("p (o h) -> p o h", o=1).to_broadcast([P, NT, H4]),
                                    mx[:, :, 0:H4], ALU.add))
            chain(dve.tensor_scalar(z2[:], z[:], 0.2, None, ALU.mult))
            chain(dve.tensor_tensor(z[:], z[:], z2[:], ALU.max))
            for q in range(2):
                chain(dve.tensor_tensor(z[:, q], z[:, q], mx[:, :, H4:2 * H4], ALU.subtract))
            dve.tensor_scalar(z[:], z[:], 0.0, None, ALU.min).then_inc(z_ready, 1)
            dve.wait_ge(e_ready, 2)
            chain(dve.tensor_tensor(ee[:, 1], ee[:, 1], wide(clamped[:], H4), ALU.mult))
            for q, h in enumerate((feat[:, :, H4:G20].rearrange("p t (h e) -> p t h e", h=H4),
                                   last[:, H4:G20].rearrange("p (o h e) -> p o h e", o=1, h=H4).to_broadcast([P, NT, H4, NE]))):
                chain(dve.tensor_tensor(tmp[:], h, ee[:, q].rearrange("p t (h o) -> p t h o", o=1).to_broadcast([P, NT, H4, NE]), ALU.mult))
                chain(dve.tensor_tensor(agg[:], tmp[:], sums[:, :, :, 1:W5] if q == 0 else agg[:], ALU.add))
            den = sums[:, :, :, 0:1].rearrange("p t h o -> p t (h o)")
            chain(dve.tensor_tensor(z[:, 0], ee[:, 0], den, ALU.add))
            chain(dve.tensor_tensor(z[:, 0], z[:, 0], ee[:, 1], ALU.add))
            chain(dve.tensor_scalar(z[:, 0], z[:, 0], 1e-16, None, ALU.add))
            chain(dve.reciprocal(z[:, 1], z[:, 0]))
            chain(dve.tensor_tensor(agg[:], agg[:], z[:, 1].rearrange("p t (h o) -> p t h o", o=1).to_broadcast([P, NT, H4, NE]), ALU.mult))
            a16 = agg[:].rearrange("p t h e -> p t (h e)")
            t16 = tmp[:].rearrange("p t h e -> p t (h e)")
            dve.wait_ge(loaded, 49)
            chain(dve.tensor_tensor(a16, a16, par[:, 0:1].to_broadcast([P, NT, 16]), ALU.add))
            chain(dve.reduce_sum(one[:, 0], a16, axis=AX.X))
            chain(dve.tensor_scalar(one[:, 0], one[:, 0], 1.0 / 16, None, ALU.mult))
            chain(dve.tensor_tensor(a16, a16, wide(one[:, 0], 16), ALU.subtract))
            chain(dve.tensor_tensor(t16, a16, a16, ALU.mult))
            dve.reduce_sum(one[:, 1], t16, axis=AX.X).then_inc(var_ready, 1)
            dve.wait_ge(sd_ready, 2)
            chain(dve.reciprocal(one[:, 3], one[:, 2]))
            chain(dve.tensor_tensor(a16, a16, wide(one[:, 3], 16), ALU.mult))
            chain(dve.tensor_tensor(a16, a16, par[:, 1:2].to_broadcast([P, NT, 16]), ALU.mult))
            chain(dve.tensor_tensor(a16, a16, par[:, 2:3].to_broadcast([P, NT, 16]), ALU.add))
            chain(dve.reduce_sum(sc[:], agg[:].rearrange("p t h e -> p t e h"), axis=AX.X))
            chain(dve.tensor_scalar(sc[:], sc[:], 1.0 / H4, None, ALU.mult))
            chain(dve.memset(rank[:], 0.0))
            for i in range(NE):
                for j in range(i + 1, NE):
                    chain(dve.tensor_tensor(beat[:], sc[:, :, i], sc[:, :, j], ALU.is_ge))
                    chain(dve.tensor_tensor(rank[:, j], rank[:, j], beat[:], ALU.add))
                    chain(dve.tensor_scalar(beat[:], beat[:], -1.0, 1.0, ALU.mult, ALU.add))
                    chain(dve.tensor_tensor(rank[:, i], rank[:, i], beat[:], ALU.add))
            chain(dve.tensor_scalar(rank[:], rank[:], 2.0, None, ALU.is_lt))
            chain(dve.reduce_max(one[:, 4], sc[:], axis=AX.X))
            dve.tensor_tensor(sc[:], sc[:], wide(one[:, 4], NE), ALU.subtract).then_inc(sc_ready, 1)
            dve.wait_ge(sm_ready, 2)
            chain(dve.tensor_tensor(sc[:], sc[:], rank[:].rearrange("p e t -> p t e"), ALU.mult))
            chain(dve.reduce_sum(one[:, 5], sc[:], axis=AX.X))
            chain(dve.reciprocal(one[:, 0], one[:, 5]))
            dve.tensor_tensor(gates[:], sc[:], wide(one[:, 0], NE), ALU.mult).then_inc(gates_ready, 1)
            for n in range(NCH):
                dve.wait_ge(t_ready, n + 2)
                dve.tensor_copy(gT[:, n * CH:(n + 1) * CH], t_ps[:, n % 2].rearrange("p j c -> p (j c)")).then_inc(t_done, 1)


class GatedExperts:
    F = 512
    KF = F // P

    def __init__(self, m):
        self.w1 = m.sb("w1_sb", [P, NE, KC, self.F])
        self.w2 = m.sb("w2_sb", [P, NE, self.KF, C])
        self.b1 = m.sb("b1_sb", [P, NE, self.KF])
        self.b2 = m.sb("b2_sb", [NE, C])
        self.loaded = m.sem("loaded", 0)

    def load(self, sp, a):
        sp.dma_start(self.w1[:], a["ew1"].rearrange("e (k p) f -> p e k f", p=P)).then_inc(self.loaded, 16)
        sp.dma_start(self.w2[:], a["ew2"].rearrange("e (k p) d -> p e k d", p=P)).then_inc(self.loaded, 16)
        sp.dma_start(self.b1[:].rearrange("p e k -> p (e k)"), a["eb1"]).then_inc(self.loaded, 16)
        sp.dma_start(self.b2[:], a["eb2"]).then_inc(self.loaded, 16)


def gated_expert_stage(nc, passed, experts, xn, gT, gates_dram, res, out):
    KF = GatedExperts.KF
    with ExitStack() as s:
        m = Memory(nc, s, "moe")
        w1, w2, b1, b2, loaded = experts.w1, experts.w2, experts.b1, experts.b2, experts.loaded
        hid = m.sb("hidden", [P, 2, CH])
        gh = m.sb("gated_hidden", [P, 4, CH])
        gb = m.sb("gate_rows", [P, 2, NE, CH])
        h_ps = m.ps("hidden_ps", [P, 2, CH])
        y_ps = m.ps("y_ps", [P, 2, KC, CH])
        gates_loaded = [m.sem("gates_loaded0"), m.sem("gates_loaded1")]
        h_ready, h_done, gated, y_ready = m.sem("h_ready"), m.sem("h_done"), m.sem("gated"), m.sem("y_ready")
        added, stored = m.sem("added"), m.sem("stored")
        o_v = out.rearrange("(k p) n -> p k n", p=P)
        block = s.enter_context(nc.Block())
        Q = NE * KF

        @block.sync
        def _(sp):
            def load_gates(n):
                sp.dma_start(gb[:, n % 2], gates_dram[:, n * CH:(n + 1) * CH].rearrange("(o e) c -> o e c", o=1)
                             .to_broadcast([P, NE, CH])).then_inc(gates_loaded[n % 2], 16)

            for n in range(2):
                load_gates(n)
            for n in range(NCH):
                sp.wait_ge(added, n + 2)
                sp.dma_start(o_v[:, :, n * CH:(n + 1) * CH], res[:, :, n * CH:(n + 1) * CH]).then_inc(stored, 16)
                if n + 2 < NCH:
                    load_gates(n + 2)
            sp.wait_ge(stored, 16 * NCH + 1)

        @block.tensor
        def _(pe):
            pe.wait_ge(loaded, 64)
            with pe.Fori(0, NCH // 2) as i:
                for b in range(2):
                    n = 2 * i + b
                    cols = bass.ds(n * CH, CH)

                    def out_tile(q):
                        pe.wait_ge(gated, Q * n + q + 2)
                        for o in range(KC):
                            mm = nc.tensor.matmul(y_ps[:, b, o], w2[:, q // KF, q % KF, o * P:(o + 1) * P], gh[:, q % 4],
                                                  start=False, stop=q == Q - 1)
                        mm.then_inc(y_ready, 1)

                    for q in range(Q):
                        e = q // KF
                        pe.wait_ge(h_done, Q * n + max(q - 1, 0) + 1)
                        for k in range(KC):
                            mm = nc.tensor.matmul(h_ps[:, q % 2], w1[:, e, k, (q % KF) * P:(q % KF + 1) * P],
                                                  xn[:, k, cols], start=k == 0, stop=k == KC - 1)
                        mm.then_inc(h_ready, 1)
                        if q == 2:
                            pe.wait_ge(added, 2 * i + 1)
                            pe.sem_inc(passed, 1)
                            for o in range(KC):
                                nc.tensor.matmul(y_ps[:, b, o], b2[:, o * P:(o + 1) * P], gT[:, cols], start=True, stop=False)
                        if q >= 2:
                            out_tile(q - 2)
                    out_tile(Q - 2)
                    out_tile(Q - 1)

        @block.scalar
        def _(act):
            act.wait_ge(loaded, 64)
            with act.Fori(0, NCH) as n:
                for q in range(Q):
                    act.wait_ge(h_ready, Q * n + q + 2)
                    act.wait_ge(gated, Q * n + max(q - 1, 0) + 1)
                    nc.scalar.activation(hid[:, q % 2], h_ps[:, q % 2], ACT.Gelu,
                                         bias=b1[:, q // KF, q % KF:q % KF + 1]).then_inc(h_done, 1)

        @block.vector
        def _(dve):
            with dve.Fori(0, NCH // 2) as i:
                for b in range(2):
                    n = 2 * i + b
                    for q in range(Q):
                        e = q // KF
                        if q == 0:
                            dve.wait_ge(gates_loaded[b], 16 * i + 16 + 1)
                        dve.wait_ge(h_done, Q * n + q + 2)
                        dve.wait_ge(y_ready, Q * n + max(q - 3, 0) + 1)
                        dve.tensor_tensor(gh[:, q % 4], hid[:, q % 2], gb[:, b, e], ALU.mult).then_inc(gated, 1)
                    dve.wait_ge(y_ready, Q * n + Q + 1)
                    c = res[:, :, bass.ds(n * CH, CH)]
                    dve.tensor_tensor(c, c, y_ps[:, b], ALU.add).then_inc(added, 1)


def program(nc, a, out):
    with ExitStack() as s:
        m = Memory(nc, s, "program")
        passed = nc.alloc_semaphore(name="passed")
        Memory.spent = []
        ones_mean = m.sb("ones_mean", [P, P])
        block_ones = m.sb("block_ones", [P, P])
        ident = m.sb("ident", [P, P])
        stack_ident = m.sb("stack_ident", [P, DH])
        col_sum = m.sb("col_sum", [P, KC])
        top_w = m.sb("top_w", [P, 2])
        top_i = m.sb("top_i", [1, 8], mybir.dt.uint32)
        qk_dram = nc.dram_tensor("qk_scratch", [4, 2, P, N], F16, kind="Internal").ap()
        v_dram = nc.dram_tensor("v_scratch", [HEADS, P, NT * DH], F32, kind="Internal").ap()
        iota128 = m.sb("iota128", [P, P])
        iota32 = m.sb("iota32", [P, NT])
        plan = m.sb("plan", [P, 4], I32)
        clamped = m.sb("clamped", [P, NT])
        counts = m.sb("counts", [64, 64])
        keys_dram = nc.dram_tensor("keys_scratch", [P, 2 * EC + LISTED + TURN], F32, kind="Internal").ap()
        node_dram = nc.dram_tensor("node_scratch", [N, G20], F32, kind="Internal").ap()
        gates_dram = nc.dram_tensor("gates_scratch", [NE, N], F32, kind="Internal").ap()
        max_dram = nc.dram_tensor("max_scratch", [N, 2 * H4], F32, kind="Internal").ap()
        fill_constants(nc, ones_mean, block_ones, ident, stack_ident)
        iotas(nc, iota128, iota32)
        qkv_stage(nc, a["x"], a["wqkvT"], a["temp"], qk_dram, v_dram, ones_mean, block_ones, ident)
        res = m.sb("residual", [P, KC, N])
        with nc.sbuf_tensor("attn", [P, KC, 16, C], F32) as attn:
            attention_stage(nc, passed, a["temp"], qk_dram, v_dram, attn, stack_ident)
            projection_stage(nc, a["x"], a["wprojT"], attn, res)
        with nc.sbuf_tensor("normed", [P, KC, N], F32) as xn:
            layer_norm_stage(nc, "ln_ffn", res, xn, 1e-5, ones_mean, ident, col_sum)
            routing_stage(nc, a, col_sum, top_w, top_i)
            expert_stage(nc, passed, a, xn, top_w, top_i, keys_dram, plan, counts)
            layer_norm_stage(nc, "ln_out", xn, res, 1e-5, ones_mean, ident, affine=(a["gamma"], a["beta"]))
        with nc.sbuf_tensor("h_padded", [P, PW * PW], F32) as hpad, nc.sbuf_tensor("h", [P, N], F32) as h, \
                nc.sbuf_tensor("h_transposed", [P, NT + 2, P], F32) as hT, \
                nc.sbuf_tensor("gate", [P, N], F32) as gate:
            with nc.sbuf_tensor("conv_normed", [P, KC, N], F32) as cn:
                layer_norm_stage(nc, "ln_conv", res, cn, 1e-6, ones_mean, ident)
                conv_in_stage(nc, a, cn, h, hpad, hT, gate, ident)
            conv_out_stage(nc, a, h, hpad, hT, gate, res, ident)
        Memory.clear_semaphores(nc)
        with nc.sbuf_tensor("graph_normed", [P, KC, N], F32) as xn, ExitStack() as gs:
            g = Memory(nc, gs, "graph")
            layer_norm_stage(nc, "ln_graph", res, xn, 1e-5, ones_mean, ident)
            feat = g.sb("feat", [P, NT, G20])
            adst = g.sb("adst", [P, NT, H4])
            shift = g.sb("shift", [P, H4])
            table = g.sb("table", [P, NT, H4])
            last = g.sb("last", [P, G20])
            mx = g.sb("mx", [P, NT, 2 * H4])
            sums = g.sb("sums", [P, NT, H4, 1 + NE])
            gates = g.sb("gates", [P, NT, NE])
            gT = g.sb("gT", [NE, N])
            experts = GatedExperts(Memory(nc, gs, "experts"))
            node_features_stage(nc, a, xn, feat, adst, node_dram, keys_dram, plan, counts, clamped, ident)
            edge_max_stage(nc, passed, keys_dram, plan, feat, node_dram, shift, table, iota128, iota32, ident)
            node_max_stage(nc, feat, adst, shift, table, clamped, last, mx, max_dram, ident)
            edge_sum_stage(nc, passed, a, experts, keys_dram, plan, node_dram, max_dram, sums, iota128, iota32)
            gate_stage(nc, a, feat, mx, clamped, last, sums, gates, gT, gates_dram, ident)
            gated_expert_stage(nc, passed, experts, xn, gT, gates_dram, res, out)


def iotas(nc, iota128, iota32):
    with ExitStack() as s:
        m = Memory(nc, s, "iotas")
        i128 = m.sb("i128", [P, P], I32)
        made, copied = m.sem("made"), m.sem("copied")
        block = s.enter_context(nc.Block())

        @block.gpsimd
        def _(pool):
            pool.iota(i128[:], pattern=[[1, P]], base=0, channel_multiplier=0).then_inc(made, 1)

        @block.vector
        def _(dve):
            dve.wait_ge(made, 2)
            dve.tensor_copy(iota128[:], i128[:]).then_inc(copied, 1)
            dve.tensor_copy(iota32[:], i128[:, 0:NT]).then_inc(copied, 1)


def layout(z):
    import numpy as np

    def cols(v, per):
        return np.ascontiguousarray(v.reshape(-1, per, P).transpose(2, 0, 1).reshape(P, -1))

    T = lambda v: np.ascontiguousarray(v.T)
    return {
        "x": np.ascontiguousarray(z["x"].reshape(C, N)),
        "wqkvT": T(z["L0_conv_w_qkv"]), "wprojT": T(z["L0_conv_w_proj"]),
        "temp": np.ascontiguousarray(z["L0_conv_temperature"].reshape(HEADS)),
        "wr": z["L0_ffn_Wr"], "br": z["L0_ffn_br"], "w1": z["L0_ffn_W1"], "w2": z["L0_ffn_W2"],
        "b1": cols(z["L0_ffn_b1"], 4), "b2": cols(z["L0_ffn_b2"], 2),
        "gamma": cols(z["L0_ffn_gamma"], 2), "beta": cols(z["L0_ffn_beta"], 2),
        "cw1T": T(z["L1_conv_W1"]), "cb1": cols(z["L1_conv_b1"], 1),
        "cw2T": T(z["L1_conv_W2"]), "cb2": cols(z["L1_conv_b2"], 1),
        "wgat": z["L1_ffn_W_gat"], "att_src": z["L1_ffn_att_src"].reshape(16), "att_dst": z["L1_ffn_att_dst"].reshape(16),
        "b_gat": z["L1_ffn_b_gat"], "ln_gamma": z["L1_ffn_ln_gamma"], "ln_beta": z["L1_ffn_ln_beta"],
        "ew1": z["L1_ffn_W1"], "ew2": z["L1_ffn_W2"], "eb1": cols(z["L1_ffn_b1"], 4), "eb2": z["L1_ffn_b2"],
        "edges": z["L1_ffn_edge_index"],
        "cwoT": T(z["L1_conv_Wout"]), "cbo": cols(z["L1_conv_bout"], 2),
    }


def kernel(**inputs):
    import numpy as np
    import concourse.bacc as bacc
    from concourse.bass_utils import run_bass_kernel_spmd

    nc = bacc.Bacc("TRN2", target_bir_lowering=False, num_devices=1)
    arrays = {f"in_{k}": np.ascontiguousarray(v) for k, v in layout({k: np.asarray(v) for k, v in inputs.items()}).items()}
    aps = {k[3:]: nc.dram_tensor(k, v.shape, mybir.dt.from_np(v.dtype), kind="ExternalInput").ap()
           for k, v in arrays.items()}
    out = nc.dram_tensor("out_dram", [C, N], F32, kind="ExternalOutput").ap()
    program(nc, aps, out)
    r = run_bass_kernel_spmd(nc, [arrays], core_ids=[0])
    return r.results[0]["out_dram"].reshape(1, C, 64, 64)
```
